# Optimizing a Trainium2 kernel written in Bass

```python
import numpy as np
import jax
import jax.numpy as jnp

def _softmax(x, axis=-1):
    return jax.nn.softmax(x, axis=axis)
def _gelu(x):
    return jax.nn.gelu(x, approximate=True)
def _silu(x):
    return jax.nn.silu(x)
def _sigmoid(x):
    return jax.nn.sigmoid(x)
def _layernorm(x, axis=-1, eps=1e-5):
    m = jnp.mean(x, axis=axis, keepdims=True)
    v = jnp.var(x, axis=axis, keepdims=True)
    return (x - m) / jnp.sqrt(v + eps)
def _scatter_add(tgt, idx, src, axis=0):
    return tgt.at[idx].add(src)
def _segment_sum(src, seg, n):
    return jax.ops.segment_sum(src, seg, n)

kernel_name = 'mk_conv_seq_d2_conv_nchw192_29c46e'

def setup_inputs(seed: int = 0):
    np.random.seed(seed)
    _w = jnp.asarray
    def _rec_inputs():
        import jax
        import jax.numpy as jnp
        _gk = jax.random.key(seed)
        x = -0.0001538 + 1 * jax.random.normal(jax.random.fold_in(_gk, 1), (2, 192, 128, 128), jnp.float32)
        return x
    x = _rec_inputs()
    def _L0_conv_setup():
        import jax, jax.numpy as jnp
        import numpy as np
        B, C, H, W = (2, 192, 128, 128)
        HEADS = 4
        M = 128
        RD = 10
        GS = 256
        TDF = 16
        HID = 4 * C
        HIDT = HID + TDF
        KS = 5

        def _ln(x, g, b):
            mu = x.mean(-1, keepdims=True)
            var = ((x - mu) ** 2).mean(-1, keepdims=True)
            return (x - mu) / jnp.sqrt(var + 1e-05) * g + b

        def _gelu(x):
            return jax.nn.gelu(x, approximate=False)
        key = jax.random.key(seed)
        ks = jax.random.split(key, 16)
        s = 0.02
        inp = {'x': jax.random.normal(ks[0], (B, C, H, W), jnp.float32), 'x_size': H, 'td': jax.random.normal(ks[1], (M, C), jnp.float32), 'g1': jnp.ones((C,)), 'b1': jnp.zeros((C,)), 'g2': jnp.ones((C,)), 'b2': jnp.zeros((C,)), 'g3': jnp.ones((C,)), 'b3': jnp.zeros((C,)), 'wq_w': jax.random.normal(ks[2], (C, RD)) * s, 'wq_b': jnp.zeros((RD,)), 'wk_w': jax.random.normal(ks[3], (C, RD)) * s, 'wk_b': jnp.zeros((RD,)), 'wv_w': jax.random.normal(ks[4], (C, C)) * s, 'wv_b': jnp.zeros((C,)), 'ca_scale': jnp.ones((1,)), 'wqkv_w': jax.random.normal(ks[5], (C, 3 * C)) * s, 'wqkv_b': jnp.zeros((3 * C,)), 'proj_w': jax.random.normal(ks[6], (C, C)) * s, 'proj_b': jnp.zeros((C,)), 'fc_td_w': jax.random.normal(ks[7], (C, TDF)) * s, 'fc_td_b': jnp.zeros((TDF,)), 'fc1_w': jax.random.normal(ks[8], (C, HID)) * s, 'fc1_b': jnp.zeros((HID,)), 'dw_w': jax.random.normal(ks[9], (HIDT, 1, KS, KS)) * s, 'dw_b': jnp.zeros((HIDT,)), 'fc2_w': jax.random.normal(ks[10], (HIDT, C)) * s, 'fc2_b': jnp.zeros((C,))}
        return inp
    _L0_conv_all = _L0_conv_setup()
    _L0_conv_in = {k: v for k, v in _L0_conv_all.items() if k in ('td', 'g1', 'b1', 'g2', 'b2', 'g3', 'b3', 'wq_w', 'wq_b', 'wk_w', 'wk_b', 'wv_w', 'wv_b', 'ca_scale', 'wqkv_w', 'wqkv_b', 'proj_w', 'proj_b', 'fc_td_w', 'fc_td_b', 'fc1_w', 'fc1_b', 'dw_w', 'dw_b', 'fc2_w', 'fc2_b', )}
    del _L0_conv_all

    def _L1_conv_setup():
        import jax, jax.numpy as jnp
        import numpy as np
        from jax import lax
        C_IN = 192
        NUM_WINDOWS = 8
        WINDOWS = [NUM_WINDOWS // 2, NUM_WINDOWS, NUM_WINDOWS + NUM_WINDOWS // 2]
        CB = C_IN // len(WINDOWS)

        def _conv1x1(x, w, b=None):
            y = jnp.einsum('nchw,oc->nohw', x, w)
            if b is not None:
                y = y + b[None, :, None, None]
            return y

        def _se(x, wse1, wse2):
            y = jnp.mean(x, axis=(2, 3))
            y = jax.nn.relu(jnp.einsum('bc,oc->bo', y, wse1))
            y = jax.nn.sigmoid(jnp.einsum('bc,oc->bo', y, wse2))
            return x * y[:, :, None, None]

        def _dwconv3x3(x, w, b):
            y = lax.conv_general_dilated(x, w, window_strides=(1, 1), padding=((1, 1), (1, 1)), feature_group_count=CB, dimension_numbers=('NCHW', 'OIHW', 'NCHW'))
            return y + b[None, :, None, None]
        key = jax.random.key(seed)
        ks = jax.random.split(key, 8)
        N, H, W = (16, 100, 100)
        rn = lambda k, s, sc: jax.random.normal(k, s, jnp.float32) * sc
        return {'x': rn(ks[0], (N, C_IN, H, W), 1.0), 'w1': rn(ks[1], (CB, C_IN), 0.05), 'b1': jnp.zeros((CB,), jnp.float32), 'w2': rn(ks[2], (CB, CB), 0.05), 'b2': jnp.zeros((CB,), jnp.float32), 'w3': rn(ks[3], (C_IN, 3 * CB), 0.05), 'b3': jnp.zeros((C_IN,), jnp.float32), 'wpos': rn(ks[4], (CB, 1, 3, 3), 0.1), 'bpos': jnp.zeros((CB,), jnp.float32), 'wse1': rn(ks[5], (CB // 16, CB), 0.1), 'wse2': rn(ks[6], (CB, CB // 16), 0.1)}
    _L1_conv_all = _L1_conv_setup()
    _L1_conv_in = {k: v for k, v in _L1_conv_all.items() if k in ('w1', 'b1', 'w2', 'b2', 'w3', 'b3', 'wpos', 'bpos', 'wse1', 'wse2', )}
    del _L1_conv_all

    return {
        "x": x,
        "L0_conv_td": _L0_conv_in["td"],
        "L0_conv_g1": _L0_conv_in["g1"],
        "L0_conv_b1": _L0_conv_in["b1"],
        "L0_conv_g2": _L0_conv_in["g2"],
        "L0_conv_b2": _L0_conv_in["b2"],
        "L0_conv_g3": _L0_conv_in["g3"],
        "L0_conv_b3": _L0_conv_in["b3"],
        "L0_conv_wq_w": _L0_conv_in["wq_w"],
        "L0_conv_wq_b": _L0_conv_in["wq_b"],
        "L0_conv_wk_w": _L0_conv_in["wk_w"],
        "L0_conv_wk_b": _L0_conv_in["wk_b"],
        "L0_conv_wv_w": _L0_conv_in["wv_w"],
        "L0_conv_wv_b": _L0_conv_in["wv_b"],
        "L0_conv_ca_scale": _L0_conv_in["ca_scale"],
        "L0_conv_wqkv_w": _L0_conv_in["wqkv_w"],
        "L0_conv_wqkv_b": _L0_conv_in["wqkv_b"],
        "L0_conv_proj_w": _L0_conv_in["proj_w"],
        "L0_conv_proj_b": _L0_conv_in["proj_b"],
        "L0_conv_fc_td_w": _L0_conv_in["fc_td_w"],
        "L0_conv_fc_td_b": _L0_conv_in["fc_td_b"],
        "L0_conv_fc1_w": _L0_conv_in["fc1_w"],
        "L0_conv_fc1_b": _L0_conv_in["fc1_b"],
        "L0_conv_dw_w": _L0_conv_in["dw_w"],
        "L0_conv_dw_b": _L0_conv_in["dw_b"],
        "L0_conv_fc2_w": _L0_conv_in["fc2_w"],
        "L0_conv_fc2_b": _L0_conv_in["fc2_b"],
        "L1_conv_w1": _L1_conv_in["w1"],
        "L1_conv_b1": _L1_conv_in["b1"],
        "L1_conv_w2": _L1_conv_in["w2"],
        "L1_conv_b2": _L1_conv_in["b2"],
        "L1_conv_w3": _L1_conv_in["w3"],
        "L1_conv_b3": _L1_conv_in["b3"],
        "L1_conv_wpos": _L1_conv_in["wpos"],
        "L1_conv_bpos": _L1_conv_in["bpos"],
        "L1_conv_wse1": _L1_conv_in["wse1"],
        "L1_conv_wse2": _L1_conv_in["wse2"],
    }

def reference(x, L0_conv_td, L0_conv_g1, L0_conv_b1, L0_conv_g2, L0_conv_b2, L0_conv_g3, L0_conv_b3, L0_conv_wq_w, L0_conv_wq_b, L0_conv_wk_w, L0_conv_wk_b, L0_conv_wv_w, L0_conv_wv_b, L0_conv_ca_scale, L0_conv_wqkv_w, L0_conv_wqkv_b, L0_conv_proj_w, L0_conv_proj_b, L0_conv_fc_td_w, L0_conv_fc_td_b, L0_conv_fc1_w, L0_conv_fc1_b, L0_conv_dw_w, L0_conv_dw_b, L0_conv_fc2_w, L0_conv_fc2_b, L1_conv_w1, L1_conv_b1, L1_conv_w2, L1_conv_b2, L1_conv_w3, L1_conv_b3, L1_conv_wpos, L1_conv_bpos, L1_conv_wse1, L1_conv_wse2):
    import jax
    import jax.numpy as jnp
    def _L0_conv_ref(x, x_size, td, g1, b1, g2, b2, g3, b3, wq_w, wq_b, wk_w, wk_b, wv_w, wv_b, ca_scale, wqkv_w, wqkv_b, proj_w, proj_b, fc_td_w, fc_td_b, fc1_w, fc1_b, dw_w, dw_b, fc2_w, fc2_b):
        import jax, jax.numpy as jnp
        import numpy as np
        B, C, H, W = (2, 192, 128, 128)
        HEADS = 4
        M = 128
        RD = 10
        GS = 256
        TDF = 16
        HID = 4 * C
        HIDT = HID + TDF
        KS = 5

        def _ln(x, g, b):
            mu = x.mean(-1, keepdims=True)
            var = ((x - mu) ** 2).mean(-1, keepdims=True)
            return (x - mu) / jnp.sqrt(var + 1e-05) * g + b

        def _gelu(x):
            return jax.nn.gelu(x, approximate=False)
        b, c, h, w = x.shape
        n = h * w
        xs = x.reshape(b, c, n).transpose(0, 2, 1)
        shortcut = xs
        xn = _ln(xs, g1, b1)
        q = xn @ wq_w + wq_b
        k = td @ wk_w + wk_b
        v = td @ wv_w + wv_b
        qn = q / jnp.maximum(jnp.linalg.norm(q, axis=-1, keepdims=True), 1e-12)
        kn = k / jnp.maximum(jnp.linalg.norm(k, axis=-1, keepdims=True), 1e-12)
        sim = jnp.einsum('bnr,mr->bnm', qn, kn)
        scale = 1.0 + jnp.clip(ca_scale, 0.0, 3.0) * np.log(M)
        sim = jax.nn.softmax(sim * scale, axis=-1)
        x_atd = jnp.einsum('bnm,mc->bnc', sim, v)
        tk_id = jnp.argmax(sim, axis=-1)
        qkv = xn @ wqkv_w + wqkv_b
        sort_idx = jnp.argsort(tk_id, axis=-1)
        inv_idx = jnp.argsort(sort_idx, axis=-1)
        shuf = jnp.take_along_axis(qkv, sort_idx[:, :, None], axis=1)
        gs = min(n, GS)
        ng = (n + gs - 1) // gs
        pad_n = ng * gs - n
        pad = jnp.flip(shuf[:, n - pad_n:n, :], axis=1)
        padded = jnp.concatenate([shuf, pad], axis=1)
        hd = c // HEADS
        y = padded.reshape(b, ng, gs, 3, HEADS, hd)
        y = jnp.transpose(y, (3, 0, 1, 4, 2, 5))
        q2, k2, v2 = (y[0], y[1], y[2])
        attn = jnp.einsum('bghqd,bghkd->bghqk', q2, k2) * hd ** (-0.5)
        attn = jax.nn.softmax(attn, axis=-1)
        o = jnp.einsum('bghqk,bghkd->bghqd', attn, v2)
        o = jnp.transpose(o, (0, 1, 3, 2, 4)).reshape(b, ng * gs, c)[:, :n, :]
        o = jnp.take_along_axis(o, inv_idx[:, :, None], axis=1)
        x_aca = o @ proj_w + proj_b
        td_feat = td @ fc_td_w + fc_td_b
        x_td = jnp.take(td_feat, tk_id, axis=0)
        xn2 = _ln(xs, g2, b2)
        h1 = _gelu(xn2 @ fc1_w + fc1_b)
        hcat = jnp.concatenate([h1, x_td], axis=-1)
        img = hcat.transpose(0, 2, 1).reshape(b, HIDT, h, w)
        conv = jax.lax.conv_general_dilated(img, dw_w, window_strides=(1, 1), padding=((KS // 2, KS // 2),) * 2, dimension_numbers=('NCHW', 'OIHW', 'NCHW'), feature_group_count=HIDT)
        conv = _gelu(conv + dw_b[None, :, None, None])
        conv = conv.reshape(b, HIDT, n).transpose(0, 2, 1)
        x_ffn = (hcat + conv) @ fc2_w + fc2_b
        x_ffn = _ln(x_ffn, g3, b3)
        out = shortcut + x_atd + x_aca + x_ffn
        return out.transpose(0, 2, 1).reshape(b, c, h, w)

    def _L1_conv_ref(x, w1, b1, w2, b2, w3, b3, wpos, bpos, wse1, wse2):
        import jax, jax.numpy as jnp
        import numpy as np
        from jax import lax
        C_IN = 192
        NUM_WINDOWS = 8
        WINDOWS = [NUM_WINDOWS // 2, NUM_WINDOWS, NUM_WINDOWS + NUM_WINDOWS // 2]
        CB = C_IN // len(WINDOWS)

        def _conv1x1(x, w, b=None):
            y = jnp.einsum('nchw,oc->nohw', x, w)
            if b is not None:
                y = y + b[None, :, None, None]
            return y

        def _se(x, wse1, wse2):
            y = jnp.mean(x, axis=(2, 3))
            y = jax.nn.relu(jnp.einsum('bc,oc->bo', y, wse1))
            y = jax.nn.sigmoid(jnp.einsum('bc,oc->bo', y, wse2))
            return x * y[:, :, None, None]

        def _dwconv3x3(x, w, b):
            y = lax.conv_general_dilated(x, w, window_strides=(1, 1), padding=((1, 1), (1, 1)), feature_group_count=CB, dimension_numbers=('NCHW', 'OIHW', 'NCHW'))
            return y + b[None, :, None, None]
        xc = _conv1x1(x, w1, b1)
        N, C, H, W = xc.shape
        out_list = []
        for nw in WINDOWS:
            s = H // nw
            k = s + H % nw
            hi = (jnp.arange(nw) * s)[:, None] + jnp.arange(k)[None, :]
            patches = xc[:, :, hi][..., hi]
            u3 = patches.transpose(0, 1, 3, 5, 2, 4).reshape(N, C * k * k, nw * nw)
            u4 = u3.reshape(-1, C, k, k)
            a = _se(_conv1x1(u4, w2, b2), wse1, wse2) + _dwconv3x3(u4, wpos, bpos)
            a3 = a.reshape(N, C * k * k, nw * nw)
            p = a3.reshape(N, C, k, k, nw, nw).transpose(0, 1, 4, 2, 5, 3)
            hidx = hi[:, :, None, None]
            widx = hi[None, None, :, :]
            folded = jnp.zeros((N, C, H, W), xc.dtype).at[:, :, hidx, widx].add(p)
            cnt = jnp.zeros((H, W), xc.dtype).at[hidx, widx].add(jnp.ones((nw, k, nw, k), xc.dtype))
            out_list.append(folded / cnt[None, None, :, :])
        out = _conv1x1(jnp.concatenate(out_list, axis=1) + x, w3, b3)
        return out

    def _gn(v, G=32, eps=1e-5):
        B_, C_, H_, W_ = v.shape
        g = v.reshape(B_, G, C_ // G, H_, W_)
        m = jnp.mean(g, axis=(2, 3, 4), keepdims=True)
        s = jnp.var(g, axis=(2, 3, 4), keepdims=True)
        return ((g - m) / jnp.sqrt(s + eps)).reshape(v.shape)

    def _ln_c(v, eps=1e-6):
        m = jnp.mean(v, axis=1, keepdims=True)
        s = jnp.var(v, axis=1, keepdims=True)
        return (v - m) / jnp.sqrt(s + eps)

    def _ln_t(v, eps=1e-5):
        m = jnp.mean(v, axis=-1, keepdims=True)
        s = jnp.var(v, axis=-1, keepdims=True)
        return (v - m) / jnp.sqrt(s + eps)

    def _to_tokens(v):
        B_, C_, H_, W_ = v.shape
        return v.reshape(B_, C_, H_ * W_).transpose(0, 2, 1)
    def _from_tokens(t, like):
        B_, C_, H_, W_ = like.shape
        return t.transpose(0, 2, 1).reshape(B_, C_, H_, W_)

    x = _L0_conv_ref(x, 128, L0_conv_td, L0_conv_g1, L0_conv_b1, L0_conv_g2, L0_conv_b2, L0_conv_g3, L0_conv_b3, L0_conv_wq_w, L0_conv_wq_b, L0_conv_wk_w, L0_conv_wk_b, L0_conv_wv_w, L0_conv_wv_b, L0_conv_ca_scale, L0_conv_wqkv_w, L0_conv_wqkv_b, L0_conv_proj_w, L0_conv_proj_b, L0_conv_fc_td_w, L0_conv_fc_td_b, L0_conv_fc1_w, L0_conv_fc1_b, L0_conv_dw_w, L0_conv_dw_b, L0_conv_fc2_w, L0_conv_fc2_b)
    x = _L1_conv_ref(x, L1_conv_w1, L1_conv_b1, L1_conv_w2, L1_conv_b2, L1_conv_w3, L1_conv_b3, L1_conv_wpos, L1_conv_bpos, L1_conv_wse1, L1_conv_wse2)
    return x


_drawn_inputs = setup_inputs


def setup_inputs(seed=0):
    import zlib

    import numpy as np

    out = dict(_drawn_inputs(seed))
    spreads = {'L0_conv_g1': (1.0, 0.2),
     'L0_conv_b1': (0.0, 0.1),
     'L0_conv_g2': (1.0, 0.2),
     'L0_conv_b2': (0.0, 0.1),
     'L0_conv_g3': (1.0, 0.2),
     'L0_conv_b3': (0.0, 0.1),
     'L0_conv_wq_b': (0.0, 0.1),
     'L0_conv_wk_b': (0.0, 0.1),
     'L0_conv_wv_b': (0.0, 0.1),
     'L0_conv_wqkv_b': (0.0, 0.435),
     'L0_conv_proj_b': (0.0, 0.1),
     'L0_conv_fc_td_b': (0.0, 0.302),
     'L0_conv_fc1_b': (0.0, 0.1),
     'L0_conv_dw_b': (0.0, 0.1),
     'L0_conv_fc2_b': (0.0, 0.1),
     'L1_conv_b1': (0.0, 0.343),
     'L1_conv_b2': (0.0, 0.1),
     'L1_conv_b3': (0.0, 0.1),
     'L1_conv_bpos': (0.0, 0.1)}
    factors = {'L0_conv_wqkv_w': 6.139, 'L0_conv_proj_w': 2.784, 'L1_conv_wse1': 8.0, 'L1_conv_wse2': 8.0}
    for name, (base, spread) in spreads.items():
        noise = np.random.default_rng([zlib.crc32(name.encode()), seed]).standard_normal(out[name].shape)
        drawn = base * np.exp(spread * noise) if base else spread * noise
        out[name] = jnp.asarray(drawn.astype(out[name].dtype))
    for name, factor in factors.items():
        out[name] = (out[name] * factor).astype(out[name].dtype)
    return out
```

```python
from contextlib import ExitStack

import numpy as np

import concourse.bass as bass
from concourse import mybir

ALU = mybir.AluOpType
ACT = mybir.ActivationFunctionType
AX = mybir.AxisListType
F32 = mybir.dt.float32
BF16 = mybir.dt.bfloat16
I32 = mybir.dt.int32
U32 = mybir.dt.uint32

B, C, H, W = 2, 192, 128, 128
N = H * W
P = 128
KC = C // 2
M = 128
RD = 10
HEADS, HD = 4, C // 4
GS = 256
TDF = 16
HID = 4 * C
KS = 5
PADY = KS // 2
HP = H + 2 * PADY
BT = 512
TT = BT // P
NB = N // BT
EPS = 1e-5


class Scratch:
    pass


def scratch(nc):
    d = Scratch()

    def t(name, shape, dt=F32):
        return nc.dram_tensor(name, shape, dt, kind="Internal").ap()

    d.xh = t("xhat_rows", (B * N, C))
    d.xt = t("xhat_chan", (B, C + 1, HP * W))
    d.td = t("td_chan", (B, TDF, HP * W))
    d.res = t("res_chan", (B, C, N))
    d.xs = t("xhat_sorted", (B * N, C))
    d.pos = t("sorted_pos", (P, B * N // P), I32)
    d.aca = t("attn_sorted", (B * N, C))
    d.tdc = t("td_sum", (B, TDF, N))
    d.x1 = t("x1_chan", (B, C, N))
    d.xc = t("xc_chan", (B, C // 3, N))
    d.u = [t(f"cut_{nw}", (B, CB, (window(nw)[1] * nw) ** 2)) for nw in WINDOWS]
    d.v = [t(f"worked_{nw}", (B, CB, (window(nw)[1] * nw) ** 2)) for nw in WINDOWS]
    d.cat = t("folded", (B, C, N))
    return d


def at(ap, lo, n):
    return ap[:, bass.ds(lo, n)]


class Link:

    def __init__(self, eng, sem):
        self.eng, self.sem, self.base, self.n = eng, sem, 0, 0

    def loop(self, i, per):
        self.base, self.n, self.per = self.base + self.n + i * per, 0, per

    def end(self, total):
        assert self.n == self.per, (self.n, self.per)
        self.base, self.n = total, 0

    def __call__(self, ins):
        ins.then_inc(self.sem, 1)
        self.n += 1
        self.eng.wait_ge(self.sem, self.base + self.n)


def phase_tokens(nc, sems, a, d):
    with ExitStack() as mem:
        def sb(name, shape, dt=F32):
            return mem.enter_context(nc.sbuf_tensor("t_" + name, shape, dt))

        def ps(name, shape, dt=F32):
            return mem.enter_context(nc.psum_tensor("t_" + name, shape, dt))

        def sem(name):
            return sems.new("t_" + name)

        ident = sb("ident", [P, P])
        identb = sb("identb", [P, P], BF16)
        onesb = sb("onesb", [P, P], BF16)
        tri = sb("tri", [P, P], BF16)
        onesf = sb("onesf", [P, P])
        zeros = sb("zeros", [P, 2 * W])
        iota = sb("iota", [P, P])
        tdr = sb("tdr", [P, C])
        tdT = sb("tdT", [KC, 2, P])
        g1 = sb("g1", [KC, 2])
        b1 = sb("b1", [KC, 2])
        wq = sb("wq", [KC, 2, RD])
        wqg = sb("wqg", [KC, 2, RD])
        wk = sb("wk", [KC, 2, RD])
        wv = sb("wv", [KC, 2, C])
        wt = sb("wt", [KC, 2, TDF])
        rows = sb("rows", [1, RD + RD + C + TDF])
        bq = sb("bq", [1, RD])
        ca = sb("ca", [P, 1])
        k0 = sb("k0", [P, RD])
        ksq = sb("ksq", [P, RD])
        kn2 = sb("kn2", [P, 1])
        kT = sb("kT", [RD, P])
        v = sb("v", [P, C])
        tdf = sb("tdf", [P, TDF])

        xin = sb("xin", [KC, 2, 2, BT])
        st6 = sb("st6", [P, TT, 6])
        mv = sb("mv", [P, TT, 2])
        rstd = sb("rstd", [P, TT])
        xh = sb("xh", [P, TT, C])
        xT = sb("xT", [KC, 2, BT])
        q = sb("q", [P, TT, RD])
        qsq = sb("qsq", [P, TT, RD])
        qn2 = sb("qn2", [P, TT])
        qn = sb("qn", [P, TT, RD])
        qT = sb("qT", [RD, BT])
        mx = sb("mx", [P, TT, 8])
        ix = sb("ix", [P, TT, 8], U32)
        nmx = sb("nmx", [P, TT])
        e = sb("e", [P, TT, M])
        esum = sb("esum", [P, TT])
        erec = sb("erec", [P, TT])
        pr = sb("pr", [P, TT, M])
        prT = sb("prT", [P, BT])
        cat = sb("cat", [P, TT])
        oh = sb("oh", [P, TT, M], BF16)
        ohT = sb("ohT", [P, BT])
        tdx = sb("tdx", [TDF, BT])
        rk = sb("rk", [P, TT, M])
        res = sb("res", [KC, 2, BT])
        seen = sb("seen", [P, M])
        cats = sb("cats", [P, B * NB * TT])
        rank = sb("rank", [P, B * NB * TT])
        tot = sb("tot", [P, B, M])
        ends = sb("ends", [P, B, M])
        off = sb("off", [P, B, M])
        pick = sb("pick", [P, M])
        eq = sb("eq", [P, M])
        posf = sb("posf", [P, B * NB * TT])
        posi = sb("posi", [P, B * NB * TT], I32)

        pT = ps("pT", [P, 2, 512])
        pX = ps("pX", [KC, 2, BT])
        pS = ps("pS", [P, TT, M])
        pP = ps("pP", [P, BT])
        pO = ps("pO", [P, BT], BF16)
        pR = ps("pR", [P, TT, M])
        pQ = pT[:, 0, 0:TT * RD].rearrange("p (t r) -> p t r", t=TT)
        pQT = pT[0:RD, 1, :]
        pD = pP[0:TDF, :]
        pN = pT[:, 0, 128:128 + M]

        marks = sem("marks")
        s_var = sem("s_var")
        s_rs = sem("s_rs")
        s_sq = sem("s_sq")
        s_pw = sem("s_pw")
        con = sem("con")
        made = sem("made")
        pads = sem("pads")
        x_in = [sem(f"x_in{h}") for h in range(2)]
        x_free = sem("x_free")
        pe = sem("pe")
        dv = sem("dv")
        dvp = sem("dvp")
        s_xT = sem("s_xT")
        s_xh = sem("s_xh")
        s_xb = sem("s_xb")
        s_xc = sem("s_xc")
        s_q = sem("s_q")
        s_qn = sem("s_qn")
        s_qt = sem("s_qt")
        s_qc = sem("s_qc")
        s_s = sem("s_s")
        s_m = sem("s_m")
        s_e = sem("s_e")
        s_p = sem("s_p")
        s_oh = sem("s_oh")
        s_pt = sem("s_pt")
        s_pc = sem("s_pc")
        s_ot = sem("s_ot")
        s_oc = sem("s_oc")
        s_a = sem("s_a")
        s_r = sem("s_r")
        s_d = sem("s_d")
        s_dc = sem("s_dc")
        s_res = sem("s_res")
        s_rk = sem("s_rk")
        o_xh = sem("o_xh")
        o_xT = sem("o_xT")
        o_td = sem("o_td")
        o_res = sem("o_res")
        s_seen = sem("s_seen")
        s_tot = sem("s_tot")
        s_cum = sem("s_cum")
        s_pos = sem("s_pos")
        o_pos = sem("o_pos")

        CON = 12
        x_v = a["x"].rearrange("b (k p) h w -> b p k (h w)", k=2)
        xt_v = d.xt[:, 0:C, :].rearrange("b (k p) n -> b p k n", k=2)
        res_v = d.res.rearrange("b (k p) n -> b p k n", k=2)
        xh_v = d.xh.rearrange("(n t p) c -> n p t c", t=TT, p=P)

        with nc.Block() as block:
            @block.sync
            def _(sp):
                def col(dst, src):
                    sp.dma_start(dst, src).then_inc(con, 16)

                with nc.allow_non_contiguous_dma('small constants'):
                    col(g1[:, :], a["L0_conv_g1"].rearrange("(k p) -> p k", k=2))
                    col(b1[:, :], a["L0_conv_b1"].rearrange("(k p) -> p k", k=2))
                    col(tdr[:, :], a["L0_conv_td"])
                    col(wq[:, :, :], a["L0_conv_wq_w"].rearrange("(k p) r -> p k r", k=2))
                    col(wk[:, :, :], a["L0_conv_wk_w"].rearrange("(k p) r -> p k r", k=2))
                    col(wv[:, :, :], a["L0_conv_wv_w"].rearrange("(k p) r -> p k r", k=2))
                    col(wt[:, :, :], a["L0_conv_fc_td_w"].rearrange("(k p) r -> p k r", k=2))
                    at0 = 0
                    for name in ("wq_b", "wk_b", "wv_b", "fc_td_b"):
                        src = a["L0_conv_" + name]
                        n = src.shape[0]
                        col(rows[:, at0:at0 + n], src.rearrange("(a n) -> a n", a=1))
                        at0 += n
                    col(ca[:, :], a["L0_conv_ca_scale"].rearrange("(a n) -> a n", a=1).broadcast_to([P, 1]))
                with sp.Fori(0, B) as b:
                    with sp.Fori(0, NB // 2) as jj:
                        for half in range(2):
                            j = jj * 2 + half
                            i = b * NB + j
                            sp.wait_ge(s_res, i + 2)
                            sp.dma_start(res_v[bass.ds(b, 1), :, :, bass.ds(j * BT, BT)]
                                         .rearrange("b p k n -> (b p) k n"), res[:, :, :]).then_inc(o_res, 16)
                sp.wait_ge(o_res, 16 * B * NB + 16)
                sp.wait_ge(s_pos, 1)
                sp.dma_start(d.pos, posi[:, :]).then_inc(o_pos, 16)
                sp.wait_ge(o_pos, 16)

            @block.gpsimd
            def _(gp):
                nc.gpsimd.memset(ident[:, :], 0.0).then_inc(made, 1)
                nc.gpsimd.memset(identb[:, :], 0.0).then_inc(made, 1)
                nc.gpsimd.memset(tri[:, :], 1.0).then_inc(made, 1)
                nc.gpsimd.memset(onesb[:, :], 1.0).then_inc(made, 1)
                nc.gpsimd.memset(onesf[:, :], 1.0).then_inc(made, 1)
                nc.gpsimd.memset(zeros[:, :], 0.0).then_inc(made, 1)
                gp.wait_ge(made, 6)
                for m in (ident, identb):
                    nc.gpsimd.affine_select(out=m[:, :], in_=m[:, :], compare_op=ALU.not_equal, fill=1.0,
                                            base=0, pattern=[[-1, P]], channel_multiplier=1).then_inc(made, 1)
                nc.gpsimd.affine_select(out=tri[:, :], in_=tri[:, :], compare_op=ALU.is_gt, fill=0.0,
                                        base=0, pattern=[[1, P]], channel_multiplier=-1).then_inc(made, 1)
                nc.gpsimd.iota(iota[:, :], pattern=[[1, P]], base=0, channel_multiplier=0,
                               allow_small_or_imprecise_dtypes=True).then_inc(made, 1)
                gp.wait_ge(made, 10)
                edge = PADY * W
                for b in range(B):
                    for lo in (0, edge + N):
                        for c0, n in ((0, P), (P, C + 1 - P)):
                            gp.dma_start(d.xt[b, c0:c0 + n, lo:lo + edge], zeros[0:n, :]).then_inc(pads, 16)
                        gp.dma_start(d.td[b, :, lo:lo + edge], zeros[0:TDF, :]).then_inc(pads, 16)
                    gp.dma_start(d.xt[b, C, edge:edge + N].rearrange("(h w) -> h w", h=H),
                                 onesf[:, :]).then_inc(pads, 16)
                gp.wait_ge(pads, 16 * B * 7)
                with gp.Fori(0, B) as b:
                    with gp.Fori(0, NB // 2) as jj:
                        for half in range(2):
                            j = jj * 2 + half
                            i = b * NB + j
                            gp.wait_ge(x_free, i + 1)
                            gp.dma_start(xin[:, :, half, :],
                                         x_v[bass.ds(b, 1), :, :, bass.ds(j * BT, BT)]
                                         .rearrange("b p k n -> (b p) k n")).then_inc(x_in[half], 16)

            @block.tensor
            def _(te):
                te.wait_ge(made, 10)
                te.wait_ge(con, 16 * CON)
                te.wait_ge(dvp, 1)
                for k in range(2):
                    nc.tensor.transpose(pT[0:KC, 0, k * P:(k + 1) * P], tdr[:, k * KC:(k + 1) * KC],
                                        ident[:, :]).then_inc(pe, 1)
                te.wait_ge(dvp, 2)
                at0 = RD
                for o, w_, n in ((0, wk, RD), (16, wv, C), (256, wt, TDF)):
                    dst = pT[:, 1, o:o + n]
                    for k in range(2):
                        nc.tensor.matmul(dst, tdT[:, k, :], w_[:, k, :], start=(k == 0), stop=False)
                    nc.tensor.matmul(dst, onesf[0:1, :], rows[:, at0:at0 + n], start=False, stop=True).then_inc(pe, 1)
                    at0 += n
                for k in range(2):
                    nc.tensor.matmul(pS[0:1, 0, 0:RD], b1[:, k:k + 1], wq[:, k, :], start=(k == 0),
                                     stop=(k == 1)).then_inc(pe, 1)
                te.wait_ge(dvp, 3)
                nc.tensor.transpose(pS[0:RD, 1, :], k0[:, :], ident[:, :]).then_inc(pe, 1)
                te.wait_ge(dvp, 4)
                with te.Fori(0, B * NB // 2) as ii:
                    for half in range(2):
                        i = ii * 2 + half
                        te.wait_ge(x_in[half], ii * 16 + 16)
                        te.wait_ge(s_qn, i + 1)
                        te.wait_ge(s_qc, i + 1)
                        te.wait_ge(s_rk, i + 1)
                        for t in range(TT):
                            for k in range(2):
                                mm = nc.tensor.transpose(
                                    pT[:, t // 2, (t % 2) * C + k * KC:(t % 2) * C + (k + 1) * KC],
                                    xin[:, k, half, t * P:(t + 1) * P],
                                    ident[0:KC, 0:KC])
                        mm.then_inc(s_xT, 1)
                        te.wait_ge(s_xh, i + 1)
                        te.wait_ge(s_res, i + 1)
                        for t in range(TT):
                            for k in range(2):
                                mm = nc.tensor.transpose(pX[:, k, t * P:(t + 1) * P], xh[:, t, k * KC:(k + 1) * KC],
                                                         ident[:, :])
                        mm.then_inc(s_xb, 1)
                        te.wait_ge(s_xc, i + 2)
                        for t in range(TT):
                            for k in range(2):
                                nc.tensor.matmul(pQ[:, t, :], xT[:, k, t * P:(t + 1) * P], wqg[:, k, :],
                                                 start=(k == 0), stop=False)
                            mm = nc.tensor.matmul(pQ[:, t, :], onesf[0:1, :], bq[:, :], start=False, stop=True)
                        mm.then_inc(s_q, 1)
                        te.wait_ge(s_qn, i + 2)
                        for t in range(TT):
                            mm = nc.tensor.transpose(pQT[:, t * P:(t + 1) * P], qn[:, t, :], ident[:, :])
                        mm.then_inc(s_qt, 1)
                        te.wait_ge(s_qc, i + 2)
                        for t in range(TT):
                            mm = nc.tensor.matmul(pS[:, t, :], qT[:, t * P:(t + 1) * P], kT[:, :], start=True, stop=True)
                        mm.then_inc(s_s, 1)
                        te.wait_ge(s_oh, i + 1)
                        for t in range(TT):
                            nc.tensor.matmul(pR[:, t, :], tri[:, :], oh[:, t, :], start=True, stop=(t == 0))
                            for u in range(t):
                                nc.tensor.matmul(pR[:, t, :], onesb[:, :], oh[:, u, :], start=False, stop=(u == t - 1))
                        for u in range(TT):
                            mm = nc.tensor.matmul(pN, onesb[:, :], oh[:, u, :], start=(u == 0), stop=(u == TT - 1))
                        mm.then_inc(s_r, 1)
                        for t in range(TT):
                            mm = nc.tensor.transpose(pO[:, t * P:(t + 1) * P], oh[:, t, :], identb[:, :])
                        mm.then_inc(s_ot, 1)
                        te.wait_ge(s_p, i + 1)
                        te.wait_ge(s_dc, i + 1)
                        for t in range(TT):
                            mm = nc.tensor.transpose(pP[:, t * P:(t + 1) * P], pr[:, t, :], ident[:, :])
                        mm.then_inc(s_pt, 1)
                        te.wait_ge(s_pc, i + 1)
                        for k in range(2):
                            mm = nc.tensor.matmul(pX[:, k, :], v[:, k * KC:(k + 1) * KC], prT[:, :], start=True, stop=True)
                        mm.then_inc(s_a, 1)
                        te.wait_ge(s_oc, i + 1)
                        nc.tensor.matmul(pD, tdf[:, :], ohT[:, :], start=True, stop=True).then_inc(s_d, 1)
                te.wait_ge(s_tot, 1)
                for b in range(B):
                    mm = nc.tensor.matmul(pS[:, b, :], onesf[:, :], ends[:, b, :], start=True, stop=True)
                mm.then_inc(s_cum, 1)

            @block.scalar
            def _(act):
                for s in (s_xc, s_qc, s_dc):
                    act.sem_inc(s, 1)
                act.sem_inc(o_xh, 16)
                act.sem_inc(o_xT, 16)
                act.sem_inc(o_td, 16)
                act.sem_inc(o_res, 16)
                act.wait_ge(s_sq, 1)
                nc.scalar.activation(kn2[:, :], kn2[:, :], ACT.Sqrt).then_inc(s_pw, 1)
                with act.Fori(0, B) as b:
                    with act.Fori(0, NB // 2) as jj:
                        for half in range(2):
                            j = jj * 2 + half
                            i = b * NB + j
                            act.wait_ge(s_var, i + 1)
                            nc.scalar.activation(rstd[:, :], rstd[:, :], ACT.Sqrt).then_inc(s_rs, 1)
                            act.wait_ge(s_xh, i + 1)
                            act.dma_start(xh_v[bass.ds(i, 1)].rearrange("a p t c -> (a p) t c"),
                                          xh[:, :, :]).then_inc(o_xh, 16)
                            act.wait_ge(s_xb, i + 1)
                            act.wait_ge(o_xT, i * 16 + 16)
                            nc.scalar.activation(xT[:, :, :], pX[:, :, :], ACT.Copy).then_inc(s_xc, 1)
                            act.wait_ge(s_xc, i + 2)
                            act.dma_start(xt_v[bass.ds(b, 1), :, :, bass.ds(j * BT + PADY * W, BT)]
                                          .rearrange("b p k n -> (b p) k n"), xT[:, :, :]).then_inc(o_xT, 16)
                            act.wait_ge(s_sq, i + 2)
                            nc.scalar.activation(qn2[:, :], qn2[:, :], ACT.Sqrt).then_inc(s_pw, 1)
                            act.wait_ge(s_qt, i + 1)
                            nc.scalar.activation(qT[:, :], pQT, ACT.Copy).then_inc(s_qc, 1)
                            act.wait_ge(s_m, i + 1)
                            for t in range(TT):
                                ins = nc.scalar.activation(e[:, t, :], pS[:, t, :], ACT.Exp, bias=nmx[:, t:t + 1],
                                                           scale=1.0, accum_out=esum[:, t:t + 1])
                            ins.then_inc(s_e, 1)
                            act.wait_ge(s_ot, i + 1)
                            nc.scalar.activation(ohT[:, :], pO[:, :], ACT.Copy).then_inc(s_oc, 1)
                            act.wait_ge(s_pt, i + 1)
                            nc.scalar.activation(prT[:, :], pP[:, :], ACT.Copy).then_inc(s_pc, 1)
                            act.wait_ge(s_d, i + 1)
                            act.wait_ge(o_td, i * 16 + 16)
                            nc.scalar.activation(tdx[:, :], pD, ACT.Copy).then_inc(s_dc, 1)
                            act.wait_ge(s_dc, i + 2)
                            act.dma_start(d.td[bass.ds(b, 1), :, bass.ds(j * BT + PADY * W, BT)]
                                          .rearrange("b p n -> (b p) n"), tdx[:, :]).then_inc(o_td, 16)
                act.wait_ge(o_xh, 16 * B * NB + 16)
                act.wait_ge(o_xT, 16 * B * NB + 16)
                act.wait_ge(o_td, 16 * B * NB + 16)

            @block.vector
            def _(ve):
                link = Link(ve, dv)
                ve.sem_inc(dvp, 1)
                ve.sem_inc(x_free, 2)
                ve.sem_inc(s_rk, 1)
                ve.wait_ge(con, 16 * CON)
                ve.wait_ge(pe, 2)
                nc.vector.tensor_copy(tdT[:, :, :], pT[0:KC, 0, 0:2 * P].rearrange("p (k n) -> p k n", k=2)).then_inc(dvp, 1)
                for k in range(2):
                    nc.vector.tensor_scalar(wqg[:, k, :], wq[:, k, :], g1[:, k:k + 1], None, ALU.mult)
                nc.vector.memset(seen[:, :], 0.0)
                link(nc.vector.tensor_scalar(ca[:, :], ca[:, :], 0.0, 3.0, ALU.max, ALU.min))
                link(nc.vector.tensor_scalar(ca[:, :], ca[:, :], float(np.log(M)), 1.0, ALU.mult, ALU.add))
                ve.wait_ge(pe, 5)
                link(nc.vector.tensor_copy(k0[:, :], pT[:, 1, 0:RD]))
                nc.vector.tensor_copy(v[:, :], pT[:, 1, 16:16 + C])
                nc.vector.tensor_copy(tdf[:, :], pT[:, 1, 256:256 + TDF])
                link(nc.vector.tensor_tensor(ksq[:, :], k0[:, :], k0[:, :], ALU.mult))
                link(nc.vector.tensor_reduce(kn2[:, :], ksq[:, :], AX.X, ALU.add))
                nc.vector.tensor_scalar(kn2[:, :], kn2[:, :], 1e-24, None, ALU.max).then_inc(s_sq, 1)
                ve.wait_ge(s_pw, 1)
                link(nc.vector.reciprocal(kn2[:, :], kn2[:, :]))
                nc.vector.tensor_scalar(k0[:, :], k0[:, :], kn2[:, 0:1], ca[:, 0:1], ALU.mult,
                                        ALU.mult).then_inc(dvp, 1)
                ve.wait_ge(pe, 8)
                nc.vector.tensor_copy(kT[:, :], pS[0:RD, 1, :])
                link(nc.vector.tensor_tensor(bq[:, :], pS[0:1, 0, 0:RD], rows[:, 0:RD], ALU.add))
                ve.sem_inc(s_qn, 1)
                ve.sem_inc(s_res, 1)
                ve.sem_inc(dvp, 1)
                per = 15
                start = link.n
                with ve.Fori(0, B) as b:
                    with ve.Fori(0, NB // 2) as jj:
                        for half in range(2):
                            j = jj * 2 + half
                            i = b * NB + j
                            link.base, link.n = i * per + start, 0
                            ve.wait_ge(s_xT, i + 1)
                            for t in range(TT):
                                ins = nc.vector.bn_stats(st6[:, t, :], pT[:, t // 2, (t % 2) * C:(t % 2) * C + C])
                            link(ins)
                            ve.sem_inc(marks, 1)
                            for t in range(TT):
                                ins = nc.vector.bn_aggr(mv[:, t, :], st6[:, t, :])
                            link(ins)
                            nc.vector.tensor_scalar(rstd[:, :], mv[:, :, 1], EPS, None, ALU.add).then_inc(s_var, 1)
                            ve.wait_ge(s_rs, i + 1)
                            link(nc.vector.reciprocal(rstd[:, :], rstd[:, :]))
                            ve.wait_ge(o_xh, i * 16 + 16)
                            for t in range(TT):
                                ins = nc.vector.tensor_scalar(xh[:, t, :], pT[:, t // 2, (t % 2) * C:(t % 2) * C + C],
                                                              mv[:, t, 0:1], rstd[:, t:t + 1], ALU.subtract, ALU.mult)
                            ins.then_inc(s_xh, 1)
                            ve.wait_ge(s_q, i + 1)
                            link(nc.vector.tensor_copy(q[:, :, :], pQ))
                            link(nc.vector.tensor_tensor(qsq[:, :, :], q[:, :, :], q[:, :, :], ALU.mult))
                            link(nc.vector.tensor_reduce(qn2[:, :], qsq[:, :, :], AX.X, ALU.add))
                            nc.vector.tensor_scalar(qn2[:, :], qn2[:, :], 1e-24, None, ALU.max).then_inc(s_sq, 1)
                            ve.wait_ge(s_pw, i + 2)
                            link(nc.vector.reciprocal(qn2[:, :], qn2[:, :]))
                            nc.vector.tensor_tensor(qn[:, :, :], q[:, :, :],
                                                    qn2[:, :].unsqueeze(2).to_broadcast([P, TT, RD]),
                                                    ALU.mult).then_inc(s_qn, 1)
                            ve.wait_ge(s_s, i + 1)
                            link(nc.vector.tensor_reduce(nmx[:, :], pS[:, :, :], AX.X, ALU.max))
                            nc.vector.tensor_scalar(nmx[:, :], nmx[:, :], -1.0, None, ALU.mult).then_inc(s_m, 1)
                            ve.wait_ge(s_e, i + 1)
                            ve.sem_inc(marks, 1)
                            for t in range(TT):
                                ins = nc.vector.max(mx[:, t, :], e[:, t, :])
                            link(ins)
                            ve.sem_inc(marks, 1)
                            for t in range(TT):
                                ins = nc.vector.max_index(ix[:, t, :], mx[:, t, :], e[:, t, :])
                            link(ins)
                            link(nc.vector.tensor_copy(cat[:, :], ix[:, :, 0]))
                            nc.vector.tensor_copy(at(cats, i * TT, TT), cat[:, :])
                            for t in range(TT):
                                ins = nc.vector.tensor_scalar(oh[:, t, :], iota[:, :], cat[:, t:t + 1], None, ALU.is_equal)
                            ins.then_inc(s_oh, 1)
                            link(nc.vector.reciprocal(erec[:, :], esum[:, :]))
                            for t in range(TT):
                                ins = nc.vector.tensor_scalar(pr[:, t, :], e[:, t, :], erec[:, t:t + 1], None, ALU.mult)
                            ins.then_inc(s_p, 1)
                            ve.wait_ge(s_r, i + 1)
                            link(nc.vector.tensor_tensor(rk[:, :, :], pR[:, :, :],
                                                         seen[:, :].unsqueeze(1).to_broadcast([P, TT, M]), ALU.add))
                            link(nc.vector.tensor_tensor(rk[:, :, :], rk[:, :, :], oh[:, :, :], ALU.mult))
                            nc.vector.tensor_reduce(at(rank, i * TT, TT), rk[:, :, :], AX.X, ALU.add)
                            link(nc.vector.tensor_tensor(seen[:, :], seen[:, :], pN, ALU.add))
                            ve.sem_inc(s_rk, 1)
                            ve.wait_ge(s_a, i + 1)
                            ve.wait_ge(o_res, i * 16 + 16)
                            nc.vector.tensor_tensor(res[:, :, :], pX[:, :, :],
                                                    xin[:, :, half, :],
                                                    ALU.add).then_inc(s_res, 1)
                            ve.wait_ge(s_res, i + 2)
                            ve.sem_inc(x_free, 1)
                            assert link.n == per, link.n
                    nc.vector.tensor_copy(tot[:, bass.ds(b, 1), :].rearrange("p a m -> p (a m)"),
                                          seen[:, :]).then_inc(s_seen, 1)
                    ve.wait_ge(s_seen, b + 1)
                link.base, link.n = B * NB * per + start, 0
                for b in range(B):
                    if b:
                        link(nc.vector.tensor_tensor(pick[:, :], tot[:, 1, :], tot[:, 0, :], ALU.subtract))
                    src = pick if b else tot[:, 0, :]
                    link(nc.vector.tensor_tensor(eq[:, :], src if b == 0 else pick[:, :], ident[:, :], ALU.mult))
                    link(nc.vector.tensor_reduce(kn2[:, :], eq[:, :], AX.X, ALU.add))
                    link(nc.vector.tensor_scalar(ends[:, b, :], tri[:, :], kn2[:, 0:1], None, ALU.mult))
                ve.sem_inc(s_tot, 1)
                ve.wait_ge(s_cum, 1)
                link(nc.vector.tensor_copy(off[:, 0, :], pS[:, 0, :]))
                link(nc.vector.tensor_tensor(eq[:, :], pS[:, 1, :], tot[:, 0, :], ALU.subtract))
                link(nc.vector.tensor_scalar(off[:, 1, :], eq[:, :], float(N), None, ALU.add))
                start2 = link.base + link.n
                with ve.Fori(0, B) as b:
                    with ve.Fori(0, NB) as j:
                        i = b * NB + j
                        link.base, link.n = i * 3 + start2, 0
                        link(nc.vector.tensor_tensor(rk[:, :, :], iota[:, :].unsqueeze(1).to_broadcast([P, TT, M]),
                                                     at(cats, i * TT, TT).unsqueeze(2).to_broadcast([P, TT, M]),
                                                     ALU.is_equal))
                        link(nc.vector.tensor_tensor(rk[:, :, :], rk[:, :, :],
                                                     off[:, bass.ds(b, 1), :].to_broadcast([P, TT, M]), ALU.mult))
                        link(nc.vector.tensor_reduce(at(posf, i * TT, TT), rk[:, :, :], AX.X, ALU.add))
                link.base, link.n = B * NB * 3 + start2, 0
                link(nc.vector.tensor_tensor(posf[:, :], posf[:, :], rank[:, :], ALU.add))
                nc.vector.tensor_copy(posi[:, :], posf[:, :]).then_inc(s_pos, 1)


def phase_sort(nc, sems, a, d):
    with ExitStack() as mem:
        def sb(name, shape, dt=F32):
            return mem.enter_context(nc.sbuf_tensor("s_" + name, shape, dt))

        def sem(name):
            return sems.new("s_" + name)

        pos = sb("pos", [P, B * N // P], I32)
        idx = sb("idx", [P, 2, TT], I32)
        rows = sb("rows", [P, 2, TT, C])
        pos_in = sem("pos_in")
        marks = sem("marks")
        rows_in = [sem(f"rows_in{h}") for h in range(2)]
        rows_out = [sem(f"rows_out{h}") for h in range(2)]
        rows_free = sem("rows_free")
        idx_set = sem("idx_set")
        xh_v = d.xh.rearrange("(n t p) c -> n p t c", t=TT, p=P)
        TURNS = B * N // P // TT

        with nc.Block() as block:
            @block.sync
            def _(sp):
                sp.dma_start(pos[:, :], d.pos).then_inc(pos_in, 16)
                with sp.Fori(0, TURNS // 2) as ii:
                    for half in range(2):
                        i = ii * 2 + half
                        sp.wait_ge(rows_free, i + 1)
                        sp.dma_start(rows[:, half, :, :],
                                     xh_v[bass.ds(i, 1)].rearrange("a p t c -> (a p) t c")).then_inc(rows_in[half], 16)

            @block.gpsimd
            def _(gp):
                gp.sem_inc(rows_free, 2)
                gp.wait_ge(pos_in, 16)

                def send(ii, half):
                    i = ii * 2 + half
                    nc.gpsimd.tensor_copy(idx[:, half, :], at(pos, i * TT, TT)).then_inc(idx_set, 1)
                    gp.wait_ge(idx_set, i + 1)
                    gp.wait_ge(rows_in[half], ii * 16 + 16)
                    gp.sem_inc(marks, 1)
                    for t in range(TT):
                        gp.indirect_dma_start(d.xs[:, :], bass.IndirectOffsetOnAxis(ap=idx[:, half, t:t + 1], axis=0),
                                              rows[:, half, t, :], None).then_inc(rows_out[half], 16)

                def sent(ii, half):
                    gp.wait_ge(rows_out[half], ii * (16 * TT) + 16 * TT)
                    gp.sem_inc(rows_free, 1)

                send(0, 0)
                with gp.Fori(0, TURNS // 2 - 1) as ii:
                    send(ii, 1)
                    sent(ii, 0)
                    send(ii + 1, 0)
                    sent(ii, 1)
                send(TURNS // 2 - 1, 1)
                sent(TURNS // 2 - 1, 0)
                sent(TURNS // 2 - 1, 1)


def phase_attend(nc, sems, a, d):
    with ExitStack() as mem:
        def sb(name, shape, dt=F32):
            return mem.enter_context(nc.sbuf_tensor("a_" + name, shape, dt))

        def ps(name, shape, dt=F32):
            return mem.enter_context(nc.psum_tensor("a_" + name, shape, dt))

        def sem(name):
            return sems.new("a_" + name)

        G = B * N // GS
        QT = GS // P
        SCALE = float(HD) ** -0.5
        ident = sb("ident", [P, P])
        ones = sb("ones", [1, P])
        g1 = sb("g1", [KC, 2])
        b1 = sb("b1", [KC, 2])
        b1w = sb("b1w", [KC, 2, P])
        wqk = sb("wqk", [KC, 2, 4, P])
        wqkg = sb("wqkg", [KC, 2, 4, P])
        wv = sb("wv", [KC, 2, C])
        wvg = sb("wvg", [KC, 2, C])
        wp = sb("wp", [KC, 2, C])
        bqk0 = sb("bqk0", [P, 4])
        bqk = sb("bqk", [P, 4])
        brow = sb("brow", [1, 2 * C])
        bv = sb("bv", [P, C])
        bp = sb("bp", [P, C])

        xs = sb("xs", [P, 2, QT, C])
        xT = sb("xT", [KC, 2, GS])
        qk = sb("qk", [P, 2, 4, GS])
        V = sb("V", [P, 2, QT, C])
        mxs = sb("mxs", [P, 2, QT])
        nmx = sb("nmx", [P, 2, QT])
        e = sb("e", [P, 2, QT, GS])
        esum = sb("esum", [P, QT, HEADS])
        erec = sb("erec", [P, QT, HEADS])
        eT = sb("eT", [P, 2, QT, GS])
        o = sb("o", [P, QT, C])
        oT = sb("oT", [KC, 2, GS])
        y = sb("y", [P, QT, C])

        pX = ps("pX", [KC, 2, GS])
        pQK = ps("pQK", [P, 4, GS])
        pS = ps("pS", [P, 2, QT, GS])
        pT = ps("pT", [P, QT, GS])
        pO = ps("pO", [P, 512])
        pM = ps("pM", [P, 512])
        oV = pO[:, 0:QT * C].rearrange("p (t h d) -> p t h d", t=QT, h=HEADS)
        mV = pM[:, 0:QT * C].rearrange("p (t c) -> p t c", t=QT)
        mT = pM[0:KC, :].rearrange("p (k n) -> p k n", k=2)

        made, con, cleared = sem("made"), sem("con"), sem("cleared")
        pre_pe, pre_dv = sem("pre_pe"), sem("pre_dv")
        dv = sem("dv")
        xs_in = [sem(f"xs_in{h}") for h in range(2)]
        s_X = sem("s_X")
        s_xc = sem("s_xc")
        s_QK = sem("s_QK")
        s_qk = sem("s_qk")
        s_V = sem("s_V")
        s_v = sem("s_v")
        s_S = sem("s_S")
        s_m = sem("s_m")
        s_E = sem("s_E")
        s_T = sem("s_T")
        s_tc = sem("s_tc")
        s_O = sem("s_O")
        s_o = sem("s_o")
        s_OT = sem("s_OT")
        s_oc = sem("s_oc")
        s_Y = sem("s_Y")
        s_y = sem("s_y")
        o_y = sem("o_y")

        xs_v = d.xs.rearrange("(g t p) c -> g p t c", t=QT, p=P)
        y_v = d.aca.rearrange("(g t p) c -> g p t c", t=QT, p=P)
        CON = 16

        def head(g, h):
            return g * HEADS + (h + 1 + HEADS)

        with nc.Block() as block:
            @block.sync
            def _(sp):
                def con_in(dst, src):
                    sp.dma_start(dst, src).then_inc(con, 16)

                wqkv, wb = a["L0_conv_wqkv_w"], a["L0_conv_wqkv_b"]
                sp.wait_ge(cleared, 2)
                with nc.allow_non_contiguous_dma("small constants"):
                    for k in range(2):
                        for w in range(2):
                            con_in(wqk[:, k, 2 * w:2 * w + 2, :].rearrange("p m (u e) -> p (m u) e", u=2)[:, :, 0:HD],
                                   wqkv[k * KC:(k + 1) * KC, w * C:(w + 1) * C].rearrange("p (h e) -> p h e", h=HEADS))
                    for u in range(2):
                        con_in(bqk0[64 * u:64 * u + HD, :],
                               wb[0:2 * C].rearrange("(m u e) -> u e m", u=2, e=HD)[u])
                    con_in(wv[:, :, :], wqkv[:, 2 * C:3 * C].rearrange("(k p) n -> p k n", k=2))
                    con_in(wp[:, :, :], a["L0_conv_proj_w"].rearrange("(k p) n -> p k n", k=2))
                    con_in(g1[:, :], a["L0_conv_g1"].rearrange("(k p) -> p k", k=2))
                    con_in(b1[:, :], a["L0_conv_b1"].rearrange("(k p) -> p k", k=2))
                    con_in(brow[:, 0:C], wb[2 * C:3 * C].rearrange("(a n) -> a n", a=1))
                    con_in(brow[:, C:2 * C], a["L0_conv_proj_b"].rearrange("(a n) -> a n", a=1))
                sp.sem_inc(o_y, 16)
                with sp.Fori(0, G) as g:
                    sp.wait_ge(s_y, g + 2)
                    sp.dma_start(y_v[bass.ds(g, 1)].rearrange("a p t c -> (a p) t c"), y[:, :, :]).then_inc(o_y, 16)
                sp.wait_ge(o_y, 16 * G + 16)

            @block.gpsimd
            def _(gp):
                nc.gpsimd.memset(ident[:, :], 0.0).then_inc(made, 1)
                nc.gpsimd.memset(ones[:, :], 1.0).then_inc(made, 1)
                gp.wait_ge(made, 2)
                nc.gpsimd.affine_select(out=ident[:, :], in_=ident[:, :], compare_op=ALU.not_equal, fill=1.0,
                                        base=0, pattern=[[-1, P]], channel_multiplier=1).then_inc(made, 1)
                with gp.Fori(0, G // 2) as gg:
                    for half in range(2):
                        gp.wait_ge(s_X, gg * 2 + (half + 1))
                        gp.dma_start(xs[:, half, :, :], xs_v[bass.ds(gg * 2 + half, 1)]
                                     .rearrange("a p t c -> (a p) t c")).then_inc(xs_in[half], 16)

            @block.tensor
            def _(te):
                te.sem_inc(s_X, 2)
                te.sem_inc(s_T, HEADS)
                te.sem_inc(s_O, HEADS)
                te.wait_ge(made, 3)
                te.wait_ge(con, 16 * 12)
                te.wait_ge(pre_dv, 1)
                for m in range(4):
                    for k in range(2):
                        nc.tensor.matmul(pQK[:, 0, m:m + 1], wqk[:, k, m, :], b1[:, k:k + 1], start=(k == 0),
                                         stop=(k == 1)).then_inc(pre_pe, 1)
                for k in range(2):
                    nc.tensor.matmul(pO[:, 0:C], b1w[:, k, :], wv[:, k, :], start=(k == 0), stop=False)
                nc.tensor.matmul(pO[:, 0:C], ones[:, :], brow[:, 0:C], start=False, stop=True).then_inc(pre_pe, 1)
                nc.tensor.matmul(pM[:, 0:C], ones[:, :], brow[:, C:2 * C], start=True, stop=True).then_inc(pre_pe, 1)
                te.wait_ge(pre_dv, 2)

                def front(gg, half, f, first=False):
                    te.wait_ge(xs_in[half], gg * 16 + 16)
                    te.wait_ge(s_xc, f + 1)
                    for t in range(QT):
                        for k in range(2):
                            mm = nc.tensor.transpose(pX[:, k, t * P:(t + 1) * P], xs[:, half, t, k * KC:(k + 1) * KC],
                                                     ident[:, :])
                    mm.then_inc(s_X, 1)
                    te.wait_ge(s_xc, f + 2)
                    te.wait_ge(s_qk, f + 1)
                    for m in range(4):
                        for k in range(2):
                            mm = nc.tensor.matmul(pQK[:, m, :], wqkg[:, k, m, :], xT[:, k, :], start=(k == 0),
                                                  stop=(k == 1))
                    mm.then_inc(s_QK, 1)
                    if not first:
                        te.wait_ge(s_y, f)
                    for t in range(QT):
                        for k in range(2):
                            mm = nc.tensor.matmul(mV[:, t, :], xT[:, k, t * P:(t + 1) * P], wvg[:, k, :],
                                                  start=(k == 0), stop=(k == 1))
                    mm.then_inc(s_V, 1)

                def scores(g, half, h):
                    te.wait_ge(s_E, head(g, h - 2))
                    lo = 64 * (h % 2)
                    for t in range(QT):
                        mm = nc.tensor.matmul(pS[:, h % 2, t, :], qk[lo:lo + HD, half, h // 2, t * P:(t + 1) * P],
                                              qk[lo:lo + HD, half, 2 + h // 2, :], start=True, stop=True)
                    mm.then_inc(s_S, 1)

                def turned(g, half, h):
                    te.wait_ge(s_E, head(g, h))
                    te.wait_ge(s_tc, head(g, h - 1))
                    for t in range(QT):
                        for k in range(QT):
                            mm = nc.tensor.transpose(pT[:, k, t * P:(t + 1) * P], e[:, h % 2, t, k * P:(k + 1) * P],
                                                     ident[:, :])
                    mm.then_inc(s_T, 1)

                def outputs(g, half, h):
                    te.wait_ge(s_tc, head(g, h))
                    if h == 0:
                        te.wait_ge(s_o, g + 1)
                        te.wait_ge(s_v, g + 2)
                    for t in range(QT):
                        for k in range(QT):
                            mm = nc.tensor.matmul(oV[:, t, h, :], eT[:, h % 2, k, t * P:(t + 1) * P],
                                                  V[:, half, k, h * HD:(h + 1) * HD], start=(k == 0), stop=(k == 1))
                    mm.then_inc(s_O, 1)

                def turn(gg, half, more):
                    g = gg * 2 + half
                    te.wait_ge(s_qk, g + 2)
                    scores(g, half, 0)
                    scores(g, half, 1)
                    if more:
                        front(gg + half, 1 - half, g + 1)
                    turned(g, half, 0)
                    scores(g, half, 2)
                    turned(g, half, 1)
                    outputs(g, half, 0)
                    scores(g, half, 3)
                    turned(g, half, 2)
                    outputs(g, half, 1)
                    turned(g, half, 3)
                    outputs(g, half, 2)
                    outputs(g, half, 3)
                    te.wait_ge(s_o, g + 2)
                    if more:
                        te.wait_ge(s_v, g + 3)
                    for t in range(QT):
                        for k in range(2):
                            mm = nc.tensor.transpose(mT[:, k, t * P:(t + 1) * P], o[:, t, k * KC:(k + 1) * KC],
                                                     ident[:, :])
                    mm.then_inc(s_OT, 1)
                    te.wait_ge(s_oc, g + 1)
                    for t in range(QT):
                        for k in range(2):
                            mm = nc.tensor.matmul(mV[:, t, :], oT[:, k, t * P:(t + 1) * P], wp[:, k, :],
                                                  start=(k == 0), stop=(k == 1))
                    mm.then_inc(s_Y, 1)

                front(0, 0, 0, first=True)
                with te.Fori(0, G // 2 - 1) as gg:
                    turn(gg, 0, True)
                    turn(gg, 1, True)
                turn(G // 2 - 1, 0, True)
                turn(G // 2 - 1, 1, False)

            @block.scalar
            def _(act):
                act.sem_inc(s_xc, 1)
                act.sem_inc(s_E, HEADS)
                act.sem_inc(s_tc, HEADS)

                def front(f):
                    act.wait_ge(s_X, f + 3)
                    act.wait_ge(s_V, f + 1)
                    nc.scalar.activation(xT[:, :, :], pX[:, :, :], ACT.Copy).then_inc(s_xc, 1)

                def expo(g, h):
                    act.wait_ge(s_m, g * HEADS + (h + 1))
                    act.wait_ge(s_T, head(g, h - 2))
                    for t in range(QT):
                        ins = nc.scalar.activation(e[:, h % 2, t, :], pS[:, h % 2, t, :], ACT.Exp,
                                                   bias=nmx[:, h % 2, t:t + 1], scale=SCALE,
                                                   accum_out=esum[:, t, h:h + 1])
                    ins.then_inc(s_E, 1)

                def copied(g, h):
                    act.wait_ge(s_T, head(g, h))
                    act.wait_ge(s_O, head(g, h - 2))
                    nc.scalar.activation(eT[:, h % 2, :, :], pT[:, :, :], ACT.Copy).then_inc(s_tc, 1)

                def turn(g, more):
                    expo(g, 0)
                    expo(g, 1)
                    if more:
                        front(g + 1)
                    copied(g, 0)
                    expo(g, 2)
                    copied(g, 1)
                    expo(g, 3)
                    copied(g, 2)
                    copied(g, 3)
                    act.wait_ge(s_OT, g + 1)
                    nc.scalar.activation(oT[:, :, :], mT, ACT.Copy).then_inc(s_oc, 1)

                front(0)
                with act.Fori(0, G - 1) as g:
                    turn(g, True)
                turn(G - 1, False)

            @block.vector
            def _(ve):
                link = Link(ve, dv)
                ve.sem_inc(s_V, 1)
                nc.vector.memset(wqk[:, :, :, :], 0.0).then_inc(cleared, 1)
                nc.vector.memset(bqk0[:, :], 0.0).then_inc(cleared, 1)
                ve.wait_ge(con, 16 * 12)
                nc.vector.tensor_copy(b1w[:, :, :], b1[:, :].unsqueeze(2).to_broadcast([KC, 2, P])).then_inc(pre_dv, 1)
                for k in range(2):
                    nc.vector.tensor_scalar(wqkg[:, k, :, :], wqk[:, k, :, :], g1[:, k:k + 1], None, ALU.mult)
                    nc.vector.tensor_scalar(wvg[:, k, :], wv[:, k, :], g1[:, k:k + 1], None, ALU.mult)
                ve.wait_ge(pre_pe, 10)
                nc.vector.tensor_tensor(bqk[:, :], pQK[:, 0, 0:4], bqk0[:, :], ALU.add)
                nc.vector.tensor_copy(bv[:, :], pO[:, 0:C])
                link(nc.vector.tensor_copy(bp[:, :], pM[:, 0:C]))
                ve.sem_inc(pre_dv, 1)
                ve.sem_inc(s_qk, 1)
                ve.sem_inc(s_v, 1)
                ve.sem_inc(s_o, 1)
                ve.sem_inc(s_y, 1)

                def front(f, half):
                    ve.wait_ge(s_QK, f + 1)
                    nc.vector.tensor_tensor(qk[:, half, :, :], pQK[:, :, :],
                                            bqk[:, :].unsqueeze(2).to_broadcast([P, 4, GS]), ALU.add).then_inc(s_qk, 1)
                    ve.wait_ge(s_V, f + 2)
                    nc.vector.tensor_tensor(V[:, half, :, :], mV, bv[:, :].unsqueeze(1).to_broadcast([P, QT, C]),
                                            ALU.add).then_inc(s_v, 1)

                def maxima(g, h):
                    ve.wait_ge(s_S, g * HEADS + (h + 1))
                    link(nc.vector.tensor_reduce(mxs[:, h % 2, :], pS[:, h % 2, :, :], AX.X, ALU.max))
                    nc.vector.tensor_scalar(nmx[:, h % 2, :], mxs[:, h % 2, :], -SCALE, None, ALU.mult).then_inc(s_m, 1)

                def turn(gg, half, more):
                    g = gg * 2 + half
                    link.base, link.n = g * 5 + 1, 0
                    maxima(g, 0)
                    maxima(g, 1)
                    if more:
                        front(g + 1, 1 - half)
                    maxima(g, 2)
                    maxima(g, 3)
                    ve.wait_ge(s_E, head(g, 3))
                    link(nc.vector.reciprocal(erec[:, :, :], esum[:, :, :]))
                    ve.wait_ge(s_O, head(g, 3))
                    nc.vector.tensor_tensor(o[:, :, :].rearrange("p t (h e) -> p t h e", h=HEADS), oV,
                                            erec[:, :, :].unsqueeze(3).to_broadcast([P, QT, HEADS, HD]),
                                            ALU.mult).then_inc(s_o, 1)
                    ve.wait_ge(s_Y, g + 1)
                    ve.wait_ge(o_y, g * 16 + 16)
                    nc.vector.tensor_tensor(y[:, :, :], mV, bp[:, :].unsqueeze(1).to_broadcast([P, QT, C]),
                                            ALU.add).then_inc(s_y, 1)

                front(0, 0)
                with ve.Fori(0, G // 2 - 1) as gg:
                    turn(gg, 0, True)
                    turn(gg, 1, True)
                turn(G // 2 - 1, 0, True)
                turn(G // 2 - 1, 1, False)


ROWS = 16
STRIPS = B * H // ROWS
HROWS = ROWS + 2 * PADY
WP = W + 2 * PADY
CH = HID // P
SN = ROWS * W
FN = 4 * W
GR = HROWS // 4
CB = 64
PE_TAPS = [(0, 0), (0, 1), (0, 2), (0, 3), (0, 4), (1, 0), (1, 1)]
VE_TAPS = [(y, x) for y in range(KS) for x in range(KS) if (y, x) not in PE_TAPS]


def phase_features(nc, sems, a, d):
    with ExitStack() as mem:
        def sb(name, shape, dt=F32):
            return mem.enter_context(nc.sbuf_tensor("d_" + name, shape, dt))

        def sem(name):
            return sems.new("d_" + name)

        h = sb("h", [P, B, HROWS, WP])
        acc = sb("acc", [P, SN])
        g = sb("g", [P, B, SN])
        w = sb("w", [P, KS * KS])
        bias = sb("bias", [P, 1])
        ld, cleared, dv, s_acc, s_g, s_sum, st = (sem(n) for n in ("ld", "cleared", "dv", "acc", "g", "sum", "st"))
        BANDS = H // ROWS
        taps = [(y, x) for y in range(KS) for x in range(KS)]
        with nc.Block() as block:
            @block.sync
            def _(sp):
                sp.wait_ge(cleared, 1)
                with nc.allow_non_contiguous_dma("small constants"):
                    for j in range(BANDS):
                        sp.dma_start(w[j * TDF:(j + 1) * TDF, :],
                                     a["L0_conv_dw_w"][HID:HID + TDF].rearrange("c o y x -> c (o y x)")).then_inc(ld, 16)
                        sp.dma_start(bias[j * TDF:(j + 1) * TDF, :],
                                     a["L0_conv_dw_b"][HID:HID + TDF].rearrange("(c o) -> c o", o=1)).then_inc(ld, 16)
                        for b in range(B):
                            lo = j * ROWS * W
                            sp.dma_start(h[j * TDF:(j + 1) * TDF, b, :, PADY:PADY + W],
                                         d.td[b, :, lo:lo + HROWS * W].rearrange("c (y x) -> c y x", x=W)).then_inc(ld, 16)
                sp.wait_ge(s_sum, 2)
                for j in range(BANDS):
                    for b in range(B):
                        sp.dma_start(d.tdc[b, :, j * SN:(j + 1) * SN], g[j * TDF:(j + 1) * TDF, b, :]).then_inc(st, 16)
                sp.wait_ge(st, 16 * B * BANDS)

            @block.scalar
            def _(act):
                for b in range(B):
                    act.wait_ge(s_acc, b + 1)
                    nc.scalar.activation(g[:, b, :], acc[:, :], ACT.Gelu, bias=bias[:, 0:1]).then_inc(s_g, 1)

            @block.vector
            def _(ve):
                link = Link(ve, dv)
                nc.vector.memset(h[:, :, :, :], 0.0).then_inc(cleared, 1)
                ve.wait_ge(ld, 16 * BANDS * (2 + B))
                for b in range(B):
                    for n, (y, x) in enumerate(taps):
                        view = h[:, b, y:y + ROWS, x:x + W]
                        out = acc[:, :].rearrange("p (y x) -> p y x", x=W)
                        if n == 0:
                            link(nc.vector.tensor_scalar(out, view, w[:, 0:1], None, ALU.mult))
                        elif n < len(taps) - 1:
                            link(nc.vector.scalar_tensor_tensor(out, view, w[:, n:n + 1], out, ALU.mult, ALU.add))
                        else:
                            nc.vector.scalar_tensor_tensor(out, view, w[:, n:n + 1], out, ALU.mult,
                                                           ALU.add).then_inc(s_acc, 1)
                    ve.wait_ge(s_g, b + 1)
                    nc.vector.tensor_tensor(g[:, b, :].rearrange("p (y x) -> p y x", x=W),
                                            g[:, b, :].rearrange("p (y x) -> p y x", x=W),
                                            h[:, b, PADY:PADY + ROWS, PADY:PADY + W], ALU.add).then_inc(s_sum, 1)


def phase_ffn(nc, sems, a, d):
    with ExitStack() as mem:
        def sb(name, shape, dt=F32):
            return mem.enter_context(nc.sbuf_tensor("f_" + name, shape, dt))

        def ps(name, shape, dt=F32):
            return mem.enter_context(nc.psum_tensor("f_" + name, shape, dt))

        def sem(name):
            return sems.new("f_" + name)

        NT = len(PE_TAPS)
        ident = sb("ident", [P, P])
        ones = sb("ones", [1, P])
        g2 = sb("g2", [KC, 2])
        b2 = sb("b2", [KC, 2])
        w1 = sb("w1", [KC + 1, 2, HID])
        dww = sb("dww", [P, CH, KS * KS])
        dwb = sb("dwb", [P, CH])
        diag = sb("diag", [P, CH, NT, P])
        w2 = sb("w2", [P, CH, C])
        w2t = sb("w2t", [TDF + 1, C])
        g3 = sb("g3", [P, C])
        b3 = sb("b3", [P, C])
        wc = sb("wc", [KC, 2, CB])
        wcr = sb("wcr", [CB, C])
        bc = sb("bc", [CB, 1])
        pos = sb("pos", [P, B * N // P], I32)
        idx = sb("idx", [P, ROWS], I32)

        xt = sb("xt", [KC + 1, 2, HROWS * W])
        h = sb("h", [P, 3, HROWS, WP])
        acc = sb("acc", [P, 2, SN])
        hs = sb("hs", [P, CH, SN])
        tds = sb("tds", [TDF + 1, SN])
        F = sb("F", [P, ROWS, C])
        brow = F[0:1, 0:HID // C, :].rearrange("a r c -> a (r c)")
        st6 = sb("st6", [P, ROWS, 6])
        mv = sb("mv", [P, ROWS, 2])
        dev = sb("dev", [P, ROWS])
        nmu = sb("nmu", [P, ROWS])
        aca = sb("aca", [P, ROWS, C])
        x1 = sb("x1", [KC, 2, SN])
        xc = sb("xc", [CB, 2, FN])

        p1 = ps("p1", [P, 2, FN])
        pC = ps("pC", [P, SN])
        p2 = ps("p2", [P, 2, 512])

        made, con, pre_dv, pre_pe, cleared = (sem(n) for n in ("made", "con", "pre_dv", "pre_pe", "cleared"))
        dv = sem("dv")
        marks = sem("marks")
        xt_in = sem("xt_in")
        tds_in = sem("tds_in")
        res_in = sem("res_in")
        aca_in = sem("aca_in")
        s_fc1 = sem("s_fc1")
        s_g = sem("s_g")
        s_tap = sem("s_tap")
        s_pc = sem("s_pc")
        s_acc = sem("s_acc")
        s_g2 = sem("s_g2")
        s_add = sem("s_add")
        s_F = sem("s_F")
        s_ev = sem("s_ev")
        s_st = sem("s_st")
        s_dev = sem("s_dev")
        s_rs = sem("s_rs")
        s_n = sem("s_n")
        s_ln = sem("s_ln")
        s_tr = sem("s_tr")
        s_x1 = sem("s_x1")
        s_xc = sem("s_xc")
        s_xcv = sem("s_xcv")
        o_xc = [sem(f"o_xc{k}") for k in range(2)]
        o_x1 = sem("o_x1")
        idx_set = sem("idx_set")
        s_lg = sem("s_lg")

        CON = 16
        xt_v = d.xt.rearrange("b c n -> (b c) n")
        PER_IMAGE = H // ROWS

        def split(s):
            return (s // PER_IMAGE, s % PER_IMAGE)

        with nc.Block() as block:
            @block.sync
            def _(sp):
                def cin(dst, src):
                    sp.dma_start(dst, src).then_inc(con, 16)

                sp.wait_ge(cleared, 1)
                with nc.allow_non_contiguous_dma("small constants"):
                    cin(hs[0:KC, 0:2, 0:HID], a["L0_conv_fc1_w"].rearrange("(k p) n -> p k n", k=2))
                    cin(g2[:, :], a["L0_conv_g2"].rearrange("(k p) -> p k", k=2))
                    cin(b2[:, :], a["L0_conv_b2"].rearrange("(k p) -> p k", k=2))
                    cin(brow, a["L0_conv_fc1_b"].rearrange("(a n) -> a n", a=1))
                    cin(dww[:, :, :], a["L0_conv_dw_w"][0:HID].rearrange("(c p) o y x -> p c (o y x)", p=P))
                    cin(dwb[:, :], a["L0_conv_dw_b"][0:HID].rearrange("(c p) -> p c", p=P))
                    cin(w2[:, :, :], a["L0_conv_fc2_w"][0:HID].rearrange("(c p) n -> p c n", p=P))
                    cin(w2t[0:TDF, :], a["L0_conv_fc2_w"][HID:HID + TDF])
                    cin(w2t[TDF:TDF + 1, :], a["L0_conv_fc2_b"].rearrange("(a n) -> a n", a=1))
                    cin(g3[:, :], a["L0_conv_g3"].rearrange("(a n) -> a n", a=1).broadcast_to([P, C]))
                    cin(b3[:, :], a["L0_conv_b3"].rearrange("(a n) -> a n", a=1).broadcast_to([P, C]))
                    cin(wcr[:, :], a["L1_conv_w1"])
                    cin(bc[:, :], a["L1_conv_b1"].rearrange("(c o) -> c o", o=1))
                    cin(pos[:, :], d.pos)

                def load_xt(b, j, s):
                    sp.dma_start(xt[0:KC, 0, :], d.xt[bass.ds(b, 1), 0:KC, bass.ds(j * SN, HROWS * W)]
                                 .rearrange("b c n -> (b c) n")).then_inc(xt_in, 16)
                    sp.dma_start(xt[:, 1, :], d.xt[bass.ds(b, 1), KC:C + 1, bass.ds(j * SN, HROWS * W)]
                                 .rearrange("b c n -> (b c) n")).then_inc(xt_in, 16)

                def tail_loads(b, j, t):
                    sp.wait_ge(s_F, t * 8 + 1)
                    sp.dma_start(tds[0:TDF, :], d.tdc[bass.ds(b, 1), :, bass.ds(j * SN, SN)]
                                 .rearrange("b c n -> (b c) n")).then_inc(tds_in, 16)
                    sp.wait_ge(o_x1, t * 16 + 16)
                    sp.wait_ge(s_xc, t * 4 + 4)
                    sp.dma_start(x1[:, :, :], d.res[bass.ds(b, 1), :, bass.ds(j * SN, SN)]
                                 .rearrange("b (k p) n -> (b p) k n", k=2)).then_inc(res_in, 16)

                def tail_stores(b, j, t):
                    sp.wait_ge(s_x1, t * 8 + 16)
                    sp.dma_start(d.x1[bass.ds(b, 1), :, bass.ds(j * SN, SN)].rearrange("b (k p) n -> (b p) k n", k=2),
                                 x1[:, :, :]).then_inc(o_x1, 16)
                    for q in range(4):
                        sp.wait_ge(s_xcv, t * 4 + (5 + q))
                        sp.dma_start(d.xc[bass.ds(b, 1), :, bass.ds(j * SN + q * FN, FN)]
                                     .rearrange("b c n -> (b c) n"), xc[:, q % 2, :]).then_inc(o_xc[q % 2], 16)

                sp.sem_inc(o_x1, 16)
                for k in range(2):
                    sp.sem_inc(o_xc[k], 16)
                load_xt(0, 0, 0)
                sp.wait_ge(s_fc1, CH * GR)
                load_xt(0, 1, 1)
                with sp.Fori(0, STRIPS - 2) as t:
                    bt, jt = t // PER_IMAGE, t % PER_IMAGE
                    tail_loads(bt, jt, t)
                    sp.wait_ge(s_fc1, t * (CH * GR) + 2 * CH * GR)
                    load_xt((t + 2) // PER_IMAGE, (t + 2) % PER_IMAGE, None)
                    tail_stores(bt, jt, t)
                for t in (STRIPS - 2, STRIPS - 1):
                    tail_loads(*split(t), t)
                    tail_stores(*split(t), t)
                sp.wait_ge(o_x1, 16 * STRIPS + 16)
                for k in range(2):
                    sp.wait_ge(o_xc[k], 16 * 2 * STRIPS + 16)

            @block.gpsimd
            def _(gp):
                nc.gpsimd.memset(ident[:, :], 0.0).then_inc(made, 1)
                nc.gpsimd.memset(ones[:, :], 1.0).then_inc(made, 1)
                gp.wait_ge(made, 2)
                nc.gpsimd.affine_select(out=ident[:, :], in_=ident[:, :], compare_op=ALU.not_equal, fill=1.0,
                                        base=0, pattern=[[-1, P]], channel_multiplier=1).then_inc(made, 1)
                nc.gpsimd.memset(tds[:, :], 1.0).then_inc(cleared, 1)
                gp.sem_inc(s_add, 2)
                gp.wait_ge(con, 16 * 14)

                def add(s, c):
                    n = s * CH + c
                    gp.wait_ge(s_g2, n + 1)
                    if not isinstance(s, int) or s >= 1:
                        gp.wait_ge(s_F, s * 8 + 8)
                    view = acc[:, c % 2, :].rearrange("p (y x) -> p y x", x=W)
                    nc.gpsimd.tensor_tensor(hs[:, c, :].rearrange("p (y x) -> p y x", x=W), view,
                                            h[:, c % 3, PADY:PADY + ROWS, PADY:PADY + W], ALU.add).then_inc(s_add, 1)

                def gathers(t, lo, hi):
                    if lo == 0:
                        nc.gpsimd.tensor_copy(idx[:, :], at(pos, t * ROWS, ROWS)).then_inc(idx_set, 1)
                        gp.wait_ge(idx_set, t + 1)
                        gp.sem_inc(marks, 1)
                    for r in range(lo, hi):
                        gp.indirect_dma_start(aca[:, r, :], None, d.aca[:, :],
                                              bass.IndirectOffsetOnAxis(ap=idx[:, r:r + 1], axis=0)).then_inc(aca_in, 16)

                def finish(t):
                    gp.wait_ge(s_n, t + 1)
                    nc.gpsimd.tensor_tensor(F[:, :, :], F[:, :, :], g3[:, :].unsqueeze(1).to_broadcast([P, ROWS, C]),
                                            ALU.mult).then_inc(s_lg, 1)
                    gp.wait_ge(s_lg, t * 2 + 1)
                    nc.gpsimd.tensor_tensor(F[:, :, :], F[:, :, :], b3[:, :].unsqueeze(1).to_broadcast([P, ROWS, C]),
                                            ALU.add).then_inc(s_lg, 1)
                    gp.wait_ge(s_lg, t * 2 + 2)
                    gp.wait_ge(aca_in, t * (16 * ROWS) + 16 * ROWS)
                    nc.gpsimd.tensor_tensor(F[:, :, :], F[:, :, :], aca[:, :, :], ALU.add).then_inc(s_ln, 1)

                def turn(s, tail):
                    t = s - 1
                    add(s, 0)
                    if tail:
                        if not isinstance(s, int) or s > 1:
                            gp.wait_ge(s_ln, t)
                        gathers(t, 0, 5)
                    add(s, 1)
                    if tail:
                        gathers(t, 5, 10)
                    add(s, 2)
                    if tail:
                        gathers(t, 10, 16)
                    add(s, 3)
                    if tail:
                        finish(t)
                    add(s, 4)
                    add(s, 5)

                turn(0, False)
                turn(1, True)
                with gp.Fori(2, STRIPS) as s:
                    turn(s, True)
                gp.wait_ge(s_ln, STRIPS - 1)
                gathers(STRIPS - 1, 0, ROWS)
                finish(STRIPS - 1)

            @block.tensor
            def _(te):
                te.sem_inc(s_F, 8)
                te.sem_inc(s_xc, 4)
                te.wait_ge(made, 3)
                te.wait_ge(con, 16 * 14)
                for k in range(2):
                    nc.tensor.transpose(pC[0:KC, k * CB:(k + 1) * CB], wcr[:, k * KC:(k + 1) * KC],
                                        ident[0:CB, 0:CB]).then_inc(pre_pe, 1)
                for o in range(2):
                    for k in range(2):
                        nc.tensor.matmul(pC[0:1, 512 * (1 + o):512 * (1 + o) + HID // 2], b2[:, k:k + 1],
                                         hs[0:KC, k, o * (HID // 2):(o + 1) * (HID // 2)], start=(k == 0),
                                         stop=(k == 1)).then_inc(pre_pe, 1)
                te.wait_ge(pre_dv, 1)

                def fc1(s, c):
                    if c == 0:
                        te.wait_ge(xt_in, s * 32 + 32)
                    for j in range(GR):
                        m = c * GR + j
                        te.wait_ge(s_g, s * (CH * GR) + (m + 1))
                        for k in range(2):
                            kk = KC + k
                            mm = nc.tensor.matmul(p1[:, m % 2, :], w1[0:kk, k, c * P:(c + 1) * P],
                                                  xt[0:kk, k, j * FN:(j + 1) * FN], start=(k == 0), stop=(k == 1))
                        mm.then_inc(s_fc1, 1)

                def taps(s, c):
                    n = s * CH + c
                    te.wait_ge(s_g, s * (CH * GR) + ((c + 1) * GR + 2))
                    te.wait_ge(s_pc, n + 1)
                    for i, (y, x) in enumerate(PE_TAPS):
                        for q in range(4):
                            mm = nc.tensor.matmul(pC[:, q * FN:(q + 1) * FN], diag[:, c, i, :],
                                                  h[:, c % 3, 4 * q + y:4 * q + y + 4, x:x + W], start=(i == 0),
                                                  stop=(i == NT - 1))
                    mm.then_inc(s_tap, 1)

                def fc2(t):
                    te.wait_ge(s_add, t * CH + CH + 2)
                    te.wait_ge(tds_in, t * 16 + 16)
                    for k in range(8):
                        te.wait_ge(s_ev, t * 8 + (k + 7) if k >= 2 else t * 8 + 8)
                        if k < 2:
                            te.wait_ge(s_xcv, t * 4 + 4)
                        for r in range(2):
                            row = 2 * k + r
                            dst = p2[:, k % 2, r * C:(r + 1) * C]
                            for c in range(CH):
                                nc.tensor.matmul(dst, hs[:, c, row * W:(row + 1) * W], w2[:, c, :], start=(c == 0), stop=False)
                            mm = nc.tensor.matmul(dst, tds[:, row * W:(row + 1) * W], w2t[:, :], start=False, stop=True)
                        mm.then_inc(s_F, 1)

                def back(t):
                    te.wait_ge(s_ln, t + 1)
                    te.wait_ge(s_ev, t * 8 + 16)
                    for k in range(8):
                        te.wait_ge(s_x1, t * 8 + (k + 7) if k >= 2 else t * 8 + 8)
                        q, kt = k // 2, k % 2
                        for r in range(4):
                            mm = nc.tensor.transpose(p2[0:KC, k % 2, r * W:(r + 1) * W],
                                                     F[:, 4 * q + r, kt * KC:(kt + 1) * KC], ident[:, :])
                        mm.then_inc(s_tr, 1)
                    for q in range(4):
                        te.wait_ge(s_x1, t * 8 + 16)
                        te.wait_ge(s_xcv, t * 4 + (q + 3) if q >= 2 else t * 4 + 4)
                        for k in range(2):
                            mm = nc.tensor.matmul(p2[0:CB, q % 2, :], wc[:, k, :], x1[:, k, q * FN:(q + 1) * FN],
                                                  start=(k == 0), stop=(k == 1))
                        mm.then_inc(s_xc, 1)

                def turn(s, tail, more):
                    taps(s, 0)
                    fc1(s, 2)
                    taps(s, 1)
                    if tail:
                        fc2(s - 1)
                    fc1(s, 3)
                    taps(s, 2)
                    fc1(s, 4)
                    taps(s, 3)
                    fc1(s, 5)
                    taps(s, 4)
                    if tail:
                        back(s - 1)
                    if more:
                        fc1(s + 1, 0)
                    taps(s, 5)
                    if more:
                        fc1(s + 1, 1)

                fc1(0, 0)
                fc1(0, 1)
                turn(0, False, True)
                with te.Fori(1, STRIPS - 1) as s:
                    turn(s, True, True)
                turn(STRIPS - 1, True, False)
                fc2(STRIPS - 1)
                back(STRIPS - 1)

            @block.scalar
            def _(act):
                act.sem_inc(s_g, 2)
                act.sem_inc(s_ev, 8)
                act.sem_inc(s_xcv, 4)

                def gelu1(s, c):
                    act.wait_ge(s_add, s * CH + c)
                    for j in range(GR):
                        m = c * GR + j
                        act.wait_ge(s_fc1, s * (CH * GR) + (m + 1))
                        nc.scalar.activation(h[:, c % 3, 4 * j:4 * j + 4, PADY:PADY + W],
                                             p1[:, m % 2, :].rearrange("p (y x) -> p y x", x=W),
                                             ACT.Gelu).then_inc(s_g, 1)

                def gelu2(s, c):
                    act.wait_ge(s_acc, s * CH + (c + 1))
                    nc.scalar.activation(acc[:, c % 2, :], acc[:, c % 2, :], ACT.Gelu,
                                         bias=dwb[:, c:c + 1]).then_inc(s_g2, 1)

                def evac(t):
                    for k in range(8):
                        act.wait_ge(s_F, t * 8 + (k + 9))
                        nc.scalar.activation(F[:, 2 * k:2 * k + 2, :], p2[:, k % 2, 0:2 * C]
                                             .rearrange("p (r c) -> p r c", r=2), ACT.Copy).then_inc(s_ev, 1)

                def deviate(t):
                    act.wait_ge(s_st, t + 1)
                    nc.scalar.activation(dev[:, :], dev[:, :], ACT.Sqrt).then_inc(s_dev, 1)
                    act.wait_ge(s_rs, t + 1)
                    for r in range(ROWS):
                        ins = nc.scalar.activation(F[:, r, :], F[:, r, :], ACT.Identity, bias=nmu[:, r:r + 1],
                                                   scale=dev[:, r:r + 1])
                    ins.then_inc(s_n, 1)

                def first(t, lo, hi):
                    for q in range(lo, hi):
                        act.wait_ge(s_xc, t * 4 + (q + 5))
                        act.wait_ge(o_xc[q % 2], t * 32 + (16 + 16 * (q // 2)))
                        nc.scalar.activation(xc[:, q % 2, :], p2[0:CB, q % 2, :], ACT.Identity,
                                             bias=bc[:, 0:1]).then_inc(s_xcv, 1)

                def turn(s, tail, more):
                    if tail:
                        gelu2(s - 1, 5)
                    gelu1(s, 2)
                    gelu2(s, 0)
                    if tail:
                        evac(s - 1)
                    gelu1(s, 3)
                    gelu2(s, 1)
                    gelu1(s, 4)
                    gelu2(s, 2)
                    if tail:
                        deviate(s - 1)
                    gelu1(s, 5)
                    gelu2(s, 3)
                    if tail:
                        first(s - 1, 0, 4)
                    if more:
                        gelu1(s + 1, 0)
                    gelu2(s, 4)
                    if more:
                        gelu1(s + 1, 1)

                gelu1(0, 0)
                gelu1(0, 1)
                turn(0, False, True)
                with act.Fori(1, STRIPS - 1) as s:
                    turn(s, True, True)
                turn(STRIPS - 1, True, False)
                gelu2(STRIPS - 1, 5)
                evac(STRIPS - 1)
                deviate(STRIPS - 1)
                first(STRIPS - 1, 0, 4)

            @block.vector
            def _(ve):
                link = Link(ve, dv)
                for i in range(3):
                    nc.vector.memset(h[:, i, :, :], 0.0)
                ve.sem_inc(s_pc, 1)
                ve.sem_inc(s_x1, 8)
                ve.wait_ge(made, 3)
                ve.wait_ge(con, 16 * 14)
                for k in range(2):
                    nc.vector.tensor_scalar(w1[0:KC, k, :], hs[0:KC, k, 0:HID], g2[:, k:k + 1], None, ALU.mult)
                for c in range(CH):
                    for i, (y, x) in enumerate(PE_TAPS):
                        n = KS * y + x
                        nc.vector.tensor_scalar(diag[:, c, i, :], ident[:, :], dww[:, c, n:n + 1], None, ALU.mult)
                ve.wait_ge(pre_pe, 6)
                nc.vector.tensor_copy(wc[:, :, :], pC[0:KC, 0:2 * CB].rearrange("p (k n) -> p k n", k=2))
                for o in range(2):
                    link(nc.vector.tensor_tensor(w1[KC:KC + 1, 1, o * (HID // 2):(o + 1) * (HID // 2)],
                                                 pC[0:1, 512 * (1 + o):512 * (1 + o) + HID // 2],
                                                 brow[:, o * (HID // 2):(o + 1) * (HID // 2)], ALU.add))
                ve.sem_inc(pre_dv, 1)
                start = link.n
                LINKS = len(VE_TAPS) - 1
                per = CH * LINKS + 4

                def chunk(s, c, extra=()):
                    n = s * CH + c
                    extra = list(extra)
                    ve.wait_ge(s_tap, n + 1)
                    ve.wait_ge(s_add, n + 1)
                    out = acc[:, c % 2, :].rearrange("p (y x) -> p y x", x=W)
                    for i, (y, x) in enumerate(VE_TAPS):
                        view = h[:, c % 3, y:y + ROWS, x:x + W]
                        w = dww[:, c, KS * y + x:KS * y + x + 1]
                        prior = out if i else pC[:, :].rearrange("p (y x) -> p y x", x=W)
                        ins = nc.vector.scalar_tensor_tensor(out, view, w, prior, ALU.mult, ALU.add)
                        if i < len(VE_TAPS) - 1:
                            link(ins)
                        else:
                            ins.then_inc(s_acc, 1)
                        if i == 0:
                            ve.sem_inc(s_pc, 1)
                        if extra and i >= 2 and i % 2 == 0:
                            extra.pop(0)()
                    for e in extra:
                        e()

                def stats(t):
                    ve.wait_ge(s_ev, t * 8 + 16)
                    ve.sem_inc(marks, 1)
                    for r in range(ROWS):
                        ins = nc.vector.bn_stats(st6[:, r, :], F[:, r, :])
                    link(ins)
                    ve.sem_inc(marks, 1)
                    for r in range(ROWS):
                        ins = nc.vector.bn_aggr(mv[:, r, :], st6[:, r, :])
                    link(ins)
                    nc.vector.tensor_scalar(dev[:, :], mv[:, :, 1], EPS, None, ALU.add).then_inc(s_st, 1)
                    ve.wait_ge(s_dev, t + 1)
                    link(nc.vector.reciprocal(dev[:, :], dev[:, :]))
                    link(nc.vector.tensor_scalar(nmu[:, :], mv[:, :, 0], -1.0, None, ALU.mult))
                    nc.vector.tensor_tensor(nmu[:, :], nmu[:, :], dev[:, :], ALU.mult).then_inc(s_rs, 1)

                def x1_adds(t):
                    def one(k):
                        def go():
                            if k == 0:
                                ve.wait_ge(res_in, t * 16 + 16)
                            ve.wait_ge(s_tr, t * 8 + (k + 1))
                            q, kt = k // 2, k % 2
                            part = x1[:, kt, q * FN:(q + 1) * FN]
                            nc.vector.tensor_tensor(part, p2[0:KC, k % 2, :], part, ALU.add).then_inc(s_x1, 1)
                        return go
                    return [one(k) for k in range(8)]

                def turn(s, tail):
                    link.base, link.n = (s - 1) * per + (start + CH * LINKS) if tail else start, 0
                    for c in range(CH):
                        if tail and c == 3:
                            stats(s - 1)
                        chunk(s, c, x1_adds(s - 1) if tail and c == 4 else ())

                turn(0, False)
                with ve.Fori(1, STRIPS) as s:
                    turn(s, True)
                link.base, link.n = (STRIPS - 1) * per + (start + CH * LINKS), 0
                stats(STRIPS - 1)
                for go in x1_adds(STRIPS - 1):
                    go()


WINDOWS = (4, 8, 12)
WB = len(WINDOWS)
PITCH = W + 2


def window(nw):
    step = H // nw
    return step, step + H % nw


def window_parts(t, nw):
    step, k = window(nw)
    parts = []
    for y0 in range(0, k, step):
        for x0 in range(0, k, step):
            v = t[:, y0:y0 + nw * step, x0:x0 + nw * step].rearrange("p (u y) (v x) -> p y x u v", u=nw, v=nw)
            parts.append((y0, min(step, k - y0), x0, min(step, k - x0), v))
    return parts


def phase_cut(nc, sems, a, d):
    with ExitStack() as mem:
        def sb(name, shape, dt=F32):
            return mem.enter_context(nc.sbuf_tensor("c_" + name, shape, dt))

        def sem(name):
            return sems.new("c_" + name)

        img = sb("img", [P, H + 2, PITCH])
        tile = sb("tile", [P, 2, max(window(n)[1] * n * n for n in WINDOWS)])
        img_in = sem("img_in")
        s_cut = [sem(f"s_cut{k}") for k in range(2)]
        stored = [sem(f"stored{k}") for k in range(2)]
        ROWS_OF = [(j, nw, part) for j, nw in enumerate(WINDOWS) for part in range(0, window(nw)[1], window(nw)[0])]

        def cut_row(eng, copy, half):
            eng.wait_ge(img_in, 32)
            done = 0
            for j, nw, y0 in ROWS_OF:
                parts = [p for p in window_parts(img, nw) if p[0] == y0]
                turns = parts[0][1] // 2
                with eng.Fori(0, turns) as i:
                    eng.wait_ge(stored[half], i * 16 + 16 * (done + 1))
                    for n, (_, _, x0, nx, v) in enumerate(parts):
                        src = v[:, bass.ds(i * 2 + half, 1), 0:nx].rearrange("p o x u v -> p (o x) u v")
                        dst = tile[:, half, x0 * nw * nw:(x0 + nx) * nw * nw].rearrange("p (x u v) -> p x u v", u=nw, v=nw)
                        ins = copy(dst, src)
                    ins.then_inc(s_cut[half], 1)
                done += turns

        with nc.Block() as block:
            @block.sync
            def _(sp):
                for b in range(B):
                    sp.dma_start(img[b * CB:(b + 1) * CB, 0:H, 0:W],
                                 d.xc[b].rearrange("c (y x) -> c y x", x=W)).then_inc(img_in, 16)
                for k in range(2):
                    sp.sem_inc(stored[k], 16)
                done = 0
                for j, nw, y0 in ROWS_OF:
                    k = window(nw)[1]
                    n = k * nw * nw
                    u = d.u[j].rearrange("b c n -> (b c) n")
                    turns = [p for p in window_parts(img, nw) if p[0] == y0][0][1] // 2
                    with sp.Fori(0, turns) as i:
                        for half in range(2):
                            sp.wait_ge(s_cut[half], i + (done + 1))
                            sp.dma_start(at(u, (i * 2 + (y0 + half)) * n, n), tile[:, half, 0:n]).then_inc(stored[half], 16)
                    done += turns
                for k in range(2):
                    sp.wait_ge(stored[k], 16 * done + 16)

            @block.vector
            def _(ve):
                cut_row(ve, nc.vector.tensor_copy, 0)

            @block.scalar
            def _(act):
                cut_row(act, lambda dst, src: nc.scalar.activation(dst, src, ACT.Copy), 1)


def phase_mix(nc, sems, a, d):
    with ExitStack() as mem:
        def sb(name, shape, dt=F32):
            return mem.enter_context(nc.sbuf_tensor("m_" + name, shape, dt))

        def ps(name, shape, dt=F32):
            return mem.enter_context(nc.psum_tensor("m_" + name, shape, dt))

        def sem(name):
            return sems.new("m_" + name)

        AT_ONCE = {4: 1, 8: 4, 12: 3}
        SE = 8
        BIG = 1024
        ident = sb("ident", [P, P])
        w2r = sb("w2r", [P, P])
        w2 = sb("w2", [P, P])
        se1r = sb("se1r", [SE, P])
        se1 = sb("se1", [P, SE])
        se2r = sb("se2r", [P, SE])
        se2 = sb("se2", [SE, P])
        b2 = sb("b2", [P, 1])
        wp = sb("wp", [P, 9])
        bp = sb("bp", [P, 1])
        u = sb("u", [P, 2, BIG])
        y = sb("y", [P, 2, BIG])
        acc = sb("acc", [P, 2, BIG])
        ysum = sb("ysum", [P, 2, 4])
        r = sb("r", [SE, 2, 4])
        sg = sb("sg", [P, 2, 4])
        pY = ps("pY", [P, 2, 3, 512])
        pE = ps("pE", [P, 512])
        pG = ps("pG", [P, 512])

        made, con, cleared, pre_pe, pre_dv = (sem(n) for n in ("made", "con", "cleared", "pre_pe", "pre_dv"))
        dv = sem("dv")
        u_in = [sem(f"u_in{k}") for k in range(2)]
        s_Y = sem("s_Y")
        s_y = sem("s_y")
        s_E = sem("s_E")
        s_r = sem("s_r")
        s_G = sem("s_G")
        s_sg = sem("s_sg")
        s_a = sem("s_a")
        a_out = [sem(f"a_out{k}") for k in range(2)]

        def chunks(nw):
            return nw * nw // AT_ONCE[nw]

        def each():
            done = 0
            for j, nw in enumerate(WINDOWS):
                yield j, nw, AT_ONCE[nw], window(nw)[1] ** 2, done
                done += chunks(nw)

        TOTAL = sum(chunks(nw) for nw in WINDOWS)

        with nc.Block() as block:
            @block.gpsimd
            def _(gp):
                nc.gpsimd.memset(ident[:, :], 0.0).then_inc(made, 1)
                gp.wait_ge(made, 1)
                nc.gpsimd.affine_select(out=ident[:, :], in_=ident[:, :], compare_op=ALU.not_equal, fill=1.0,
                                        base=0, pattern=[[-1, P]], channel_multiplier=1).then_inc(made, 1)
                for j, nw, nb, kk, done in each():
                    src = [d.u[j][b].rearrange("c n -> (c n)").rearrange("(w c n) -> c w n", c=CB, n=kk) for b in range(B)]
                    with gp.Fori(0, chunks(nw) // 2) as ii:
                        for half in range(2):
                            gp.wait_ge(s_a, ii * 2 + (done + half + 1))
                            for b in range(B):
                                gp.dma_start(u[b * CB:(b + 1) * CB, half, 0:nb * kk].rearrange("p (w n) -> p w n", n=kk),
                                             src[b][:, bass.ds((ii * 2 + half) * nb, nb), :]).then_inc(u_in[half], 16)

            @block.sync
            def _(sp):
                def cin(dst, src):
                    sp.dma_start(dst, src).then_inc(con, 16)

                sp.wait_ge(cleared, 3)
                with nc.allow_non_contiguous_dma("small constants"):
                    for b in range(B):
                        s = slice(b * CB, (b + 1) * CB)
                        e = slice(b * SE // 2, (b + 1) * SE // 2)
                        cin(w2r[s, s], a["L1_conv_w2"])
                        cin(se1r[e, s], a["L1_conv_wse1"])
                        cin(se2r[s, e], a["L1_conv_wse2"])
                        cin(b2[s, :], a["L1_conv_b2"].rearrange("(c o) -> c o", o=1))
                        cin(bp[s, :], a["L1_conv_bpos"].rearrange("(c o) -> c o", o=1))
                        cin(wp[s, :], a["L1_conv_wpos"].rearrange("c o y x -> c (o y x)"))
                for k in range(2):
                    sp.sem_inc(a_out[k], 32)
                for j, nw, nb, kk, done in each():
                    dst = [d.v[j][b].rearrange("c n -> (c n)").rearrange("(w c n) -> c w n", c=CB, n=kk) for b in range(B)]
                    with sp.Fori(0, chunks(nw) // 2) as ii:
                        for half in range(2):
                            sp.wait_ge(s_a, ii * 2 + (done + half + 3))
                            for b in range(B):
                                sp.dma_start(dst[b][:, bass.ds((ii * 2 + half) * nb, nb), :],
                                             acc[b * CB:(b + 1) * CB, half, 0:nb * kk]
                                             .rearrange("p (w n) -> p w n", n=kk)).then_inc(a_out[half], 16)
                for k in range(2):
                    sp.wait_ge(a_out[k], 16 * TOTAL + 32)

            @block.tensor
            def _(te):
                te.wait_ge(made, 2)
                te.wait_ge(con, 16 * 12)
                nc.tensor.transpose(pE[:, 0:P], w2r[:, :], ident[:, :]).then_inc(pre_pe, 1)
                nc.tensor.transpose(pE[:, P:P + SE], se1r[:, :], ident[0:SE, 0:SE]).then_inc(pre_pe, 1)
                nc.tensor.transpose(pG[0:SE, 0:P], se2r[:, :], ident[:, :]).then_inc(pre_pe, 1)
                te.wait_ge(pre_dv, 1)
                for j, nw, nb, kk, done in each():
                    g = max(kk, 512) if kk > 512 else (512 // kk) * kk
                    g = min(g, 512)
                    with te.Fori(0, chunks(nw) // 2) as ii:
                        for half in range(2):
                            i = ii * 2 + (done + half)
                            te.wait_ge(u_in[half], ii * 32 + (32 + 16 * done))
                            te.wait_ge(s_y, i + 1)
                            for q in range(nb * kk // g):
                                mm = nc.tensor.matmul(pY[:, half, q, 0:g], w2[:, :], u[:, half, q * g:(q + 1) * g],
                                                      start=True, stop=True)
                            mm.then_inc(s_Y, 1)
                            te.wait_ge(s_y, i + 3)
                            nc.tensor.matmul(pE[0:SE, 0:nb], se1[:, :], ysum[:, half, 0:nb], start=True,
                                             stop=True).then_inc(s_E, 1)
                            te.wait_ge(s_r, i + 1)
                            nc.tensor.matmul(pG[:, 0:nb], se2[:, :], r[:, half, 0:nb], start=True,
                                             stop=True).then_inc(s_G, 1)

            @block.scalar
            def _(act):
                act.sem_inc(s_y, 2)
                for j, nw, nb, kk, done in each():
                    with act.Fori(0, chunks(nw) // 2) as ii:
                        for half in range(2):
                            i = ii * 2 + (done + half)
                            act.wait_ge(s_Y, i + 1)
                            act.wait_ge(s_a, i + 1)
                            for w in range(nb):
                                if kk > 512:
                                    src = pY[:, half, 0:kk // 512, :].rearrange("p q n -> p (q n)")
                                elif 512 // kk == 1:
                                    src = pY[:, half, w, 0:kk]
                                else:
                                    per = 512 // kk
                                    src = pY[:, half, w // per, (w % per) * kk:(w % per + 1) * kk]
                                ins = nc.scalar.activation(y[:, half, w * kk:(w + 1) * kk], src, ACT.Identity,
                                                           bias=b2[:, 0:1], accum_out=ysum[:, half, w:w + 1])
                            ins.then_inc(s_y, 1)
                            act.wait_ge(s_E, i + 1)
                            nc.scalar.activation(r[:, half, 0:nb], pE[0:SE, 0:nb], ACT.Relu,
                                                 scale=1.0 / kk).then_inc(s_r, 1)
                            act.wait_ge(s_G, i + 1)
                            nc.scalar.activation(sg[:, half, 0:nb], pG[:, 0:nb], ACT.Sigmoid).then_inc(s_sg, 1)

            @block.vector
            def _(ve):
                link = Link(ve, dv)
                nc.vector.memset(w2r[:, :], 0.0).then_inc(cleared, 1)
                nc.vector.memset(se1r[:, :], 0.0).then_inc(cleared, 1)
                nc.vector.memset(se2r[:, :], 0.0).then_inc(cleared, 1)
                ve.sem_inc(s_a, 2)
                ve.wait_ge(pre_pe, 3)
                link(nc.vector.tensor_copy(w2[:, :], pE[:, 0:P]))
                link(nc.vector.tensor_copy(se1[:, :], pE[:, P:P + SE]))
                link(nc.vector.tensor_copy(se2[:, :], pG[0:SE, 0:P]))
                ve.sem_inc(pre_dv, 1)
                start = link.n
                per = 9
                for j, nw, nb, kk, done in each():
                    k = window(nw)[1]
                    with ve.Fori(0, chunks(nw) // 2) as ii:
                        for half in range(2):
                            i = ii * 2 + (done + half)
                            link.base, link.n = i * per + start, 0
                            ve.wait_ge(u_in[half], ii * 32 + (32 + 16 * done))
                            ve.wait_ge(a_out[half], ii * 32 + (32 + 16 * done))
                            n = nb * kk
                            link(nc.vector.tensor_scalar(acc[:, half, 0:n], u[:, half, 0:n], wp[:, 4:5], bp[:, 0:1],
                                                         ALU.mult, ALU.add))
                            uv = u[:, half, 0:n].rearrange("p (w y x) -> p w y x", y=k, x=k)
                            av = acc[:, half, 0:n].rearrange("p (w y x) -> p w y x", y=k, x=k)
                            for t in (0, 1, 2, 3, 5, 6, 7, 8):
                                dy, dx = t // 3 - 1, t % 3 - 1
                                ys, xs = slice(max(0, -dy), k - max(0, dy)), slice(max(0, -dx), k - max(0, dx))
                                yi, xi = slice(ys.start + dy, ys.stop + dy), slice(xs.start + dx, xs.stop + dx)
                                for w in range(nb):
                                    ins = nc.vector.scalar_tensor_tensor(av[:, w, ys, xs], uv[:, w, yi, xi], wp[:, t:t + 1],
                                                                         av[:, w, ys, xs], ALU.mult, ALU.add)
                                link(ins)
                            ve.wait_ge(s_sg, i + 1)
                            for w in range(nb):
                                o = acc[:, half, w * kk:(w + 1) * kk]
                                ins = nc.vector.scalar_tensor_tensor(o, y[:, half, w * kk:(w + 1) * kk],
                                                                     sg[:, half, w:w + 1], o, ALU.mult, ALU.add)
                            ins.then_inc(s_a, 1)


def phase_fold(nc, sems, a, d):
    with ExitStack() as mem:
        def sb(name, shape, dt=F32):
            return mem.enter_context(nc.sbuf_tensor("b_" + name, shape, dt))

        def sem(name):
            return sems.new("b_" + name)

        field = [sb(f"field{k}", [P, H + 2, PITCH]) for k in range(2)]
        tile = sb("tile", [P, 2, max(window(n)[1] * n * n for n in WINDOWS)])
        tile_in = [sem(f"tile_in{k}") for k in range(2)]
        s_used = [sem(f"s_used{k}") for k in range(2)]
        s_zero = sem("s_zero")
        dv = sem("dv")
        s_done = sem("s_done")
        out_f = [sem(f"out_f{k}") for k in range(WB)]
        ROWS_OF = [(j, nw, part) for j, nw in enumerate(WINDOWS) for part in range(0, window(nw)[1], window(nw)[0])]
        PLAIN = [x for x in ROWS_OF if H % x[1] == 0]
        SHARED = [x for x in ROWS_OF if H % x[1]]

        def turns_of(nw, y0):
            return min(window(nw)[0], window(nw)[1] - y0) // 2

        def place(eng, copy, half):
            done = 0
            for j, nw, y0 in PLAIN:
                y0_, ny, x0, nx, v = window_parts(field[j % 2], nw)[0]
                with eng.Fori(0, ny // 2) as i:
                    eng.wait_ge(tile_in[half], i * 16 + 16 * (done + 1))
                    dst = v[:, bass.ds(i * 2 + half, 1), 0:nx].rearrange("p o x u v -> p (o x) u v")
                    src = tile[:, half, 0:nx * nw * nw].rearrange("p (x u v) -> p x u v", u=nw, v=nw)
                    copy(dst, src).then_inc(s_used[half], 1)
                done += ny // 2
            return done

        with nc.Block() as block:
            @block.gpsimd
            def _(gp):
                done = 0
                for j, nw, y0 in ROWS_OF:
                    k = window(nw)[1]
                    n = k * nw * nw
                    v = d.v[j].rearrange("b c n -> (b c) n")
                    with gp.Fori(0, turns_of(nw, y0)) as i:
                        for half in range(2):
                            gp.wait_ge(s_used[half], i + (done + 1))
                            gp.dma_start(tile[:, half, 0:n], at(v, (i * 2 + (y0 + half)) * n, n)).then_inc(tile_in[half], 16)
                    done += turns_of(nw, y0)

            @block.sync
            def _(sp):
                def store(j):
                    for b in range(B):
                        sp.dma_start(d.cat[b, j * CB:(j + 1) * CB].rearrange("c (y x) -> c y x", x=W),
                                     field[j % 2][b * CB:(b + 1) * CB, 0:H, 0:W]).then_inc(out_f[j], 16)

                done = 0
                for j, nw, y0 in PLAIN:
                    done += turns_of(nw, y0)
                    for k in range(2):
                        sp.wait_ge(s_used[k], done + 1)
                    store(j)
                sp.wait_ge(s_done, 1)
                store(WB - 1)
                for k in range(WB):
                    sp.wait_ge(out_f[k], 16 * B)

            @block.scalar
            def _(act):
                act.sem_inc(s_used[1], 1)
                place(act, lambda dst, src: nc.scalar.activation(dst, src, ACT.Copy), 1)

            @block.vector
            def _(ve):
                link = Link(ve, dv)
                ve.sem_inc(s_used[0], 1)
                done = place(ve, nc.vector.tensor_copy, 0)
                F_ = field[(WB - 1) % 2]
                ve.wait_ge(out_f[0], 16 * B)
                ve.wait_ge(s_used[1], done + 1)
                link(nc.vector.memset(F_[:, :, :], 0.0))
                base = link.n
                for j, nw, y0 in SHARED:
                    parts = [p for p in window_parts(F_, nw) if p[0] == y0]
                    turns = turns_of(nw, y0)
                    with ve.Fori(0, turns) as i:
                        for half in range(2):
                            link.base, link.n = i * 4 + base, 2 * half
                            ve.wait_ge(tile_in[half], i * 16 + 16 * (done + 1))
                            for _, _, x0, nx, v in parts:
                                dst = v[:, bass.ds(i * 2 + half, 1), 0:nx].rearrange("p o x u v -> p (o x) u v")
                                src = tile[:, half, x0 * nw * nw:(x0 + nx) * nw * nw].rearrange("p (x u v) -> p x u v", u=nw, v=nw)
                                link(nc.vector.tensor_tensor(dst, dst, src, ALU.add))
                            ve.sem_inc(s_used[half], 1)
                    base += turns * 4
                    done += turns
                link.base, link.n = base, 0
                nw = WINDOWS[-1]
                step, k = window(nw)
                rows = F_[:, step:nw * step, 0:W].rearrange("p (u y) x -> p u y x", y=step)[:, :, 0:k - step]
                link(nc.vector.tensor_scalar(rows, rows, 0.5, None, ALU.mult))
                cols = F_[:, 0:H, step:nw * step].rearrange("p y (v x) -> p y v x", x=step)[:, :, :, 0:k - step]
                nc.vector.tensor_scalar(cols, cols, 0.5, None, ALU.mult).then_inc(s_done, 1)


def phase_last(nc, sems, a, d, out):
    with ExitStack() as mem:
        def sb(name, shape, dt=F32):
            return mem.enter_context(nc.sbuf_tensor("l_" + name, shape, dt))

        def ps(name, shape, dt=F32):
            return mem.enter_context(nc.psum_tensor("l_" + name, shape, dt))

        def sem(name):
            return sems.new("l_" + name)

        TN = 2048
        TURNS = B * N // TN
        PI = N // TN
        ident = sb("ident", [P, P])
        w3r = sb("w3r", [KC, 2, C])
        w3 = sb("w3", [KC, 2, C])
        b3 = sb("b3", [KC, 2])
        x = sb("x", [KC, 2, 2, TN])
        f = sb("f", [KC, 2, 2, TN])
        o = sb("o", [KC, 2, 2, TN])
        pO = ps("pO", [KC, 8, 512])
        made, con, pre_pe, pre_dv = (sem(n) for n in ("made", "con", "pre_pe", "pre_dv"))
        x_in = [sem(f"x_in{k}") for k in range(2)]
        s_x = sem("s_x")
        s_O = sem("s_O")
        s_o = sem("s_o")
        o_out = [sem(f"o_out{k}") for k in range(2)]
        x_v = d.x1.rearrange("b (k p) n -> b p k n", k=2)
        f_v = d.cat.rearrange("b (k p) n -> b p k n", k=2)
        o_v = out.rearrange("b (k p) h w -> b p k (h w)", k=2)

        with nc.Block() as block:
            @block.gpsimd
            def _(gp):
                nc.gpsimd.memset(ident[:, :], 0.0).then_inc(made, 1)
                gp.wait_ge(made, 1)
                nc.gpsimd.affine_select(out=ident[:, :], in_=ident[:, :], compare_op=ALU.not_equal, fill=1.0,
                                        base=0, pattern=[[-1, P]], channel_multiplier=1).then_inc(made, 1)
                with gp.Fori(0, TURNS // 2) as ii:
                    for half in range(2):
                        i = ii * 2 + half
                        gp.wait_ge(s_O, i * 8 + 8)
                        for t, v in ((x, x_v), (f, f_v)):
                            gp.dma_start(t[:, half, :, :], v[bass.ds(i // PI, 1), :, :, bass.ds((i % PI) * TN, TN)]
                                         .rearrange("b p k n -> (b p) k n")).then_inc(x_in[half], 16)

            @block.sync
            def _(sp):
                sp.dma_start(w3r[:, :, :], a["L1_conv_w3"].rearrange("(m p) c -> p m c", m=2)).then_inc(con, 16)
                with nc.allow_non_contiguous_dma("small constants"):
                    sp.dma_start(b3[:, :], a["L1_conv_b3"].rearrange("(m p) -> p m", m=2)).then_inc(con, 16)
                for k in range(2):
                    sp.sem_inc(o_out[k], 16)
                with sp.Fori(0, TURNS // 2) as ii:
                    for half in range(2):
                        i = ii * 2 + half
                        sp.wait_ge(s_o, i * 8 + 16)
                        sp.dma_start(o_v[bass.ds(i // PI, 1), :, :, bass.ds((i % PI) * TN, TN)]
                                     .rearrange("b p k n -> (b p) k n"), o[:, half, :, :]).then_inc(o_out[half], 16)
                for k in range(2):
                    sp.wait_ge(o_out[k], 16 * (TURNS // 2) + 16)

            @block.tensor
            def _(te):
                te.sem_inc(s_O, 16)
                te.wait_ge(made, 2)
                te.wait_ge(con, 32)
                for m in range(2):
                    for k in range(2):
                        nc.tensor.transpose(pO[:, k, m * KC:(m + 1) * KC], w3r[:, m, k * KC:(k + 1) * KC],
                                            ident[0:KC, 0:KC]).then_inc(pre_pe, 1)
                te.wait_ge(pre_dv, 1)
                with te.Fori(0, TURNS // 2) as ii:
                    for half in range(2):
                        i = ii * 2 + half
                        te.wait_ge(s_x, i + 1)
                        for m in range(2):
                            for q in range(4):
                                n = m * 4 + q
                                te.wait_ge(s_o, i * 8 + (n + 1))
                                for k in range(2):
                                    mm = nc.tensor.matmul(pO[:, n, :], w3[:, k, m * KC:(m + 1) * KC],
                                                          x[:, half, k, q * 512:(q + 1) * 512], start=(k == 0), stop=(k == 1))
                                mm.then_inc(s_O, 1)

            @block.scalar
            def _(act):
                act.sem_inc(s_o, 8)
                with act.Fori(0, TURNS // 2) as ii:
                    for half in range(2):
                        i = ii * 2 + half
                        act.wait_ge(o_out[half], ii * 16 + 16)
                        for n in range(8):
                            act.wait_ge(s_O, i * 8 + (n + 17))
                            m, q = n // 4, n % 4
                            nc.scalar.activation(o[:, half, m, q * 512:(q + 1) * 512], pO[:, n, :], ACT.Identity,
                                                 bias=b3[:, m:m + 1]).then_inc(s_o, 1)

            @block.vector
            def _(ve):
                ve.wait_ge(pre_pe, 4)
                nc.vector.tensor_copy(w3[:, :, :], pO[:, 0:2, 0:C]).then_inc(pre_dv, 1)
                with ve.Fori(0, TURNS // 2) as ii:
                    for half in range(2):
                        ve.wait_ge(x_in[half], ii * 32 + 32)
                        nc.vector.tensor_tensor(x[:, half, :, :], x[:, half, :, :], f[:, half, :, :], ALU.add).then_inc(s_x, 1)


class Semaphores:

    def __init__(self, nc):
        self.nc, self.held = nc, []

    def new(self, name):
        self.held.append(self.nc.alloc_semaphore(name=name))
        return self.held[-1]

    def clear(self):
        self.nc.clear_and_free_semaphores(self.held)
        self.held = []
        self.nc.all_engine_barrier()


def build(nc, a, out, phases="tsadfcmbl"):
    d = scratch(nc)
    sems = Semaphores(nc)
    work = {"t": phase_tokens, "s": phase_sort, "a": phase_attend, "d": phase_features, "f": phase_ffn,
            "c": phase_cut, "m": phase_mix, "b": phase_fold}
    for phase in phases:
        if phase == "l":
            phase_last(nc, sems, a, d, out)
        else:
            work[phase](nc, sems, a, d)
        if phase != phases[-1]:
            sems.clear()


_INS = ['x', 'L0_conv_td', 'L0_conv_g1', 'L0_conv_b1', 'L0_conv_g2', 'L0_conv_b2', 'L0_conv_g3', 'L0_conv_b3',
        'L0_conv_wq_w', 'L0_conv_wq_b', 'L0_conv_wk_w', 'L0_conv_wk_b', 'L0_conv_wv_w', 'L0_conv_wv_b',
        'L0_conv_ca_scale', 'L0_conv_wqkv_w', 'L0_conv_wqkv_b', 'L0_conv_proj_w', 'L0_conv_proj_b',
        'L0_conv_fc_td_w', 'L0_conv_fc_td_b', 'L0_conv_fc1_w', 'L0_conv_fc1_b', 'L0_conv_dw_w', 'L0_conv_dw_b',
        'L0_conv_fc2_w', 'L0_conv_fc2_b', 'L1_conv_w1', 'L1_conv_b1', 'L1_conv_w2', 'L1_conv_b2', 'L1_conv_w3',
        'L1_conv_b3', 'L1_conv_wpos', 'L1_conv_bpos', 'L1_conv_wse1', 'L1_conv_wse2']


def kernel(**inputs):
    import concourse.bacc as bacc
    from concourse.bass_utils import run_bass_kernel_spmd

    nc = bacc.Bacc("TRN2", target_bir_lowering=False, num_devices=1)
    arrays, args = {}, {}
    for name in _INS:
        x = np.ascontiguousarray(inputs[name])
        arrays["in_" + name] = x
        args[name] = nc.dram_tensor("in_" + name, x.shape, mybir.dt.from_np(x.dtype), kind="ExternalInput").ap()
    out = nc.dram_tensor("out_0", (B, C, H, W), F32, kind="ExternalOutput").ap()
    build(nc, args, out)
    r = run_bass_kernel_spmd(nc, [arrays], core_ids=[0])
    return r.results[0]["out_0"]
```

```python
from contextlib import ExitStack

import numpy as np

import concourse.bass as bass
from concourse import mybir

ALU = mybir.AluOpType
ACT = mybir.ActivationFunctionType
AX = mybir.AxisListType
F32 = mybir.dt.float32
BF16 = mybir.dt.bfloat16
I32 = mybir.dt.int32
U32 = mybir.dt.uint32

B, C, H, W = 2, 192, 128, 128
N = H * W
P = 128
KC = C // 2
M = 128
RD = 10
HEADS, HD = 4, C // 4
GS = 256
TDF = 16
HID = 4 * C
KS = 5
PADY = KS // 2
HP = H + 2 * PADY
BT = 512
TT = BT // P
NB = N // BT
EPS = 1e-5


class Scratch:
    pass


def scratch(nc):
    d = Scratch()

    def t(name, shape, dt=F32):
        return nc.dram_tensor(name, shape, dt, kind="Internal").ap()

    d.xh = t("xhat_rows", (B * N, C))
    d.xt = t("xhat_chan", (B, C + 1, HP * W))
    d.td = t("td_chan", (B, TDF, HP * W))
    d.res = t("res_chan", (B, C, N))
    d.xs = t("xhat_sorted", (B * N, C))
    d.pos = t("sorted_pos", (P, B * N // P), I32)
    d.aca = t("attn_sorted", (B * N, C))
    d.tdc = t("td_sum", (B, TDF, N))
    d.x1 = t("x1_chan", (B, C, N))
    d.xc = t("xc_chan", (B, C // 3, N))
    d.u = [t(f"cut_{nw}", (B, CB, (window(nw)[1] * nw) ** 2)) for nw in WINDOWS]
    d.v = [t(f"worked_{nw}", (B, CB, (window(nw)[1] * nw) ** 2)) for nw in WINDOWS]
    d.cat = t("folded", (B, C, N))
    return d


def at(ap, lo, n):
    return ap[:, bass.ds(lo, n)]


class Link:

    def __init__(self, eng, sem):
        self.eng, self.sem, self.base, self.n = eng, sem, 0, 0

    def loop(self, i, per):
        self.base, self.n, self.per = self.base + self.n + i * per, 0, per

    def end(self, total):
        assert self.n == self.per, (self.n, self.per)
        self.base, self.n = total, 0

    def __call__(self, ins):
        ins.then_inc(self.sem, 1)
        self.n += 1
        self.eng.wait_ge(self.sem, self.base + self.n)


def phase_tokens(nc, sems, a, d):
    with ExitStack() as mem:
        def sb(name, shape, dt=F32):
            return mem.enter_context(nc.sbuf_tensor("t_" + name, shape, dt))

        def ps(name, shape, dt=F32):
            return mem.enter_context(nc.psum_tensor("t_" + name, shape, dt))

        def sem(name):
            return sems.new("t_" + name)

        ident = sb("ident", [P, P])
        identb = sb("identb", [P, P], BF16)
        onesb = sb("onesb", [P, P], BF16)
        tri = sb("tri", [P, P], BF16)
        onesf = sb("onesf", [P, P])
        zeros = sb("zeros", [P, 2 * W])
        iota = sb("iota", [P, P])
        tdr = sb("tdr", [P, C])
        tdT = sb("tdT", [KC, 2, P])
        g1 = sb("g1", [KC, 2])
        b1 = sb("b1", [KC, 2])
        wq = sb("wq", [KC, 2, RD])
        wqg = sb("wqg", [KC, 2, RD])
        wk = sb("wk", [KC, 2, RD])
        wv = sb("wv", [KC, 2, C])
        wt = sb("wt", [KC, 2, TDF])
        rows = sb("rows", [1, RD + RD + C + TDF])
        bq = sb("bq", [1, RD])
        ca = sb("ca", [P, 1])
        k0 = sb("k0", [P, RD])
        ksq = sb("ksq", [P, RD])
        kn2 = sb("kn2", [P, 1])
        kT = sb("kT", [RD, P])
        v = sb("v", [P, C])
        tdf = sb("tdf", [P, TDF])

        xin = sb("xin", [KC, 2, 2, BT])
        st6 = sb("st6", [P, TT, 6])
        mv = sb("mv", [P, TT, 2])
        rstd = sb("rstd", [P, TT])
        xh = sb("xh", [P, TT, C])
        xT = sb("xT", [KC, 2, BT])
        q = sb("q", [P, TT, RD])
        qsq = sb("qsq", [P, TT, RD])
        qn2 = sb("qn2", [P, TT])
        qn = sb("qn", [P, TT, RD])
        qT = sb("qT", [RD, BT])
        mx = sb("mx", [P, TT, 8])
        ix = sb("ix", [P, TT, 8], U32)
        nmx = sb("nmx", [P, TT])
        e = sb("e", [P, TT, M])
        esum = sb("esum", [P, TT])
        erec = sb("erec", [P, TT])
        pr = sb("pr", [P, TT, M])
        prT = sb("prT", [P, BT])
        cat = sb("cat", [P, TT])
        oh = sb("oh", [P, TT, M], BF16)
        ohT = sb("ohT", [P, BT])
        tdx = sb("tdx", [TDF, BT])
        rk = sb("rk", [P, TT, M])
        res = sb("res", [KC, 2, BT])
        seen = sb("seen", [P, M])
        cats = sb("cats", [P, B * NB * TT])
        rank = sb("rank", [P, B * NB * TT])
        tot = sb("tot", [P, B, M])
        ends = sb("ends", [P, B, M])
        off = sb("off", [P, B, M])
        pick = sb("pick", [P, M])
        eq = sb("eq", [P, M])
        posf = sb("posf", [P, B * NB * TT])
        posi = sb("posi", [P, B * NB * TT], I32)

        pT = ps("pT", [P, 2, 512])
        pX = ps("pX", [KC, 2, BT])
        pS = ps("pS", [P, TT, M])
        pP = ps("pP", [P, BT])
        pO = ps("pO", [P, BT], BF16)
        pR = ps("pR", [P, TT, M])
        pQ = pT[:, 0, 0:TT * RD].rearrange("p (t r) -> p t r", t=TT)
        pQT = pT[0:RD, 1, :]
        pD = pP[0:TDF, :]
        pN = pT[:, 1, 0:M]

        marks = sem("marks")
        s_var = sem("s_var")
        s_rs = sem("s_rs")
        s_sq = sem("s_sq")
        s_pw = sem("s_pw")
        con = sem("con")
        made = sem("made")
        pads = sem("pads")
        x_in = [sem(f"x_in{h}") for h in range(2)]
        x_free = sem("x_free")
        pe = sem("pe")
        dv = sem("dv")
        dvp = sem("dvp")
        s_xT = sem("s_xT")
        s_xh = sem("s_xh")
        s_xb = sem("s_xb")
        s_xc = sem("s_xc")
        s_q = sem("s_q")
        s_qn = sem("s_qn")
        s_qt = sem("s_qt")
        s_qc = sem("s_qc")
        s_s = sem("s_s")
        s_m = sem("s_m")
        s_e = sem("s_e")
        s_p = sem("s_p")
        s_oh = sem("s_oh")
        s_pt = sem("s_pt")
        s_pc = sem("s_pc")
        s_ot = sem("s_ot")
        s_oc = sem("s_oc")
        s_a = sem("s_a")
        s_r = sem("s_r")
        s_d = sem("s_d")
        s_dc = sem("s_dc")
        s_res = sem("s_res")
        s_rk = sem("s_rk")
        o_xh = sem("o_xh")
        o_xT = sem("o_xT")
        o_td = sem("o_td")
        o_res = sem("o_res")
        s_tot = sem("s_tot")
        s_cum = sem("s_cum")
        s_pos = sem("s_pos")
        o_pos = sem("o_pos")

        CON = 12
        x_v = a["x"].rearrange("b (k p) h w -> b p k (h w)", k=2)
        xt_v = d.xt[:, 0:C, :].rearrange("b (k p) n -> b p k n", k=2)
        res_v = d.res.rearrange("b (k p) n -> b p k n", k=2)
        xh_v = d.xh.rearrange("(n t p) c -> n p t c", t=TT, p=P)

        BLOCKS = B * NB

        def image(v, i, skip):
            return v[bass.ds(i // NB, 1), :, :, bass.ds((i % NB) * BT + skip, BT)].rearrange("b p k n -> (b p) k n")

        with nc.Block() as block:
            @block.sync
            def _(sp):
                def col(dst, src):
                    sp.dma_start(dst, src).then_inc(con, 16)

                with nc.allow_non_contiguous_dma('small constants'):
                    col(g1[:, :], a["L0_conv_g1"].rearrange("(k p) -> p k", k=2))
                    col(b1[:, :], a["L0_conv_b1"].rearrange("(k p) -> p k", k=2))
                    col(tdr[:, :], a["L0_conv_td"])
                    col(wq[:, :, :], a["L0_conv_wq_w"].rearrange("(k p) r -> p k r", k=2))
                    col(wk[:, :, :], a["L0_conv_wk_w"].rearrange("(k p) r -> p k r", k=2))
                    col(wv[:, :, :], a["L0_conv_wv_w"].rearrange("(k p) r -> p k r", k=2))
                    col(wt[:, :, :], a["L0_conv_fc_td_w"].rearrange("(k p) r -> p k r", k=2))
                    at0 = 0
                    for name in ("wq_b", "wk_b", "wv_b", "fc_td_b"):
                        src = a["L0_conv_" + name]
                        n = src.shape[0]
                        col(rows[:, at0:at0 + n], src.rearrange("(a n) -> a n", a=1))
                        at0 += n
                    col(ca[:, :], a["L0_conv_ca_scale"].rearrange("(a n) -> a n", a=1).broadcast_to([P, 1]))
                with sp.Fori(0, BLOCKS) as i:
                    sp.wait_ge(s_res, i + 2)
                    sp.dma_start(image(res_v, i, 0), res[:, :, :]).then_inc(o_res, 16)
                sp.wait_ge(o_res, 16 * B * NB + 16)
                sp.wait_ge(s_pos, 1)
                sp.dma_start(d.pos, posi[:, :]).then_inc(o_pos, 16)
                sp.wait_ge(o_pos, 16)

            @block.gpsimd
            def _(gp):
                nc.gpsimd.memset(ident[:, :], 0.0).then_inc(made, 1)
                nc.gpsimd.memset(identb[:, :], 0.0).then_inc(made, 1)
                nc.gpsimd.memset(tri[:, :], 1.0).then_inc(made, 1)
                nc.gpsimd.memset(onesb[:, :], 1.0).then_inc(made, 1)
                nc.gpsimd.memset(onesf[:, :], 1.0).then_inc(made, 1)
                nc.gpsimd.memset(zeros[:, :], 0.0).then_inc(made, 1)
                gp.wait_ge(made, 6)
                for m in (ident, identb):
                    nc.gpsimd.affine_select(out=m[:, :], in_=m[:, :], compare_op=ALU.not_equal, fill=1.0,
                                            base=0, pattern=[[-1, P]], channel_multiplier=1).then_inc(made, 1)
                nc.gpsimd.affine_select(out=tri[:, :], in_=tri[:, :], compare_op=ALU.is_gt, fill=0.0,
                                        base=0, pattern=[[1, P]], channel_multiplier=-1).then_inc(made, 1)
                nc.gpsimd.iota(iota[:, :], pattern=[[1, P]], base=0, channel_multiplier=0,
                               allow_small_or_imprecise_dtypes=True).then_inc(made, 1)
                gp.wait_ge(made, 10)
                edge = PADY * W
                for b in range(B):
                    for lo in (0, edge + N):
                        for c0, n in ((0, P), (P, C + 1 - P)):
                            gp.dma_start(d.xt[b, c0:c0 + n, lo:lo + edge], zeros[0:n, :]).then_inc(pads, 16)
                        gp.dma_start(d.td[b, :, lo:lo + edge], zeros[0:TDF, :]).then_inc(pads, 16)
                    gp.dma_start(d.xt[b, C, edge:edge + N].rearrange("(h w) -> h w", h=H),
                                 onesf[:, :]).then_inc(pads, 16)
                gp.wait_ge(pads, 16 * B * 7)
                with gp.Fori(0, BLOCKS // 2) as ii:
                    for half in range(2):
                        i = ii * 2 + half
                        gp.wait_ge(x_free, i + 1)
                        gp.dma_start(xin[:, :, half, :], image(x_v, i, 0)).then_inc(x_in[half], 16)

            @block.tensor
            def _(te):
                te.wait_ge(made, 10)
                te.wait_ge(con, 16 * CON)
                te.wait_ge(dvp, 1)
                for k in range(2):
                    nc.tensor.transpose(pT[0:KC, 0, k * P:(k + 1) * P], tdr[:, k * KC:(k + 1) * KC],
                                        ident[:, :]).then_inc(pe, 1)
                te.wait_ge(dvp, 2)
                at0 = RD
                for o, w_, n in ((0, wk, RD), (16, wv, C), (256, wt, TDF)):
                    dst = pT[:, 1, o:o + n]
                    for k in range(2):
                        nc.tensor.matmul(dst, tdT[:, k, :], w_[:, k, :], start=(k == 0), stop=False)
                    nc.tensor.matmul(dst, onesf[0:1, :], rows[:, at0:at0 + n], start=False, stop=True).then_inc(pe, 1)
                    at0 += n
                for k in range(2):
                    nc.tensor.matmul(pS[0:1, 0, 0:RD], b1[:, k:k + 1], wq[:, k, :], start=(k == 0),
                                     stop=(k == 1)).then_inc(pe, 1)
                te.wait_ge(dvp, 3)
                nc.tensor.transpose(pS[0:RD, 1, :], k0[:, :], ident[:, :]).then_inc(pe, 1)
                te.wait_ge(dvp, 4)

                def x_turned(i, half, turn):
                    te.wait_ge(x_in[half], turn * 16 + 16)
                    te.wait_ge(s_qn, i + 1)
                    te.wait_ge(s_qc, i + 1)
                    for t in range(TT):
                        for k in range(2):
                            mm = nc.tensor.transpose(
                                pT[:, t // 2, (t % 2) * C + k * KC:(t % 2) * C + (k + 1) * KC],
                                xin[:, k, half, t * P:(t + 1) * P], ident[0:KC, 0:KC])
                    mm.then_inc(s_xT, 1)

                def onehot_turned(b):
                    te.wait_ge(s_oh, b + 1)
                    for t in range(TT):
                        mm = nc.tensor.transpose(pO[:, t * P:(t + 1) * P], oh[:, t, :], identb[:, :])
                    mm.then_inc(s_ot, 1)

                def xhat_turned(i, first):
                    te.wait_ge(s_xh, i + 1)
                    if not first:
                        te.wait_ge(s_res, i)
                    for t in range(TT):
                        for k in range(2):
                            mm = nc.tensor.transpose(pX[:, k, t * P:(t + 1) * P], xh[:, t, k * KC:(k + 1) * KC],
                                                     ident[:, :])
                    mm.then_inc(s_xb, 1)

                def ranks(b):
                    te.wait_ge(s_rk, b + 1)
                    for t in range(TT):
                        nc.tensor.matmul(pR[:, t, :], tri[:, :], oh[:, t, :], start=True, stop=(t == 0))
                        for u in range(t):
                            nc.tensor.matmul(pR[:, t, :], onesb[:, :], oh[:, u, :], start=False, stop=(u == t - 1))
                    for u in range(TT):
                        mm = nc.tensor.matmul(pN, onesb[:, :], oh[:, u, :], start=(u == 0), stop=(u == TT - 1))
                    mm.then_inc(s_r, 1)

                def probs_turned(b):
                    te.wait_ge(s_p, b + 1)
                    te.wait_ge(s_dc, b + 1)
                    for t in range(TT):
                        mm = nc.tensor.transpose(pP[:, t * P:(t + 1) * P], pr[:, t, :], ident[:, :])
                    mm.then_inc(s_pt, 1)

                def queries(i):
                    te.wait_ge(s_xc, i + 2)
                    for t in range(TT):
                        for k in range(2):
                            nc.tensor.matmul(pQ[:, t, :], xT[:, k, t * P:(t + 1) * P], wqg[:, k, :],
                                             start=(k == 0), stop=False)
                        mm = nc.tensor.matmul(pQ[:, t, :], onesf[0:1, :], bq[:, :], start=False, stop=True)
                    mm.then_inc(s_q, 1)

                def looked_up(b):
                    te.wait_ge(s_pc, b + 1)
                    te.wait_ge(s_res, b + 1)
                    for k in range(2):
                        mm = nc.tensor.matmul(pX[:, k, :], v[:, k * KC:(k + 1) * KC], prT[:, :], start=True, stop=True)
                    mm.then_inc(s_a, 1)
                    te.wait_ge(s_oc, b + 1)
                    nc.tensor.matmul(pD, tdf[:, :], ohT[:, :], start=True, stop=True).then_inc(s_d, 1)

                def similarities(i, first):
                    te.wait_ge(s_qn, i + 2)
                    te.wait_ge(s_rk, i + 1)
                    for t in range(TT):
                        mm = nc.tensor.transpose(pQT[:, t * P:(t + 1) * P], qn[:, t, :], ident[:, :])
                    mm.then_inc(s_qt, 1)
                    te.wait_ge(s_qc, i + 2)
                    if not first:
                        te.wait_ge(s_e, i)
                    for t in range(TT):
                        mm = nc.tensor.matmul(pS[:, t, :], qT[:, t * P:(t + 1) * P], kT[:, :], start=True, stop=True)
                    mm.then_inc(s_s, 1)

                def period(i, half, turn, first=False, last=False):
                    if not last:
                        x_turned(i, half, turn)
                    if not first:
                        onehot_turned(i - 1)
                    if not last:
                        xhat_turned(i, first)
                    if not first:
                        ranks(i - 1)
                        probs_turned(i - 1)
                    if not last:
                        queries(i)
                    if not first:
                        looked_up(i - 1)
                    if not last:
                        similarities(i, first)

                period(0, 0, 0, first=True)
                with te.Fori(0, BLOCKS // 2 - 1) as ii:
                    period(ii * 2 + 1, 1, ii)
                    period(ii * 2 + 2, 0, ii + 1)
                period(BLOCKS - 1, 1, BLOCKS // 2 - 1)
                period(BLOCKS, None, None, last=True)
                te.wait_ge(s_tot, 1)
                for b in range(B):
                    mm = nc.tensor.matmul(pS[:, b, :], onesf[:, :], ends[:, b, :], start=True, stop=True)
                mm.then_inc(s_cum, 1)

            @block.scalar
            def _(act):
                for s in (s_xc, s_qc, s_dc):
                    act.sem_inc(s, 1)
                act.sem_inc(o_xh, 16)
                act.sem_inc(o_xT, 16)
                act.sem_inc(o_td, 16)
                act.sem_inc(o_res, 16)
                act.wait_ge(s_sq, 1)
                nc.scalar.activation(kn2[:, :], kn2[:, :], ACT.Sqrt).then_inc(s_pw, 1)

                def period(i, first=False, last=False):
                    b = i - 1
                    if not first:
                        act.wait_ge(s_m, b + 1)
                        for t in range(TT):
                            ins = nc.scalar.activation(e[:, t, :], pS[:, t, :], ACT.Exp, bias=nmx[:, t:t + 1],
                                                       scale=1.0, accum_out=esum[:, t:t + 1])
                        ins.then_inc(s_e, 1)
                    if not last:
                        act.wait_ge(s_var, i + 1)
                        nc.scalar.activation(rstd[:, :], rstd[:, :], ACT.Sqrt).then_inc(s_rs, 1)
                    if not first:
                        act.wait_ge(s_ot, b + 1)
                        nc.scalar.activation(ohT[:, :], pO[:, :], ACT.Copy).then_inc(s_oc, 1)
                    if not last:
                        act.wait_ge(s_xh, i + 1)
                        act.dma_start(xh_v[bass.ds(i, 1)].rearrange("a p t c -> (a p) t c"),
                                      xh[:, :, :]).then_inc(o_xh, 16)
                        act.wait_ge(s_xb, i + 1)
                        act.wait_ge(o_xT, i * 16 + 16)
                        nc.scalar.activation(xT[:, :, :], pX[:, :, :], ACT.Copy).then_inc(s_xc, 1)
                        act.wait_ge(s_xc, i + 2)
                        act.dma_start(image(xt_v, i, PADY * W), xT[:, :, :]).then_inc(o_xT, 16)
                    if not first:
                        act.wait_ge(s_pt, b + 1)
                        nc.scalar.activation(prT[:, :], pP[:, :], ACT.Copy).then_inc(s_pc, 1)
                    if not last:
                        act.wait_ge(s_sq, i + 2)
                        nc.scalar.activation(qn2[:, :], qn2[:, :], ACT.Sqrt).then_inc(s_pw, 1)
                    if not first:
                        act.wait_ge(s_d, b + 1)
                        act.wait_ge(o_td, b * 16 + 16)
                        nc.scalar.activation(tdx[:, :], pD, ACT.Copy).then_inc(s_dc, 1)
                        act.wait_ge(s_dc, b + 2)
                        act.dma_start(d.td[bass.ds(b // NB, 1), :, bass.ds((b % NB) * BT + PADY * W, BT)]
                                      .rearrange("b p n -> (b p) n"), tdx[:, :]).then_inc(o_td, 16)
                    if not last:
                        act.wait_ge(s_qt, i + 1)
                        nc.scalar.activation(qT[:, :], pQT, ACT.Copy).then_inc(s_qc, 1)

                period(0, first=True)
                with act.Fori(1, BLOCKS) as i:
                    period(i)
                period(BLOCKS, last=True)
                act.wait_ge(o_xh, 16 * B * NB + 16)
                act.wait_ge(o_xT, 16 * B * NB + 16)
                act.wait_ge(o_td, 16 * B * NB + 16)

            @block.vector
            def _(ve):
                link = Link(ve, dv)
                ve.sem_inc(dvp, 1)
                ve.sem_inc(x_free, 2)
                ve.sem_inc(s_rk, 1)
                ve.wait_ge(con, 16 * CON)
                ve.wait_ge(pe, 2)
                nc.vector.tensor_copy(tdT[:, :, :], pT[0:KC, 0, 0:2 * P].rearrange("p (k n) -> p k n", k=2)).then_inc(dvp, 1)
                for k in range(2):
                    nc.vector.tensor_scalar(wqg[:, k, :], wq[:, k, :], g1[:, k:k + 1], None, ALU.mult)
                nc.vector.memset(seen[:, :], 0.0)
                link(nc.vector.tensor_scalar(ca[:, :], ca[:, :], 0.0, 3.0, ALU.max, ALU.min))
                link(nc.vector.tensor_scalar(ca[:, :], ca[:, :], float(np.log(M)), 1.0, ALU.mult, ALU.add))
                ve.wait_ge(pe, 5)
                link(nc.vector.tensor_copy(k0[:, :], pT[:, 1, 0:RD]))
                nc.vector.tensor_copy(v[:, :], pT[:, 1, 16:16 + C])
                nc.vector.tensor_copy(tdf[:, :], pT[:, 1, 256:256 + TDF])
                link(nc.vector.tensor_tensor(ksq[:, :], k0[:, :], k0[:, :], ALU.mult))
                link(nc.vector.tensor_reduce(kn2[:, :], ksq[:, :], AX.X, ALU.add))
                nc.vector.tensor_scalar(kn2[:, :], kn2[:, :], 1e-24, None, ALU.max).then_inc(s_sq, 1)
                ve.wait_ge(s_pw, 1)
                link(nc.vector.reciprocal(kn2[:, :], kn2[:, :]))
                nc.vector.tensor_scalar(k0[:, :], k0[:, :], kn2[:, 0:1], ca[:, 0:1], ALU.mult,
                                        ALU.mult).then_inc(dvp, 1)
                ve.wait_ge(pe, 8)
                nc.vector.tensor_copy(kT[:, :], pS[0:RD, 1, :])
                link(nc.vector.tensor_tensor(bq[:, :], pS[0:1, 0, 0:RD], rows[:, 0:RD], ALU.add))
                ve.sem_inc(s_qn, 1)
                ve.sem_inc(s_res, 1)
                ve.sem_inc(dvp, 1)
                start = link.n
                AHEAD, BEHIND = 7, 8

                def statistics(i):
                    ve.wait_ge(s_xT, i + 1)
                    for t in range(TT):
                        ins = nc.vector.bn_stats(st6[:, t, :], pT[:, t // 2, (t % 2) * C:(t % 2) * C + C])
                    link(ins)
                    ve.sem_inc(marks, 1)
                    for t in range(TT):
                        ins = nc.vector.bn_aggr(mv[:, t, :], st6[:, t, :])
                    link(ins)
                    nc.vector.tensor_scalar(rstd[:, :], mv[:, :, 1], EPS, None, ALU.add).then_inc(s_var, 1)

                def normalised(i):
                    ve.wait_ge(s_rs, i + 1)
                    link(nc.vector.reciprocal(rstd[:, :], rstd[:, :]))
                    ve.wait_ge(o_xh, i * 16 + 16)
                    for t in range(TT):
                        ins = nc.vector.tensor_scalar(xh[:, t, :], pT[:, t // 2, (t % 2) * C:(t % 2) * C + C],
                                                      mv[:, t, 0:1], rstd[:, t:t + 1], ALU.subtract, ALU.mult)
                    ins.then_inc(s_xh, 1)

                def query_norms(i):
                    ve.wait_ge(s_q, i + 1)
                    link(nc.vector.tensor_copy(q[:, :, :], pQ))
                    link(nc.vector.tensor_tensor(qsq[:, :, :], q[:, :, :], q[:, :, :], ALU.mult))
                    link(nc.vector.tensor_reduce(qn2[:, :], qsq[:, :, :], AX.X, ALU.add))
                    nc.vector.tensor_scalar(qn2[:, :], qn2[:, :], 1e-24, None, ALU.max).then_inc(s_sq, 1)

                def queries_normed(i):
                    ve.wait_ge(s_pw, i + 2)
                    link(nc.vector.reciprocal(qn2[:, :], qn2[:, :]))
                    nc.vector.tensor_tensor(qn[:, :, :], q[:, :, :], qn2[:, :].unsqueeze(2).to_broadcast([P, TT, RD]),
                                            ALU.mult).then_inc(s_qn, 1)

                def maxima(b):
                    ve.wait_ge(s_s, b + 1)
                    link(nc.vector.tensor_reduce(nmx[:, :], pS[:, :, :], AX.X, ALU.max))
                    nc.vector.tensor_scalar(nmx[:, :], nmx[:, :], -1.0, None, ALU.mult).then_inc(s_m, 1)

                def categories(b):
                    ve.wait_ge(s_e, b + 1)
                    ve.sem_inc(marks, 1)
                    for t in range(TT):
                        ins = nc.vector.max(mx[:, t, :], e[:, t, :])
                    link(ins)
                    ve.sem_inc(marks, 1)
                    for t in range(TT):
                        ins = nc.vector.max_index(ix[:, t, :], mx[:, t, :], e[:, t, :])
                    link(ins)
                    link(nc.vector.tensor_copy(cat[:, :], ix[:, :, 0]))
                    nc.vector.tensor_copy(at(cats, b * TT, TT), cat[:, :])
                    for t in range(TT):
                        ins = nc.vector.tensor_scalar(oh[:, t, :], iota[:, :], cat[:, t:t + 1], None, ALU.is_equal)
                    ins.then_inc(s_oh, 1)

                def probabilities(b):
                    link(nc.vector.reciprocal(erec[:, :], esum[:, :]))
                    for t in range(TT):
                        ins = nc.vector.tensor_scalar(pr[:, t, :], e[:, t, :], erec[:, t:t + 1], None, ALU.mult)
                    ins.then_inc(s_p, 1)

                def ranked(b):
                    ve.wait_ge(s_r, b + 1)
                    link(nc.vector.tensor_tensor(rk[:, :, :], pR[:, :, :],
                                                 seen[:, :].unsqueeze(1).to_broadcast([P, TT, M]), ALU.add))
                    nc.vector.tensor_tensor(seen[:, :], seen[:, :], pN, ALU.add)
                    link(nc.vector.tensor_tensor(rk[:, :, :], rk[:, :, :], oh[:, :, :], ALU.mult))
                    ve.sem_inc(s_rk, 1)
                    nc.vector.tensor_reduce(at(rank, b * TT, TT), rk[:, :, :], AX.X, ALU.add)
                    link(nc.vector.tensor_copy(tot[:, bass.ds(b // NB, 1), :].rearrange("p a m -> p (a m)"), seen[:, :]))

                def result(b, half):
                    ve.wait_ge(s_a, b + 1)
                    ve.wait_ge(o_res, b * 16 + 16)
                    nc.vector.tensor_tensor(res[:, :, :], pX[:, :, :], xin[:, :, half, :], ALU.add).then_inc(s_res, 1)
                    ve.wait_ge(s_res, b + 2)
                    ve.sem_inc(x_free, 1)

                def period(i, half, first=False, last=False):
                    b = i - 1
                    link.base, link.n = (start if first else b * (AHEAD + BEHIND) + (start + AHEAD)), 0
                    if not first:
                        maxima(b)
                    if not last:
                        statistics(i)
                    if not first:
                        categories(b)
                    if not last:
                        normalised(i)
                    if not first:
                        probabilities(b)
                        ranked(b)
                    if not last:
                        query_norms(i)
                    if not first:
                        result(b, 1 - half)
                    if not last:
                        queries_normed(i)
                    assert link.n == AHEAD * (not last) + BEHIND * (not first), link.n

                period(0, 0, first=True)
                with ve.Fori(0, BLOCKS // 2 - 1) as ii:
                    period(ii * 2 + 1, 1)
                    period(ii * 2 + 2, 0)
                period(BLOCKS - 1, 1)
                period(BLOCKS, 0, last=True)
                link.base, link.n = BLOCKS * (AHEAD + BEHIND) + start, 0
                for b in range(B):
                    if b:
                        link(nc.vector.tensor_tensor(pick[:, :], tot[:, 1, :], tot[:, 0, :], ALU.subtract))
                    src = pick if b else tot[:, 0, :]
                    link(nc.vector.tensor_tensor(eq[:, :], src if b == 0 else pick[:, :], ident[:, :], ALU.mult))
                    link(nc.vector.tensor_reduce(kn2[:, :], eq[:, :], AX.X, ALU.add))
                    link(nc.vector.tensor_scalar(ends[:, b, :], tri[:, :], kn2[:, 0:1], None, ALU.mult))
                ve.sem_inc(s_tot, 1)
                ve.wait_ge(s_cum, 1)
                link(nc.vector.tensor_copy(off[:, 0, :], pS[:, 0, :]))
                link(nc.vector.tensor_tensor(eq[:, :], pS[:, 1, :], tot[:, 0, :], ALU.subtract))
                link(nc.vector.tensor_scalar(off[:, 1, :], eq[:, :], float(N), None, ALU.add))
                start2 = link.base + link.n
                with ve.Fori(0, B) as b:
                    with ve.Fori(0, NB) as j:
                        i = b * NB + j
                        link.base, link.n = i + start2, 0
                        for t in range(TT):
                            ins = nc.vector.scalar_tensor_tensor(
                                rk[:, t, :], iota[:, :], at(cats, i * TT + t, 1),
                                off[:, bass.ds(b, 1), :].rearrange("p a m -> p (a m)"), ALU.is_equal, ALU.mult,
                                accum_out=at(posf, i * TT + t, 1))
                        link(ins)
                link.base, link.n = B * NB + start2, 0
                link(nc.vector.tensor_tensor(posf[:, :], posf[:, :], rank[:, :], ALU.add))
                nc.vector.tensor_copy(posi[:, :], posf[:, :]).then_inc(s_pos, 1)


def phase_sort(nc, sems, a, d):
    with ExitStack() as mem:
        def sb(name, shape, dt=F32):
            return mem.enter_context(nc.sbuf_tensor("s_" + name, shape, dt))

        def sem(name):
            return sems.new("s_" + name)

        pos = sb("pos", [P, B * N // P], I32)
        idx = sb("idx", [P, 2, TT], I32)
        rows = sb("rows", [P, 2, TT, C])
        pos_in = sem("pos_in")
        marks = sem("marks")
        rows_in = [sem(f"rows_in{h}") for h in range(2)]
        rows_out = [sem(f"rows_out{h}") for h in range(2)]
        rows_free = sem("rows_free")
        idx_set = sem("idx_set")
        xh_v = d.xh.rearrange("(n t p) c -> n p t c", t=TT, p=P)
        TURNS = B * N // P // TT

        h = sb("h", [P, B, HROWS, WP])
        acc = sb("acc", [P, SN])
        g = sb("g", [P, B, SN])
        w = sb("w", [P, KS * KS])
        bias = sb("bias", [P, 1])
        cleared = sem("cleared")
        feat_in = sem("feat_in")
        dv = sem("dv")
        s_acc = sem("s_acc")
        s_g = sem("s_g")
        s_sum = sem("s_sum")
        stored = sem("stored")
        BANDS = H // ROWS

        with nc.Block() as block:
            @block.sync
            def _(sp):
                sp.dma_start(pos[:, :], d.pos).then_inc(pos_in, 16)
                sp.wait_ge(cleared, 1)
                with nc.allow_non_contiguous_dma("small constants"):
                    for j in range(BANDS):
                        sp.dma_start(w[j * TDF:(j + 1) * TDF, :],
                                     a["L0_conv_dw_w"][HID:HID + TDF].rearrange("c o y x -> c (o y x)")).then_inc(feat_in, 16)
                        sp.dma_start(bias[j * TDF:(j + 1) * TDF, :],
                                     a["L0_conv_dw_b"][HID:HID + TDF].rearrange("(c o) -> c o", o=1)).then_inc(feat_in, 16)
                        for b in range(B):
                            lo = j * ROWS * W
                            sp.dma_start(h[j * TDF:(j + 1) * TDF, b, :, PADY:PADY + W],
                                         d.td[b, :, lo:lo + HROWS * W].rearrange("c (y x) -> c y x", x=W)).then_inc(feat_in, 16)
                with sp.Fori(0, TURNS // 2) as ii:
                    for half in range(2):
                        i = ii * 2 + half
                        sp.wait_ge(rows_free, i + 1)
                        sp.dma_start(rows[:, half, :, :],
                                     xh_v[bass.ds(i, 1)].rearrange("a p t c -> (a p) t c")).then_inc(rows_in[half], 16)
                sp.wait_ge(s_sum, B)
                for j in range(BANDS):
                    for b in range(B):
                        sp.dma_start(d.tdc[b, :, j * SN:(j + 1) * SN], g[j * TDF:(j + 1) * TDF, b, :]).then_inc(stored, 16)
                sp.wait_ge(stored, 16 * B * BANDS)

            @block.gpsimd
            def _(gp):
                gp.sem_inc(rows_free, 2)
                gp.wait_ge(pos_in, 16)

                def send(ii, half):
                    i = ii * 2 + half
                    nc.gpsimd.tensor_copy(idx[:, half, :], at(pos, i * TT, TT)).then_inc(idx_set, 1)
                    gp.wait_ge(idx_set, i + 1)
                    gp.wait_ge(rows_in[half], ii * 16 + 16)
                    gp.sem_inc(marks, 1)
                    for t in range(TT):
                        gp.indirect_dma_start(d.xs[:, :], bass.IndirectOffsetOnAxis(ap=idx[:, half, t:t + 1], axis=0),
                                              rows[:, half, t, :], None).then_inc(rows_out[half], 16)

                def sent(ii, half):
                    gp.wait_ge(rows_out[half], ii * (16 * TT) + 16 * TT)
                    gp.sem_inc(rows_free, 1)

                send(0, 0)
                with gp.Fori(0, TURNS // 2 - 1) as ii:
                    send(ii, 1)
                    sent(ii, 0)
                    send(ii + 1, 0)
                    sent(ii, 1)
                send(TURNS // 2 - 1, 1)
                sent(TURNS // 2 - 1, 0)
                sent(TURNS // 2 - 1, 1)

            @block.scalar
            def _(act):
                for b in range(B):
                    act.wait_ge(s_acc, b + 1)
                    nc.scalar.activation(g[:, b, :], acc[:, :], ACT.Gelu, bias=bias[:, 0:1]).then_inc(s_g, 1)

            @block.vector
            def _(ve):
                link = Link(ve, dv)
                nc.vector.memset(h[:, :, :, :], 0.0).then_inc(cleared, 1)
                ve.wait_ge(feat_in, 16 * BANDS * (2 + B))
                for b in range(B):
                    for n, (y, x) in enumerate(ALL_TAPS):
                        view = h[:, b, y:y + ROWS, x:x + W]
                        out = acc[:, :].rearrange("p (y x) -> p y x", x=W)
                        if n == 0:
                            link(nc.vector.tensor_scalar(out, view, w[:, 0:1], None, ALU.mult))
                        elif n < len(ALL_TAPS) - 1:
                            link(nc.vector.scalar_tensor_tensor(out, view, w[:, n:n + 1], out, ALU.mult, ALU.add))
                        else:
                            nc.vector.scalar_tensor_tensor(out, view, w[:, n:n + 1], out, ALU.mult,
                                                           ALU.add).then_inc(s_acc, 1)
                    ve.wait_ge(s_g, b + 1)
                    nc.vector.tensor_tensor(g[:, b, :].rearrange("p (y x) -> p y x", x=W),
                                            g[:, b, :].rearrange("p (y x) -> p y x", x=W),
                                            h[:, b, PADY:PADY + ROWS, PADY:PADY + W], ALU.add).then_inc(s_sum, 1)


def phase_attend(nc, sems, a, d):
    with ExitStack() as mem:
        def sb(name, shape, dt=F32):
            return mem.enter_context(nc.sbuf_tensor("a_" + name, shape, dt))

        def ps(name, shape, dt=F32):
            return mem.enter_context(nc.psum_tensor("a_" + name, shape, dt))

        def sem(name):
            return sems.new("a_" + name)

        G = B * N // GS
        QT = GS // P
        SCALE = float(HD) ** -0.5
        ident = sb("ident", [P, P])
        ones = sb("ones", [1, P])
        g1 = sb("g1", [KC, 2])
        b1 = sb("b1", [KC, 2])
        b1w = sb("b1w", [KC, 2, P])
        wqk = sb("wqk", [KC, 2, 4, P])
        wqkg = sb("wqkg", [KC, 2, 4, P])
        wv = sb("wv", [KC, 2, C])
        wvg = sb("wvg", [KC, 2, C])
        wp = sb("wp", [KC, 2, C])
        bqk0 = sb("bqk0", [P, 4])
        bqk = sb("bqk", [P, 4])
        brow = sb("brow", [1, 2 * C])
        bv = sb("bv", [P, C])
        bp = sb("bp", [P, C])

        xs = sb("xs", [P, 2, QT, C])
        xT = sb("xT", [KC, 2, GS])
        qk = sb("qk", [P, 2, 4, GS])
        V = sb("V", [P, 2, QT, C])
        mxs = sb("mxs", [P, 2, QT])
        nmx = sb("nmx", [P, 2, QT])
        e = sb("e", [P, 2, QT, GS])
        esum = sb("esum", [P, QT, HEADS])
        erec = sb("erec", [P, QT, HEADS])
        eT = sb("eT", [P, 2, QT, GS])
        o = sb("o", [P, QT, C])
        oT = sb("oT", [KC, 2, GS])
        y = sb("y", [P, QT, C])

        pX = ps("pX", [KC, 2, GS])
        pQK = ps("pQK", [P, 4, GS])
        pS = ps("pS", [P, 2, QT, GS])
        pT = ps("pT", [P, QT, GS])
        pO = ps("pO", [P, 512])
        pM = ps("pM", [P, 512])
        oV = pO[:, 0:QT * C].rearrange("p (t h d) -> p t h d", t=QT, h=HEADS)
        mV = pM[:, 0:QT * C].rearrange("p (t c) -> p t c", t=QT)
        mT = pM[0:KC, :].rearrange("p (k n) -> p k n", k=2)

        made, con, cleared = sem("made"), sem("con"), sem("cleared")
        pre_pe, pre_dv = sem("pre_pe"), sem("pre_dv")
        dv = sem("dv")
        xs_in = [sem(f"xs_in{h}") for h in range(2)]
        s_X = sem("s_X")
        s_xc = sem("s_xc")
        s_QK = sem("s_QK")
        s_qk = sem("s_qk")
        s_V = sem("s_V")
        s_v = sem("s_v")
        s_S = sem("s_S")
        s_m = sem("s_m")
        s_E = sem("s_E")
        s_T = sem("s_T")
        s_tc = sem("s_tc")
        s_O = sem("s_O")
        s_o = sem("s_o")
        s_OT = sem("s_OT")
        s_oc = sem("s_oc")
        s_Y = sem("s_Y")
        s_y = sem("s_y")
        o_y = sem("o_y")

        xs_v = d.xs.rearrange("(g t p) c -> g p t c", t=QT, p=P)
        y_v = d.aca.rearrange("(g t p) c -> g p t c", t=QT, p=P)
        CON = 16

        def head(g, h):
            return g * HEADS + (h + 1 + HEADS)

        with nc.Block() as block:
            @block.sync
            def _(sp):
                def con_in(dst, src):
                    sp.dma_start(dst, src).then_inc(con, 16)

                wqkv, wb = a["L0_conv_wqkv_w"], a["L0_conv_wqkv_b"]
                sp.wait_ge(cleared, 2)
                with nc.allow_non_contiguous_dma("small constants"):
                    for k in range(2):
                        for w in range(2):
                            con_in(wqk[:, k, 2 * w:2 * w + 2, :].rearrange("p m (u e) -> p (m u) e", u=2)[:, :, 0:HD],
                                   wqkv[k * KC:(k + 1) * KC, w * C:(w + 1) * C].rearrange("p (h e) -> p h e", h=HEADS))
                    for u in range(2):
                        con_in(bqk0[64 * u:64 * u + HD, :],
                               wb[0:2 * C].rearrange("(m u e) -> u e m", u=2, e=HD)[u])
                    con_in(wv[:, :, :], wqkv[:, 2 * C:3 * C].rearrange("(k p) n -> p k n", k=2))
                    con_in(wp[:, :, :], a["L0_conv_proj_w"].rearrange("(k p) n -> p k n", k=2))
                    con_in(g1[:, :], a["L0_conv_g1"].rearrange("(k p) -> p k", k=2))
                    con_in(b1[:, :], a["L0_conv_b1"].rearrange("(k p) -> p k", k=2))
                    con_in(brow[:, 0:C], wb[2 * C:3 * C].rearrange("(a n) -> a n", a=1))
                    con_in(brow[:, C:2 * C], a["L0_conv_proj_b"].rearrange("(a n) -> a n", a=1))
                sp.sem_inc(o_y, 16)
                with sp.Fori(0, G) as g:
                    sp.wait_ge(s_y, g + 2)
                    sp.dma_start(y_v[bass.ds(g, 1)].rearrange("a p t c -> (a p) t c"), y[:, :, :]).then_inc(o_y, 16)
                sp.wait_ge(o_y, 16 * G + 16)

            @block.gpsimd
            def _(gp):
                nc.gpsimd.memset(ident[:, :], 0.0).then_inc(made, 1)
                nc.gpsimd.memset(ones[:, :], 1.0).then_inc(made, 1)
                gp.wait_ge(made, 2)
                nc.gpsimd.affine_select(out=ident[:, :], in_=ident[:, :], compare_op=ALU.not_equal, fill=1.0,
                                        base=0, pattern=[[-1, P]], channel_multiplier=1).then_inc(made, 1)
                with gp.Fori(0, G // 2) as gg:
                    for half in range(2):
                        gp.wait_ge(s_X, gg * 2 + (half + 1))
                        gp.dma_start(xs[:, half, :, :], xs_v[bass.ds(gg * 2 + half, 1)]
                                     .rearrange("a p t c -> (a p) t c")).then_inc(xs_in[half], 16)

            @block.tensor
            def _(te):
                te.sem_inc(s_X, 2)
                te.sem_inc(s_T, HEADS)
                te.sem_inc(s_O, HEADS)
                te.wait_ge(made, 3)
                te.wait_ge(con, 16 * 12)
                te.wait_ge(pre_dv, 1)
                for m in range(4):
                    for k in range(2):
                        nc.tensor.matmul(pQK[:, 0, m:m + 1], wqk[:, k, m, :], b1[:, k:k + 1], start=(k == 0),
                                         stop=(k == 1)).then_inc(pre_pe, 1)
                for k in range(2):
                    nc.tensor.matmul(pO[:, 0:C], b1w[:, k, :], wv[:, k, :], start=(k == 0), stop=False)
                nc.tensor.matmul(pO[:, 0:C], ones[:, :], brow[:, 0:C], start=False, stop=True).then_inc(pre_pe, 1)
                nc.tensor.matmul(pM[:, 0:C], ones[:, :], brow[:, C:2 * C], start=True, stop=True).then_inc(pre_pe, 1)
                te.wait_ge(pre_dv, 2)

                def rows_turned(gg, half, f):
                    te.wait_ge(xs_in[half], gg * 16 + 16)
                    te.wait_ge(s_xc, f + 1)
                    for t in range(QT):
                        for k in range(2):
                            mm = nc.tensor.transpose(pX[:, k, t * P:(t + 1) * P], xs[:, half, t, k * KC:(k + 1) * KC],
                                                     ident[:, :])
                    mm.then_inc(s_X, 1)

                def queries_keys(f):
                    te.wait_ge(s_xc, f + 2)
                    te.wait_ge(s_qk, f + 1)
                    for m in range(4):
                        for k in range(2):
                            mm = nc.tensor.matmul(pQK[:, m, :], wqkg[:, k, m, :], xT[:, k, :], start=(k == 0),
                                                  stop=(k == 1))
                    mm.then_inc(s_QK, 1)

                def values(f, first=False):
                    if not first:
                        te.wait_ge(s_y, f)
                    for t in range(QT):
                        for k in range(2):
                            mm = nc.tensor.matmul(mV[:, t, :], xT[:, k, t * P:(t + 1) * P], wvg[:, k, :],
                                                  start=(k == 0), stop=(k == 1))
                    mm.then_inc(s_V, 1)

                def scores(g, half, h):
                    te.wait_ge(s_E, head(g, h - 2))
                    lo = 64 * (h % 2)
                    for t in range(QT):
                        mm = nc.tensor.matmul(pS[:, h % 2, t, :], qk[lo:lo + HD, half, h // 2, t * P:(t + 1) * P],
                                              qk[lo:lo + HD, half, 2 + h // 2, :], start=True, stop=True)
                    mm.then_inc(s_S, 1)

                def turned(g, half, h):
                    te.wait_ge(s_E, head(g, h))
                    te.wait_ge(s_tc, head(g, h - 1))
                    for t in range(QT):
                        for k in range(QT):
                            mm = nc.tensor.transpose(pT[:, k, t * P:(t + 1) * P], e[:, h % 2, t, k * P:(k + 1) * P],
                                                     ident[:, :])
                    mm.then_inc(s_T, 1)

                def outputs(g, half, h):
                    te.wait_ge(s_tc, head(g, h))
                    if h == 0:
                        te.wait_ge(s_o, g + 1)
                        te.wait_ge(s_v, g + 2)
                    for t in range(QT):
                        for k in range(QT):
                            mm = nc.tensor.matmul(oV[:, t, h, :], eT[:, h % 2, k, t * P:(t + 1) * P],
                                                  V[:, half, k, h * HD:(h + 1) * HD], start=(k == 0), stop=(k == 1))
                    mm.then_inc(s_O, 1)

                def outputs_turned(g):
                    te.wait_ge(s_o, g + 2)
                    if not (isinstance(g, int) and g == G - 1):
                        te.wait_ge(s_v, g + 3)
                    for t in range(QT):
                        for k in range(2):
                            mm = nc.tensor.transpose(mT[:, k, t * P:(t + 1) * P], o[:, t, k * KC:(k + 1) * KC],
                                                     ident[:, :])
                    mm.then_inc(s_OT, 1)

                def project(g):
                    te.wait_ge(s_oc, g + 1)
                    for t in range(QT):
                        for k in range(2):
                            mm = nc.tensor.matmul(mV[:, t, :], oT[:, k, t * P:(t + 1) * P], wp[:, k, :],
                                                  start=(k == 0), stop=(k == 1))
                    mm.then_inc(s_Y, 1)

                def turn(gg, half, before, after):
                    g = gg * 2 + half
                    if after:
                        rows_turned(gg + half, 1 - half, g + 1)
                    te.wait_ge(s_qk, g + 2)
                    scores(g, half, 0)
                    scores(g, half, 1)
                    if before:
                        outputs_turned(g - 1)
                    if after:
                        queries_keys(g + 1)
                    if before:
                        project(g - 1)
                    turned(g, half, 0)
                    scores(g, half, 2)
                    turned(g, half, 1)
                    outputs(g, half, 0)
                    scores(g, half, 3)
                    outputs(g, half, 1)
                    turned(g, half, 2)
                    if after:
                        values(g + 1)
                    outputs(g, half, 2)
                    turned(g, half, 3)
                    outputs(g, half, 3)

                rows_turned(0, 0, 0)
                queries_keys(0)
                values(0, first=True)
                turn(0, 0, False, True)
                turn(0, 1, True, True)
                with te.Fori(1, G // 2 - 1) as gg:
                    turn(gg, 0, True, True)
                    turn(gg, 1, True, True)
                turn(G // 2 - 1, 0, True, True)
                turn(G // 2 - 1, 1, True, False)
                outputs_turned(G - 1)
                project(G - 1)

            @block.scalar
            def _(act):
                act.sem_inc(s_xc, 1)
                act.sem_inc(s_E, HEADS)
                act.sem_inc(s_tc, HEADS)

                def front(f):
                    act.wait_ge(s_X, f + 3)
                    act.wait_ge(s_V, f + 1)
                    nc.scalar.activation(xT[:, :, :], pX[:, :, :], ACT.Copy).then_inc(s_xc, 1)

                def expo(g, h):
                    act.wait_ge(s_m, g * HEADS + (h + 1))
                    act.wait_ge(s_T, head(g, h - 2))
                    for t in range(QT):
                        ins = nc.scalar.activation(e[:, h % 2, t, :], pS[:, h % 2, t, :], ACT.Exp,
                                                   bias=nmx[:, h % 2, t:t + 1], scale=SCALE,
                                                   accum_out=esum[:, t, h:h + 1])
                    ins.then_inc(s_E, 1)

                def copied(g, h):
                    act.wait_ge(s_T, head(g, h))
                    act.wait_ge(s_O, head(g, h - 2))
                    nc.scalar.activation(eT[:, h % 2, :, :], pT[:, :, :], ACT.Copy).then_inc(s_tc, 1)

                def turned_back(g):
                    act.wait_ge(s_OT, g + 1)
                    nc.scalar.activation(oT[:, :, :], mT, ACT.Copy).then_inc(s_oc, 1)

                def turn(g, before, after):
                    if after:
                        front(g + 1)
                    expo(g, 0)
                    if before:
                        turned_back(g - 1)
                    expo(g, 1)
                    copied(g, 0)
                    expo(g, 2)
                    copied(g, 1)
                    expo(g, 3)
                    copied(g, 2)
                    copied(g, 3)

                front(0)
                turn(0, False, True)
                with act.Fori(1, G - 1) as g:
                    turn(g, True, True)
                turn(G - 1, True, False)
                turned_back(G - 1)

            @block.vector
            def _(ve):
                link = Link(ve, dv)
                ve.sem_inc(s_V, 1)
                nc.vector.memset(wqk[:, :, :, :], 0.0).then_inc(cleared, 1)
                nc.vector.memset(bqk0[:, :], 0.0).then_inc(cleared, 1)
                ve.wait_ge(con, 16 * 12)
                nc.vector.tensor_copy(b1w[:, :, :], b1[:, :].unsqueeze(2).to_broadcast([KC, 2, P])).then_inc(pre_dv, 1)
                for k in range(2):
                    nc.vector.tensor_scalar(wqkg[:, k, :, :], wqk[:, k, :, :], g1[:, k:k + 1], None, ALU.mult)
                    nc.vector.tensor_scalar(wvg[:, k, :], wv[:, k, :], g1[:, k:k + 1], None, ALU.mult)
                ve.wait_ge(pre_pe, 10)
                nc.vector.tensor_tensor(bqk[:, :], pQK[:, 0, 0:4], bqk0[:, :], ALU.add)
                nc.vector.tensor_copy(bv[:, :], pO[:, 0:C])
                link(nc.vector.tensor_copy(bp[:, :], pM[:, 0:C]))
                ve.sem_inc(pre_dv, 1)
                ve.sem_inc(s_qk, 1)
                ve.sem_inc(s_v, 1)
                ve.sem_inc(s_o, 1)
                ve.sem_inc(s_y, 1)

                def queries_keys(f, half):
                    ve.wait_ge(s_QK, f + 1)
                    nc.vector.tensor_tensor(qk[:, half, :, :], pQK[:, :, :],
                                            bqk[:, :].unsqueeze(2).to_broadcast([P, 4, GS]), ALU.add).then_inc(s_qk, 1)

                def values(f, half):
                    ve.wait_ge(s_V, f + 2)
                    nc.vector.tensor_tensor(V[:, half, :, :], mV, bv[:, :].unsqueeze(1).to_broadcast([P, QT, C]),
                                            ALU.add).then_inc(s_v, 1)

                def maxima(g, h):
                    ve.wait_ge(s_S, g * HEADS + (h + 1))
                    link(nc.vector.tensor_reduce(mxs[:, h % 2, :], pS[:, h % 2, :, :], AX.X, ALU.max))
                    nc.vector.tensor_scalar(nmx[:, h % 2, :], mxs[:, h % 2, :], -SCALE, None, ALU.mult).then_inc(s_m, 1)

                def projected(g):
                    ve.wait_ge(s_Y, g + 1)
                    ve.wait_ge(o_y, g * 16 + 16)
                    nc.vector.tensor_tensor(y[:, :, :], mV, bp[:, :].unsqueeze(1).to_broadcast([P, QT, C]),
                                            ALU.add).then_inc(s_y, 1)

                def turn(gg, half, before, after):
                    g = gg * 2 + half
                    link.base, link.n = g * 5 + 1, 0
                    maxima(g, 0)
                    maxima(g, 1)
                    if after:
                        queries_keys(g + 1, 1 - half)
                    if before:
                        projected(g - 1)
                    maxima(g, 2)
                    maxima(g, 3)
                    if after:
                        values(g + 1, 1 - half)
                    ve.wait_ge(s_E, head(g, 3))
                    link(nc.vector.reciprocal(erec[:, :, :], esum[:, :, :]))
                    ve.wait_ge(s_O, head(g, 3))
                    nc.vector.tensor_tensor(o[:, :, :].rearrange("p t (h e) -> p t h e", h=HEADS), oV,
                                            erec[:, :, :].unsqueeze(3).to_broadcast([P, QT, HEADS, HD]),
                                            ALU.mult).then_inc(s_o, 1)

                queries_keys(0, 0)
                values(0, 0)
                turn(0, 0, False, True)
                turn(0, 1, True, True)
                with ve.Fori(1, G // 2 - 1) as gg:
                    turn(gg, 0, True, True)
                    turn(gg, 1, True, True)
                turn(G // 2 - 1, 0, True, True)
                turn(G // 2 - 1, 1, True, False)
                projected(G - 1)


ROWS = 16
STRIPS = B * H // ROWS
HROWS = ROWS + 2 * PADY
WP = W + 2 * PADY
CH = HID // P
SN = ROWS * W
FN = 4 * W
GR = HROWS // 4
CB = 64
ALL_TAPS = [(y, x) for y in range(KS) for x in range(KS)]
PE_SHARE = [6, 6, 9, 9, 8, 8]
HN = SN // 2


def phase_ffn(nc, sems, a, d):
    with ExitStack() as mem:
        def sb(name, shape, dt=F32):
            return mem.enter_context(nc.sbuf_tensor("f_" + name, shape, dt))

        def ps(name, shape, dt=F32):
            return mem.enter_context(nc.psum_tensor("f_" + name, shape, dt))

        def sem(name):
            return sems.new("f_" + name)

        ident = sb("ident", [P, P])
        ones = sb("ones", [1, P])
        g2 = sb("g2", [KC, 2])
        b2 = sb("b2", [KC, 2])
        w1 = sb("w1", [KC + 1, 2, HID])
        dww = sb("dww", [P, CH, KS * KS])
        dwb = sb("dwb", [P, CH])
        diag = sb("diag", [P, sum(PE_SHARE), P])
        w2 = sb("w2", [P, CH, C])
        w2t = sb("w2t", [TDF + 1, C])
        g3 = sb("g3", [P, C])
        b3 = sb("b3", [P, C])
        wc = sb("wc", [KC, 2, CB])
        wcr = sb("wcr", [CB, C])
        bc = sb("bc", [CB, 1])
        pos = sb("pos", [P, B * N // P], I32)
        idx = sb("idx", [P, ROWS], I32)

        xt = sb("xt", [KC + 1, 2, HROWS * W])
        h = sb("h", [P, 3, HROWS, WP])
        g = sb("g", [P, 2, SN])
        hs = sb("hs", [P, CH, SN])
        tds = sb("tds", [TDF + 1, SN])
        F = sb("F", [P, ROWS, C])
        brow = F[0:1, 0:HID // C, :].rearrange("a r c -> a (r c)")
        st6 = sb("st6", [P, ROWS, 6])
        mv = sb("mv", [P, ROWS, 2])
        dev = sb("dev", [P, ROWS])
        nmu = sb("nmu", [P, ROWS])
        aca = sb("aca", [P, ROWS, C])
        x1 = sb("x1", [KC, 2, SN // 2])
        res = sb("res", [KC, 2, SN // 2])
        xc = sb("xc", [CB, 2, FN])

        p1 = ps("p1", [P, 2, FN])
        pC = ps("pC", [P, 2, HN])
        p2 = ps("p2", [P, 2, 512])

        made, con, pre_dv, pre_pe, cleared = (sem(n) for n in ("made", "con", "pre_dv", "pre_pe", "cleared"))
        dv = sem("dv")
        marks = sem("marks")
        xt_in = sem("xt_in")
        tds_in = sem("tds_in")
        res_in = sem("res_in")
        aca_in = sem("aca_in")
        s_fc1 = sem("s_fc1")
        s_g = sem("s_g")
        s_tap = sem("s_tap")
        s_acc = sem("s_acc")
        s_g2 = sem("s_g2")
        s_add = sem("s_add")
        s_p2 = sem("s_p2")
        s_p2f = sem("s_p2f")
        s_st = sem("s_st")
        s_dev = sem("s_dev")
        s_rs = sem("s_rs")
        s_n = sem("s_n")
        s_ln = sem("s_ln")
        s_x1c = sem("s_x1c")
        s_x1 = sem("s_x1")
        o_xc = [sem(f"o_xc{k}") for k in range(2)]
        o_x1 = sem("o_x1")
        idx_set = sem("idx_set")
        s_lg = sem("s_lg")

        CON = 16
        xt_v = d.xt.rearrange("b c n -> (b c) n")
        PER_IMAGE = H // ROWS
        USES = 20

        def split(s):
            return (s // PER_IMAGE, s % PER_IMAGE)

        with nc.Block() as block:
            @block.sync
            def _(sp):
                def cin(dst, src):
                    sp.dma_start(dst, src).then_inc(con, 16)

                sp.wait_ge(cleared, 1)
                with nc.allow_non_contiguous_dma("small constants"):
                    cin(hs[0:KC, 0:2, 0:HID], a["L0_conv_fc1_w"].rearrange("(k p) n -> p k n", k=2))
                    cin(g2[:, :], a["L0_conv_g2"].rearrange("(k p) -> p k", k=2))
                    cin(b2[:, :], a["L0_conv_b2"].rearrange("(k p) -> p k", k=2))
                    cin(brow, a["L0_conv_fc1_b"].rearrange("(a n) -> a n", a=1))
                    cin(dww[:, :, :], a["L0_conv_dw_w"][0:HID].rearrange("(c p) o y x -> p c (o y x)", p=P))
                    cin(dwb[:, :], a["L0_conv_dw_b"][0:HID].rearrange("(c p) -> p c", p=P))
                    cin(w2[:, :, :], a["L0_conv_fc2_w"][0:HID].rearrange("(c p) n -> p c n", p=P))
                    cin(w2t[0:TDF, :], a["L0_conv_fc2_w"][HID:HID + TDF])
                    cin(w2t[TDF:TDF + 1, :], a["L0_conv_fc2_b"].rearrange("(a n) -> a n", a=1))
                    cin(g3[:, :], a["L0_conv_g3"].rearrange("(a n) -> a n", a=1).broadcast_to([P, C]))
                    cin(b3[:, :], a["L0_conv_b3"].rearrange("(a n) -> a n", a=1).broadcast_to([P, C]))
                    cin(wcr[:, :], a["L1_conv_w1"])
                    cin(bc[:, :], a["L1_conv_b1"].rearrange("(c o) -> c o", o=1))
                    cin(pos[:, :], d.pos)

                def load_xt(b, j, s):
                    sp.dma_start(xt[0:KC, 0, :], d.xt[bass.ds(b, 1), 0:KC, bass.ds(j * SN, HROWS * W)]
                                 .rearrange("b c n -> (b c) n")).then_inc(xt_in, 16)
                    sp.dma_start(xt[:, 1, :], d.xt[bass.ds(b, 1), KC:C + 1, bass.ds(j * SN, HROWS * W)]
                                 .rearrange("b c n -> (b c) n")).then_inc(xt_in, 16)

                def tail_loads(b, j, t):
                    if not isinstance(t, int) or t:
                        sp.wait_ge(s_p2, t * USES - (USES - 8))
                    sp.dma_start(tds[0:TDF, :], d.tdc[bass.ds(b, 1), :, bass.ds(j * SN, SN)]
                                 .rearrange("b c n -> (b c) n")).then_inc(tds_in, 16)

                def load_res(b, j, t, half):
                    if not isinstance(t, int) or t or half:
                        sp.wait_ge(s_x1, t * 2 + half)
                    sp.dma_start(res[:, :, :], d.res[bass.ds(b, 1), :, bass.ds(j * SN + half * (SN // 2), SN // 2)]
                                 .rearrange("b (k p) n -> (b p) k n", k=2)).then_inc(res_in, 16)

                def tail_stores(b, j, t, half):
                    sp.wait_ge(s_x1, t * 2 + (half + 1))
                    sp.dma_start(d.x1[bass.ds(b, 1), :, bass.ds(j * SN + half * (SN // 2), SN // 2)]
                                 .rearrange("b (k p) n -> (b p) k n", k=2), x1[:, :, :]).then_inc(o_x1, 16)
                    if half == 0:
                        load_res(b, j, t, 1)
                    for q in range(2):
                        sp.wait_ge(s_p2f, t * USES + (8 + 6 * half + 4 + q + 3))
                        sp.dma_start(d.xc[bass.ds(b, 1), :, bass.ds(j * SN + (2 * half + q) * FN, FN)]
                                     .rearrange("b c n -> (b c) n"), xc[:, q, :]).then_inc(o_xc[q], 16)

                sp.sem_inc(o_x1, 16)
                for k in range(2):
                    sp.sem_inc(o_xc[k], 16)
                load_xt(0, 0, 0)
                sp.wait_ge(s_fc1, CH * GR)
                load_xt(0, 1, 1)

                def turn(t, more):
                    bt, jt = (t // PER_IMAGE, t % PER_IMAGE)
                    tail_loads(bt, jt, t)
                    load_res(bt, jt, t, 0)
                    if more:
                        sp.wait_ge(s_fc1, t * (CH * GR) + 2 * CH * GR)
                        load_xt((t + 2) // PER_IMAGE, (t + 2) % PER_IMAGE, None)
                    tail_stores(bt, jt, t, 0)
                    tail_stores(bt, jt, t, 1)

                turn(0, True)
                with sp.Fori(1, STRIPS - 2) as t:
                    turn(t, True)
                for t in (STRIPS - 2, STRIPS - 1):
                    turn(t, False)
                sp.wait_ge(o_x1, 32 * STRIPS + 16)
                for k in range(2):
                    sp.wait_ge(o_xc[k], 16 * 2 * STRIPS + 16)

            @block.gpsimd
            def _(gp):
                nc.gpsimd.memset(ident[:, :], 0.0).then_inc(made, 1)
                nc.gpsimd.memset(ones[:, :], 1.0).then_inc(made, 1)
                gp.wait_ge(made, 2)
                nc.gpsimd.affine_select(out=ident[:, :], in_=ident[:, :], compare_op=ALU.not_equal, fill=1.0,
                                        base=0, pattern=[[-1, P]], channel_multiplier=1).then_inc(made, 1)
                nc.gpsimd.memset(tds[:, :], 1.0).then_inc(cleared, 1)
                gp.sem_inc(s_add, 2)
                gp.wait_ge(con, 16 * 14)

                def add(s, c):
                    n = s * CH + c
                    gp.wait_ge(s_g2, n * 2 + 4)
                    if not isinstance(s, int) or s >= 1:
                        gp.wait_ge(s_p2, (s - 1) * USES + 8)
                    view = g[:, c % 2, :].rearrange("p (y x) -> p y x", x=W)
                    nc.gpsimd.tensor_tensor(hs[:, c, :].rearrange("p (y x) -> p y x", x=W), view,
                                            h[:, c % 3, PADY:PADY + ROWS, PADY:PADY + W], ALU.add).then_inc(s_add, 1)

                def gathers(t, lo, hi):
                    if lo == 0:
                        nc.gpsimd.tensor_copy(idx[:, :], at(pos, t * ROWS, ROWS)).then_inc(idx_set, 1)
                        gp.wait_ge(idx_set, t + 1)
                        gp.sem_inc(marks, 1)
                    for r in range(lo, hi):
                        gp.indirect_dma_start(aca[:, r, :], None, d.aca[:, :],
                                              bass.IndirectOffsetOnAxis(ap=idx[:, r:r + 1], axis=0)).then_inc(aca_in, 16)

                def finish(t):
                    gp.wait_ge(s_n, t + 1)
                    nc.gpsimd.tensor_tensor(F[:, :, :], F[:, :, :], g3[:, :].unsqueeze(1).to_broadcast([P, ROWS, C]),
                                            ALU.mult).then_inc(s_lg, 1)
                    gp.wait_ge(s_lg, t * 2 + 1)
                    nc.gpsimd.tensor_tensor(F[:, :, :], F[:, :, :], b3[:, :].unsqueeze(1).to_broadcast([P, ROWS, C]),
                                            ALU.add).then_inc(s_lg, 1)
                    gp.wait_ge(s_lg, t * 2 + 2)
                    gp.wait_ge(aca_in, t * (16 * ROWS) + 16 * ROWS)
                    nc.gpsimd.tensor_tensor(F[:, :, :], F[:, :, :], aca[:, :, :], ALU.add).then_inc(s_ln, 1)

                def add_res(t, half):
                    gp.wait_ge(res_in, t * 32 + 16 * (half + 1))
                    gp.wait_ge(s_x1c, t * 8 + 4 * (half + 1))
                    nc.gpsimd.tensor_tensor(x1[:, :, :], x1[:, :, :], res[:, :, :], ALU.add).then_inc(s_x1, 1)

                def turn(s, tail):
                    t = s - 1
                    if tail:
                        if not isinstance(s, int) or s > 1:
                            gp.wait_ge(s_ln, t)
                        gathers(t, 0, 8)
                    add(s, 0)
                    if tail:
                        gathers(t, 8, 16)
                    add(s, 1)
                    if tail:
                        finish(t)
                    add(s, 2)
                    add(s, 3)
                    if tail:
                        add_res(t, 0)
                    add(s, 4)
                    if tail:
                        add_res(t, 1)
                    add(s, 5)

                turn(0, False)
                turn(1, True)
                with gp.Fori(2, STRIPS) as s:
                    turn(s, True)
                gp.wait_ge(s_ln, STRIPS - 1)
                gathers(STRIPS - 1, 0, ROWS)
                finish(STRIPS - 1)
                add_res(STRIPS - 1, 0)
                add_res(STRIPS - 1, 1)

            @block.tensor
            def _(te):
                te.wait_ge(made, 3)
                te.wait_ge(con, 16 * 14)
                for k in range(2):
                    nc.tensor.transpose(pC[0:KC, 0, k * CB:(k + 1) * CB], wcr[:, k * KC:(k + 1) * KC],
                                        ident[0:CB, 0:CB]).then_inc(pre_pe, 1)
                for o in range(2):
                    for k in range(2):
                        nc.tensor.matmul(pC[0:1, 1, 512 * o:512 * o + HID // 2], b2[:, k:k + 1],
                                         hs[0:KC, k, o * (HID // 2):(o + 1) * (HID // 2)], start=(k == 0),
                                         stop=(k == 1)).then_inc(pre_pe, 1)
                te.wait_ge(pre_dv, 1)

                def fc1(s, c):
                    if c == 0:
                        te.wait_ge(xt_in, s * 32 + 32)
                    for j in range(GR):
                        m = c * GR + j
                        te.wait_ge(s_g, s * (CH * GR) + (m + 1))
                        for k in range(2):
                            kk = KC + k
                            mm = nc.tensor.matmul(p1[:, m % 2, :], w1[0:kk, k, c * P:(c + 1) * P],
                                                  xt[0:kk, k, j * FN:(j + 1) * FN], start=(k == 0), stop=(k == 1))
                        mm.then_inc(s_fc1, 1)

                def taps(s, c, half):
                    n = s * CH + c
                    te.wait_ge(s_g, s * (CH * GR) + ((c + 1) * GR + 2))
                    te.wait_ge(s_g2, n * 2 + (half + 1))
                    at0 = sum(PE_SHARE[:c])
                    for i, (y, x) in enumerate(ALL_TAPS[:PE_SHARE[c]]):
                        for q in range(2):
                            row = 8 * half + 4 * q + y
                            mm = nc.tensor.matmul(pC[:, half, q * FN:(q + 1) * FN], diag[:, at0 + i, :],
                                                  h[:, c % 3, row:row + 4, x:x + W], start=(i == 0),
                                                  stop=(i == PE_SHARE[c] - 1))
                    mm.then_inc(s_tap, 1)

                def use(t, n):
                    te.wait_ge(s_p2f, t * USES + (n + 1))

                def fc2(t, half):
                    te.wait_ge(s_add, t * CH + CH + 2)
                    te.wait_ge(tds_in, t * 16 + 16)
                    for k in range(4 * half, 4 * half + 4):
                        use(t, k)
                        for r in range(2):
                            row = 2 * k + r
                            dst = p2[:, k % 2, r * C:(r + 1) * C]
                            for c in range(CH):
                                nc.tensor.matmul(dst, hs[:, c, row * W:(row + 1) * W], w2[:, c, :], start=(c == 0), stop=False)
                            mm = nc.tensor.matmul(dst, tds[:, row * W:(row + 1) * W], w2t[:, :], start=False, stop=True)
                        mm.then_inc(s_p2, 1)

                def turned(t, half):
                    te.wait_ge(s_ln, t + 1)
                    for k in range(4):
                        use(t, 8 + 6 * half + k)
                        q, kt = 2 * half + k // 2, k % 2
                        for r in range(4):
                            mm = nc.tensor.transpose(p2[0:KC, k % 2, r * W:(r + 1) * W],
                                                     F[:, 4 * q + r, kt * KC:(kt + 1) * KC], ident[:, :])
                        mm.then_inc(s_p2, 1)

                def first(t, half):
                    te.wait_ge(s_x1, t * 2 + (half + 1))
                    for q in range(2):
                        use(t, 8 + 6 * half + 4 + q)
                        for k in range(2):
                            mm = nc.tensor.matmul(p2[0:CB, q, :], wc[:, k, :], x1[:, k, q * FN:(q + 1) * FN],
                                                  start=(k == 0), stop=(k == 1))
                        mm.then_inc(s_p2, 1)

                def turn(s, tail, more):
                    t = s - 1
                    taps(s, 0, 1)
                    fc1(s, 2)
                    if tail:
                        fc2(t, 0)
                    taps(s, 1, 0)
                    taps(s, 1, 1)
                    if tail:
                        fc2(t, 1)
                    taps(s, 2, 0)
                    fc1(s, 3)
                    taps(s, 2, 1)
                    fc1(s, 4)
                    taps(s, 3, 0)
                    taps(s, 3, 1)
                    fc1(s, 5)
                    taps(s, 4, 0)
                    taps(s, 4, 1)
                    if more:
                        fc1(s + 1, 0)
                    if tail:
                        turned(t, 0)
                    taps(s, 5, 0)
                    taps(s, 5, 1)
                    if tail:
                        first(t, 0)
                        turned(t, 1)
                    if more:
                        fc1(s + 1, 1)
                    if tail:
                        first(t, 1)
                    if more:
                        taps(s + 1, 0, 0)

                fc1(0, 0)
                fc1(0, 1)
                taps(0, 0, 0)
                turn(0, False, True)
                with te.Fori(1, STRIPS - 1) as s:
                    turn(s, True, True)
                turn(STRIPS - 1, True, False)
                for half in range(2):
                    fc2(STRIPS - 1, half)
                for half in range(2):
                    turned(STRIPS - 1, half)
                    first(STRIPS - 1, half)

            @block.scalar
            def _(act):
                act.sem_inc(s_g, 2)
                act.sem_inc(s_g2, 2)
                act.sem_inc(s_p2f, 2)

                def gelu1(s, c):
                    act.wait_ge(s_add, s * CH + c)
                    for j in range(GR):
                        m = c * GR + j
                        act.wait_ge(s_fc1, s * (CH * GR) + (m + 1))
                        nc.scalar.activation(h[:, c % 3, 4 * j:4 * j + 4, PADY:PADY + W],
                                             p1[:, m % 2, :].rearrange("p (y x) -> p y x", x=W),
                                             ACT.Gelu).then_inc(s_g, 1)

                def gelu2(s, c, half):
                    act.wait_ge(s_acc, s * (CH * 2) + (2 * c + half + 1))
                    act.wait_ge(s_add, s * CH + (c + 1))
                    nc.scalar.activation(g[:, c % 2, half * HN:(half + 1) * HN], pC[:, half, :], ACT.Gelu,
                                         bias=dwb[:, c:c + 1]).then_inc(s_g2, 1)

                def evac(t, half):
                    for k in range(4 * half, 4 * half + 4):
                        act.wait_ge(s_p2, t * USES + (k + 1))
                        nc.scalar.activation(F[:, 2 * k:2 * k + 2, :], p2[:, k % 2, 0:2 * C]
                                             .rearrange("p (r c) -> p r c", r=2), ACT.Copy).then_inc(s_p2f, 1)

                def deviate(t):
                    act.wait_ge(s_st, t + 1)
                    nc.scalar.activation(dev[:, :], dev[:, :], ACT.Sqrt).then_inc(s_dev, 1)

                def normalise(t):
                    act.wait_ge(s_rs, t + 1)
                    for r in range(ROWS):
                        ins = nc.scalar.activation(F[:, r, :], F[:, r, :], ACT.Identity, bias=nmu[:, r:r + 1],
                                                   scale=dev[:, r:r + 1])
                    ins.then_inc(s_n, 1)

                def turned(t, half):
                    act.wait_ge(o_x1, t * 32 + 16 * (half + 1))
                    for k in range(4):
                        q, kt = k // 2, k % 2
                        act.wait_ge(s_p2, t * USES + (8 + 6 * half + k + 1))
                        nc.scalar.activation(x1[:, kt, q * FN:(q + 1) * FN], p2[0:KC, k % 2, :], ACT.Copy)\
                            .then_inc(s_x1c, 1)
                        act.wait_ge(s_x1c, t * 8 + (4 * half + k + 1))
                        act.sem_inc(s_p2f, 1)

                def first(t, half):
                    for q in range(2):
                        act.wait_ge(s_p2, t * USES + (8 + 6 * half + 4 + q + 1))
                        act.wait_ge(o_xc[q], t * 32 + 16 * (half + 1))
                        nc.scalar.activation(xc[:, q, :], p2[0:CB, q, :], ACT.Identity,
                                             bias=bc[:, 0:1]).then_inc(s_p2f, 1)

                def turn(s, tail, more):
                    t = s - 1
                    if tail:
                        gelu2(t, 5, 1)
                    gelu1(s, 2)
                    if tail:
                        evac(t, 0)
                    gelu2(s, 0, 0)
                    gelu2(s, 0, 1)
                    if tail:
                        evac(t, 1)
                    gelu2(s, 1, 0)
                    gelu1(s, 3)
                    gelu2(s, 1, 1)
                    if tail:
                        deviate(t)
                    gelu1(s, 4)
                    gelu2(s, 2, 0)
                    if tail:
                        normalise(t)
                    gelu2(s, 2, 1)
                    gelu1(s, 5)
                    gelu2(s, 3, 0)
                    gelu2(s, 3, 1)
                    if more:
                        gelu1(s + 1, 0)
                    if tail:
                        turned(t, 0)
                    gelu2(s, 4, 0)
                    gelu2(s, 4, 1)
                    if tail:
                        first(t, 0)
                        turned(t, 1)
                    if more:
                        gelu1(s + 1, 1)
                    if tail:
                        first(t, 1)
                    gelu2(s, 5, 0)

                gelu1(0, 0)
                gelu1(0, 1)
                turn(0, False, True)
                with act.Fori(1, STRIPS - 1) as s:
                    turn(s, True, True)
                turn(STRIPS - 1, True, False)
                t = STRIPS - 1
                gelu2(t, 5, 1)
                for half in range(2):
                    evac(t, half)
                deviate(t)
                normalise(t)
                for half in range(2):
                    turned(t, half)
                    first(t, half)

            @block.vector
            def _(ve):
                link = Link(ve, dv)
                for i in range(3):
                    nc.vector.memset(h[:, i, :, :], 0.0)
                ve.wait_ge(made, 3)
                ve.wait_ge(con, 16 * 14)
                for k in range(2):
                    nc.vector.tensor_scalar(w1[0:KC, k, :], hs[0:KC, k, 0:HID], g2[:, k:k + 1], None, ALU.mult)
                for c in range(CH):
                    for n in range(PE_SHARE[c]):
                        nc.vector.tensor_scalar(diag[:, sum(PE_SHARE[:c]) + n, :], ident[:, :], dww[:, c, n:n + 1],
                                                None, ALU.mult)
                ve.wait_ge(pre_pe, 6)
                nc.vector.tensor_copy(wc[:, :, :], pC[0:KC, 0, 0:2 * CB].rearrange("p (k n) -> p k n", k=2))
                for o in range(2):
                    link(nc.vector.tensor_tensor(w1[KC:KC + 1, 1, o * (HID // 2):(o + 1) * (HID // 2)],
                                                 pC[0:1, 1, 512 * o:512 * o + HID // 2],
                                                 brow[:, o * (HID // 2):(o + 1) * (HID // 2)], ALU.add))
                ve.sem_inc(pre_dv, 1)
                start = link.n
                LINKS = sum(2 * (KS * KS - n - 1) for n in PE_SHARE)
                per = LINKS + 4

                def chunk(s, c, half):
                    ve.wait_ge(s_tap, s * (CH * 2) + (2 * c + half + 1))
                    out = pC[:, half, :].rearrange("p (y x) -> p y x", x=W)
                    for n in range(PE_SHARE[c], KS * KS):
                        y, x = ALL_TAPS[n]
                        ins = nc.vector.scalar_tensor_tensor(out, h[:, c % 3, y + 8 * half:y + 8 * half + 8, x:x + W],
                                                             dww[:, c, n:n + 1], out, ALU.mult, ALU.add)
                        if n < KS * KS - 1:
                            link(ins)
                        else:
                            ins.then_inc(s_acc, 1)

                def stats(t):
                    ve.wait_ge(s_p2f, t * USES + 10)
                    ve.sem_inc(marks, 1)
                    for r in range(ROWS):
                        ins = nc.vector.bn_stats(st6[:, r, :], F[:, r, :])
                    link(ins)
                    ve.sem_inc(marks, 1)
                    for r in range(ROWS):
                        ins = nc.vector.bn_aggr(mv[:, r, :], st6[:, r, :])
                    link(ins)
                    nc.vector.tensor_scalar(dev[:, :], mv[:, :, 1], EPS, None, ALU.add).then_inc(s_st, 1)

                def scales(t):
                    ve.wait_ge(s_dev, t + 1)
                    link(nc.vector.reciprocal(dev[:, :], dev[:, :]))
                    link(nc.vector.tensor_scalar(nmu[:, :], mv[:, :, 0], -1.0, None, ALU.mult))
                    nc.vector.tensor_tensor(nmu[:, :], nmu[:, :], dev[:, :], ALU.mult).then_inc(s_rs, 1)

                def turn(s, tail):
                    link.base, link.n = (s - 1) * per + (start + LINKS) if tail else start, 0
                    for c in range(CH):
                        if tail and c == 2:
                            stats(s - 1)
                        chunk(s, c, 0)
                        if tail and c == 2:
                            scales(s - 1)
                        chunk(s, c, 1)
                    assert link.n == (per if tail else LINKS)

                turn(0, False)
                with ve.Fori(1, STRIPS) as s:
                    turn(s, True)
                link.base, link.n = (STRIPS - 1) * per + (start + LINKS), 0
                stats(STRIPS - 1)
                scales(STRIPS - 1)


WINDOWS = (4, 8, 12)
WB = len(WINDOWS)
PITCH = W + 2


def window(nw):
    step = H // nw
    return step, step + H % nw


def window_parts(t, nw):
    step, k = window(nw)
    parts = []
    for y0 in range(0, k, step):
        for x0 in range(0, k, step):
            v = t[:, y0:y0 + nw * step, x0:x0 + nw * step].rearrange("p (u y) (v x) -> p y x u v", u=nw, v=nw)
            parts.append((y0, min(step, k - y0), x0, min(step, k - x0), v))
    return parts


def phase_cut(nc, sems, a, d):
    with ExitStack() as mem:
        def sb(name, shape, dt=F32):
            return mem.enter_context(nc.sbuf_tensor("c_" + name, shape, dt))

        def sem(name):
            return sems.new("c_" + name)

        img = sb("img", [P, H + 2, PITCH])
        tile = sb("tile", [P, 2, max(window(n)[1] * n * n for n in WINDOWS)])
        img_in = sem("img_in")
        s_cut = [sem(f"s_cut{k}") for k in range(2)]
        stored = [sem(f"stored{k}") for k in range(2)]
        ROWS_OF = [(j, nw, part) for j, nw in enumerate(WINDOWS) for part in range(0, window(nw)[1], window(nw)[0])]

        def cut_row(eng, copy, half):
            eng.wait_ge(img_in, 32)
            done = 0
            for j, nw, y0 in ROWS_OF:
                parts = [p for p in window_parts(img, nw) if p[0] == y0]
                turns = parts[0][1] // 2
                with eng.Fori(0, turns) as i:
                    eng.wait_ge(stored[half], i * 16 + 16 * (done + 1))
                    for n, (_, _, x0, nx, v) in enumerate(parts):
                        src = v[:, bass.ds(i * 2 + half, 1), 0:nx].rearrange("p o x u v -> p (o x) u v")
                        dst = tile[:, half, x0 * nw * nw:(x0 + nx) * nw * nw].rearrange("p (x u v) -> p x u v", u=nw, v=nw)
                        ins = copy(dst, src)
                    ins.then_inc(s_cut[half], 1)
                done += turns

        with nc.Block() as block:
            @block.sync
            def _(sp):
                for b in range(B):
                    sp.dma_start(img[b * CB:(b + 1) * CB, 0:H, 0:W],
                                 d.xc[b].rearrange("c (y x) -> c y x", x=W)).then_inc(img_in, 16)
                for k in range(2):
                    sp.sem_inc(stored[k], 16)
                done = 0
                for j, nw, y0 in ROWS_OF:
                    k = window(nw)[1]
                    n = k * nw * nw
                    u = d.u[j].rearrange("b c n -> (b c) n")
                    turns = [p for p in window_parts(img, nw) if p[0] == y0][0][1] // 2
                    with sp.Fori(0, turns) as i:
                        for half in range(2):
                            sp.wait_ge(s_cut[half], i + (done + 1))
                            sp.dma_start(at(u, (i * 2 + (y0 + half)) * n, n), tile[:, half, 0:n]).then_inc(stored[half], 16)
                    done += turns
                for k in range(2):
                    sp.wait_ge(stored[k], 16 * done + 16)

            @block.vector
            def _(ve):
                cut_row(ve, nc.vector.tensor_copy, 0)

            @block.scalar
            def _(act):
                cut_row(act, lambda dst, src: nc.scalar.activation(dst, src, ACT.Copy), 1)


def phase_mix(nc, sems, a, d):
    with ExitStack() as mem:
        def sb(name, shape, dt=F32):
            return mem.enter_context(nc.sbuf_tensor("m_" + name, shape, dt))

        def ps(name, shape, dt=F32):
            return mem.enter_context(nc.psum_tensor("m_" + name, shape, dt))

        def sem(name):
            return sems.new("m_" + name)

        AT_ONCE = {4: 1, 8: 4, 12: 2}
        TAPS = (4, 3, 5, 1, 7, 0, 2, 6, 8)
        PE_TAPS = {4: 4, 8: 4, 12: 4}
        UB = 4
        BANK = 512
        SE = 8
        BIG = 1024
        ident = sb("ident", [P, P])
        w2r = sb("w2r", [P, P])
        w2 = sb("w2", [P, P])
        se1r = sb("se1r", [SE, P])
        se1 = sb("se1", [P, SE])
        se2r = sb("se2r", [P, SE])
        se2 = sb("se2", [SE, P])
        b2 = sb("b2", [P, 1])
        wp = sb("wp", [P, 9])
        bp = sb("bp", [P, 1])
        diag = sb("diag", [P, max(PE_TAPS.values()), P])
        u = sb("u", [P, UB, BIG])
        y = sb("y", [P, 2, BIG])
        acc = sb("acc", [P, 2, BIG])
        ysum = sb("ysum", [P, 2, 4])
        r = sb("r", [SE, 2, 4])
        sg = sb("sg", [P, 2, 4])
        pY = ps("pY", [P, BIG])
        pC = ps("pC", [P, 2, BIG])
        pE = ps("pE", [P, 512])
        pG = ps("pG", [P, 512])

        made, con, cleared, pre_pe, pre_dv = (sem(n) for n in ("made", "con", "cleared", "pre_pe", "pre_dv"))
        dv = sem("dv")
        u_in = [sem(f"u_in{k}") for k in range(UB)]
        s_Y = sem("s_Y")
        s_t = sem("s_t")
        s_y = sem("s_y")
        s_E = sem("s_E")
        s_r = sem("s_r")
        s_G = sem("s_G")
        s_sg = sem("s_sg")
        s_z = sem("s_z")
        s_a = sem("s_a")
        a_out = [sem(f"a_out{k}") for k in range(2)]

        def chunks(nw):
            return nw * nw // AT_ONCE[nw]

        def each():
            done = 0
            for j, nw in enumerate(WINDOWS):
                yield j, nw, AT_ONCE[nw], window(nw)[1] ** 2, done
                done += chunks(nw)

        TOTAL = sum(chunks(nw) for nw in WINDOWS)

        def by_window(t, nw):
            k, nb = window(nw)[1], AT_ONCE[nw]
            return t.rearrange("p (w n) -> p w n", w=nb)[:, :, 0:k * k]

        def shifted(k, t, lo=0, hi=None):
            dy, dx = t // 3 - 1, t % 3 - 1
            hi = k if hi is None else hi
            ys, xs = slice(max(lo, -dy), min(hi, k - dy)), slice(max(0, -dx), k - max(0, dx))
            return ys, xs, slice(ys.start + dy, ys.stop + dy), slice(xs.start + dx, xs.stop + dx)

        with nc.Block() as block:
            @block.gpsimd
            def _(gp):
                nc.gpsimd.memset(ident[:, :], 0.0).then_inc(made, 1)
                gp.wait_ge(made, 1)
                nc.gpsimd.affine_select(out=ident[:, :], in_=ident[:, :], compare_op=ALU.not_equal, fill=1.0,
                                        base=0, pattern=[[-1, P]], channel_multiplier=1).then_inc(made, 1)
                for j, nw, nb, kk, done in each():
                    src = [d.u[j][b].rearrange("c n -> (c n)").rearrange("(w c n) -> c w n", c=CB, n=kk) for b in range(B)]
                    with gp.Fori(0, chunks(nw) // UB) as ii:
                        for n in range(UB):
                            gp.wait_ge(s_a, ii * UB + (done + n + 1))
                            for b in range(B):
                                gp.dma_start(by_window(u[b * CB:(b + 1) * CB, n, :], nw),
                                             src[b][:, bass.ds((ii * UB + n) * nb, nb), :]).then_inc(u_in[n], 16)

            @block.sync
            def _(sp):
                def cin(dst, src):
                    sp.dma_start(dst, src).then_inc(con, 16)

                sp.wait_ge(cleared, 3)
                with nc.allow_non_contiguous_dma("small constants"):
                    for b in range(B):
                        s = slice(b * CB, (b + 1) * CB)
                        e = slice(b * SE // 2, (b + 1) * SE // 2)
                        cin(w2r[s, s], a["L1_conv_w2"])
                        cin(se1r[e, s], a["L1_conv_wse1"])
                        cin(se2r[s, e], a["L1_conv_wse2"])
                        cin(b2[s, :], a["L1_conv_b2"].rearrange("(c o) -> c o", o=1))
                        cin(bp[s, :], a["L1_conv_bpos"].rearrange("(c o) -> c o", o=1))
                        cin(wp[s, :], a["L1_conv_wpos"].rearrange("c o y x -> c (o y x)"))
                for k in range(2):
                    sp.sem_inc(a_out[k], 32)
                for j, nw, nb, kk, done in each():
                    dst = [d.v[j][b].rearrange("c n -> (c n)").rearrange("(w c n) -> c w n", c=CB, n=kk) for b in range(B)]
                    with sp.Fori(0, chunks(nw) // 2) as ii:
                        for half in range(2):
                            sp.wait_ge(s_a, ii * 2 + (done + half + UB + 1))
                            for b in range(B):
                                sp.dma_start(dst[b][:, bass.ds((ii * 2 + half) * nb, nb), :],
                                             by_window(acc[b * CB:(b + 1) * CB, half, :], nw)).then_inc(a_out[half], 16)
                for k in range(2):
                    sp.wait_ge(a_out[k], 16 * TOTAL + 32)

            @block.tensor
            def _(te):
                te.wait_ge(made, 2)
                te.wait_ge(con, 16 * 12)
                nc.tensor.transpose(pE[:, 0:P], w2r[:, :], ident[:, :]).then_inc(pre_pe, 1)
                nc.tensor.transpose(pE[:, P:P + SE], se1r[:, :], ident[0:SE, 0:SE]).then_inc(pre_pe, 1)
                nc.tensor.transpose(pG[0:SE, 0:P], se2r[:, :], ident[:, :]).then_inc(pre_pe, 1)
                te.wait_ge(pre_dv, 1)

                def taps(n, half, nw, bank):
                    k, per = window(nw)[1], BANK * AT_ONCE[nw] // BIG
                    uw, cw = by_window(u[:, n, :], nw), by_window(pC[:, half, :], nw)
                    if per:
                        ws, lo, hi = slice(bank * per, (bank + 1) * per), 0, k
                    else:
                        ws, lo, hi = slice(0, 1), bank * k // 2, (bank + 1) * k // 2
                    uw = uw[:, ws].rearrange("p w (y x) -> p w y x", x=k)
                    cw = cw[:, ws].rearrange("p w (y x) -> p w y x", x=k)
                    for m, t in enumerate(TAPS[:PE_TAPS[nw]]):
                        ys, xs, yi, xi = shifted(k, t, lo, hi)
                        mm = nc.tensor.matmul(cw[:, :, ys, xs], diag[:, m, :], uw[:, :, yi, xi], start=(m == 0),
                                              stop=(m == PE_TAPS[nw] - 1))
                    return mm

                for j, nw, nb, kk, done in each():
                    cols = [(q * BANK, BANK) for q in range(2)] if nb != 2 else [(q * BANK, kk) for q in range(2)]
                    with te.Fori(0, chunks(nw) // UB) as ii:
                        for n in range(UB):
                            half = n % 2
                            i = ii * UB + (done + n)
                            te.wait_ge(u_in[n], ii * 32 + (32 + 32 * (done // UB)))
                            te.wait_ge(s_y, i + 1)
                            for lo, size in cols:
                                mm = nc.tensor.matmul(pY[:, lo:lo + size], w2[:, :], u[:, n, lo:lo + size],
                                                      start=True, stop=True)
                            mm.then_inc(s_Y, 1)
                            te.wait_ge(s_a, i + (UB - 1))
                            taps(n, half, nw, 0)
                            te.wait_ge(s_y, i + 2)
                            nc.tensor.matmul(pE[0:SE, 0:nb], se1[:, :], ysum[:, half, 0:nb], start=True,
                                             stop=True).then_inc(s_E, 1)
                            taps(n, half, nw, 1).then_inc(s_t, 1)
                            te.wait_ge(s_r, i + 1)
                            nc.tensor.matmul(pG[:, 0:nb], se2[:, :], r[:, half, 0:nb], start=True,
                                             stop=True).then_inc(s_G, 1)

            @block.scalar
            def _(act):
                act.sem_inc(s_y, 1)
                for j, nw, nb, kk, done in each():
                    with act.Fori(0, chunks(nw) // 2) as ii:
                        for half in range(2):
                            i = ii * 2 + (done + half)
                            yw, pw = by_window(y[:, half, :], nw), by_window(pY[:, :], nw)
                            act.wait_ge(s_Y, i + 1)
                            act.wait_ge(s_a, i + (UB - 1))
                            for w in range(nb):
                                ins = nc.scalar.activation(yw[:, w], pw[:, w], ACT.Identity, bias=b2[:, 0:1],
                                                           accum_out=ysum[:, half, w:w + 1])
                            ins.then_inc(s_y, 1)
                            act.wait_ge(s_E, i + 1)
                            nc.scalar.activation(r[:, half, 0:nb], pE[0:SE, 0:nb], ACT.Relu,
                                                 scale=1.0 / kk).then_inc(s_r, 1)
                            act.wait_ge(s_G, i + 1)
                            nc.scalar.activation(sg[:, half, 0:nb], pG[:, 0:nb], ACT.Sigmoid).then_inc(s_sg, 1)
                            act.wait_ge(s_sg, i + 1)
                            for w in range(nb):
                                ins = nc.scalar.activation(yw[:, w], yw[:, w], ACT.Identity, bias=bp[:, 0:1],
                                                           scale=sg[:, half, w:w + 1])
                            ins.then_inc(s_z, 1)

            @block.vector
            def _(ve):
                link = Link(ve, dv)
                nc.vector.memset(w2r[:, :], 0.0).then_inc(cleared, 1)
                nc.vector.memset(se1r[:, :], 0.0).then_inc(cleared, 1)
                nc.vector.memset(se2r[:, :], 0.0).then_inc(cleared, 1)
                ve.sem_inc(s_a, UB)
                ve.wait_ge(pre_pe, 3)
                link(nc.vector.tensor_copy(w2[:, :], pE[:, 0:P]))
                link(nc.vector.tensor_copy(se1[:, :], pE[:, P:P + SE]))
                link(nc.vector.tensor_copy(se2[:, :], pG[0:SE, 0:P]))
                for m in range(max(PE_TAPS.values())):
                    t = TAPS[m]
                    link(nc.vector.tensor_scalar(diag[:, m, :], ident[:, :], wp[:, t:t + 1], None, ALU.mult))
                ve.sem_inc(pre_dv, 1)
                start = link.n
                for j, nw, nb, kk, done in each():
                    k = window(nw)[1]
                    per = len(TAPS) - PE_TAPS[nw]
                    with ve.Fori(0, chunks(nw) // UB) as ii:
                        for n in range(UB):
                            half = n % 2
                            link.base, link.n = ii * (UB * per) + (start + n * per), 0
                            ve.wait_ge(s_t, ii * UB + (done + n + 1))
                            uw = by_window(u[:, n, :], nw).rearrange("p w (y x) -> p w y x", x=k)
                            cw = by_window(pC[:, half, :], nw).rearrange("p w (y x) -> p w y x", x=k)
                            for t in TAPS[PE_TAPS[nw]:]:
                                ys, xs, yi, xi = shifted(k, t)
                                for w in range(nb):
                                    ins = nc.vector.scalar_tensor_tensor(cw[:, w, ys, xs], uw[:, w, yi, xi],
                                                                         wp[:, t:t + 1], cw[:, w, ys, xs],
                                                                         ALU.mult, ALU.add)
                                link(ins)
                            ve.wait_ge(s_z, ii * UB + (done + n + 1))
                            ve.wait_ge(a_out[half], ii * 64 + (16 * done + 32 * (n // 2) + 32))
                            nc.vector.tensor_tensor(by_window(acc[:, half, :], nw), by_window(y[:, half, :], nw),
                                                    by_window(pC[:, half, :], nw), ALU.add).then_inc(s_a, 1)
                    start += chunks(nw) * per


def phase_fold(nc, sems, a, d):
    with ExitStack() as mem:
        def sb(name, shape, dt=F32):
            return mem.enter_context(nc.sbuf_tensor("b_" + name, shape, dt))

        def sem(name):
            return sems.new("b_" + name)

        field = [sb(f"field{k}", [P, H + 2, PITCH]) for k in range(2)]
        tile = sb("tile", [P, 2, max(window(n)[1] * n * n for n in WINDOWS)])
        tile_in = [sem(f"tile_in{k}") for k in range(2)]
        s_used = [sem(f"s_used{k}") for k in range(2)]
        s_zero = sem("s_zero")
        dv = sem("dv")
        s_done = sem("s_done")
        out_f = [sem(f"out_f{k}") for k in range(WB)]
        ROWS_OF = [(j, nw, part) for j, nw in enumerate(WINDOWS) for part in range(0, window(nw)[1], window(nw)[0])]
        PLAIN = [x for x in ROWS_OF if H % x[1] == 0]
        SHARED = [x for x in ROWS_OF if H % x[1]]

        def turns_of(nw, y0):
            return min(window(nw)[0], window(nw)[1] - y0) // 2

        def place(eng, copy, half):
            done = 0
            for j, nw, y0 in PLAIN:
                y0_, ny, x0, nx, v = window_parts(field[j % 2], nw)[0]
                with eng.Fori(0, ny // 2) as i:
                    eng.wait_ge(tile_in[half], i * 16 + 16 * (done + 1))
                    dst = v[:, bass.ds(i * 2 + half, 1), 0:nx].rearrange("p o x u v -> p (o x) u v")
                    src = tile[:, half, 0:nx * nw * nw].rearrange("p (x u v) -> p x u v", u=nw, v=nw)
                    copy(dst, src).then_inc(s_used[half], 1)
                done += ny // 2
            return done

        with nc.Block() as block:
            @block.gpsimd
            def _(gp):
                done = 0
                for j, nw, y0 in ROWS_OF:
                    k = window(nw)[1]
                    n = k * nw * nw
                    v = d.v[j].rearrange("b c n -> (b c) n")
                    with gp.Fori(0, turns_of(nw, y0)) as i:
                        for half in range(2):
                            gp.wait_ge(s_used[half], i + (done + 1))
                            gp.dma_start(tile[:, half, 0:n], at(v, (i * 2 + (y0 + half)) * n, n)).then_inc(tile_in[half], 16)
                    done += turns_of(nw, y0)

            @block.sync
            def _(sp):
                def store(j):
                    for b in range(B):
                        sp.dma_start(d.cat[b, j * CB:(j + 1) * CB].rearrange("c (y x) -> c y x", x=W),
                                     field[j % 2][b * CB:(b + 1) * CB, 0:H, 0:W]).then_inc(out_f[j], 16)

                done = 0
                for j, nw, y0 in PLAIN:
                    done += turns_of(nw, y0)
                    for k in range(2):
                        sp.wait_ge(s_used[k], done + 1)
                    store(j)
                sp.wait_ge(s_done, 1)
                store(WB - 1)
                for k in range(WB):
                    sp.wait_ge(out_f[k], 16 * B)

            @block.scalar
            def _(act):
                act.sem_inc(s_used[1], 1)
                place(act, lambda dst, src: nc.scalar.activation(dst, src, ACT.Copy), 1)

            @block.vector
            def _(ve):
                link = Link(ve, dv)
                ve.sem_inc(s_used[0], 1)
                done = place(ve, nc.vector.tensor_copy, 0)
                F_ = field[(WB - 1) % 2]
                ve.wait_ge(out_f[0], 16 * B)
                ve.wait_ge(s_used[1], done + 1)
                link(nc.vector.memset(F_[:, :, :], 0.0))
                base = link.n
                for j, nw, y0 in SHARED:
                    parts = [p for p in window_parts(F_, nw) if p[0] == y0]
                    turns = turns_of(nw, y0)
                    with ve.Fori(0, turns) as i:
                        for half in range(2):
                            link.base, link.n = i * 4 + base, 2 * half
                            ve.wait_ge(tile_in[half], i * 16 + 16 * (done + 1))
                            for _, _, x0, nx, v in parts:
                                dst = v[:, bass.ds(i * 2 + half, 1), 0:nx].rearrange("p o x u v -> p (o x) u v")
                                src = tile[:, half, x0 * nw * nw:(x0 + nx) * nw * nw].rearrange("p (x u v) -> p x u v", u=nw, v=nw)
                                link(nc.vector.tensor_tensor(dst, dst, src, ALU.add))
                            ve.sem_inc(s_used[half], 1)
                    base += turns * 4
                    done += turns
                link.base, link.n = base, 0
                nw = WINDOWS[-1]
                step, k = window(nw)
                rows = F_[:, step:nw * step, 0:W].rearrange("p (u y) x -> p u y x", y=step)[:, :, 0:k - step]
                link(nc.vector.tensor_scalar(rows, rows, 0.5, None, ALU.mult))
                cols = F_[:, 0:H, step:nw * step].rearrange("p y (v x) -> p y v x", x=step)[:, :, :, 0:k - step]
                nc.vector.tensor_scalar(cols, cols, 0.5, None, ALU.mult).then_inc(s_done, 1)


def phase_last(nc, sems, a, d, out):
    with ExitStack() as mem:
        def sb(name, shape, dt=F32):
            return mem.enter_context(nc.sbuf_tensor("l_" + name, shape, dt))

        def ps(name, shape, dt=F32):
            return mem.enter_context(nc.psum_tensor("l_" + name, shape, dt))

        def sem(name):
            return sems.new("l_" + name)

        TN = 2048
        TURNS = B * N // TN
        PI = N // TN
        ident = sb("ident", [P, P])
        w3r = sb("w3r", [KC, 2, C])
        w3 = sb("w3", [KC, 2, C])
        b3 = sb("b3", [KC, 2])
        x = sb("x", [KC, 2, 2, TN])
        f = sb("f", [KC, 2, 2, TN])
        o = sb("o", [KC, 2, 2, TN])
        pO = ps("pO", [KC, 8, 512])
        made, con, pre_pe, pre_dv = (sem(n) for n in ("made", "con", "pre_pe", "pre_dv"))
        x_in = [sem(f"x_in{k}") for k in range(2)]
        s_x = sem("s_x")
        s_O = sem("s_O")
        s_o = sem("s_o")
        o_out = [sem(f"o_out{k}") for k in range(2)]
        x_v = d.x1.rearrange("b (k p) n -> b p k n", k=2)
        f_v = d.cat.rearrange("b (k p) n -> b p k n", k=2)
        o_v = out.rearrange("b (k p) h w -> b p k (h w)", k=2)

        with nc.Block() as block:
            @block.gpsimd
            def _(gp):
                nc.gpsimd.memset(ident[:, :], 0.0).then_inc(made, 1)
                gp.wait_ge(made, 1)
                nc.gpsimd.affine_select(out=ident[:, :], in_=ident[:, :], compare_op=ALU.not_equal, fill=1.0,
                                        base=0, pattern=[[-1, P]], channel_multiplier=1).then_inc(made, 1)
                with gp.Fori(0, TURNS // 2) as ii:
                    for half in range(2):
                        i = ii * 2 + half
                        gp.wait_ge(s_O, i * 8 + 8)
                        for t, v in ((x, x_v), (f, f_v)):
                            gp.dma_start(t[:, half, :, :], v[bass.ds(i // PI, 1), :, :, bass.ds((i % PI) * TN, TN)]
                                         .rearrange("b p k n -> (b p) k n")).then_inc(x_in[half], 16)

            @block.sync
            def _(sp):
                sp.dma_start(w3r[:, :, :], a["L1_conv_w3"].rearrange("(m p) c -> p m c", m=2)).then_inc(con, 16)
                with nc.allow_non_contiguous_dma("small constants"):
                    sp.dma_start(b3[:, :], a["L1_conv_b3"].rearrange("(m p) -> p m", m=2)).then_inc(con, 16)
                for k in range(2):
                    sp.sem_inc(o_out[k], 16)
                with sp.Fori(0, TURNS // 2) as ii:
                    for half in range(2):
                        i = ii * 2 + half
                        sp.wait_ge(s_o, i * 8 + 16)
                        sp.dma_start(o_v[bass.ds(i // PI, 1), :, :, bass.ds((i % PI) * TN, TN)]
                                     .rearrange("b p k n -> (b p) k n"), o[:, half, :, :]).then_inc(o_out[half], 16)
                for k in range(2):
                    sp.wait_ge(o_out[k], 16 * (TURNS // 2) + 16)

            @block.tensor
            def _(te):
                te.sem_inc(s_O, 16)
                te.wait_ge(made, 2)
                te.wait_ge(con, 32)
                for m in range(2):
                    for k in range(2):
                        nc.tensor.transpose(pO[:, k, m * KC:(m + 1) * KC], w3r[:, m, k * KC:(k + 1) * KC],
                                            ident[0:KC, 0:KC]).then_inc(pre_pe, 1)
                te.wait_ge(pre_dv, 1)
                with te.Fori(0, TURNS // 2) as ii:
                    for half in range(2):
                        i = ii * 2 + half
                        te.wait_ge(s_x, i + 1)
                        for m in range(2):
                            for q in range(4):
                                n = m * 4 + q
                                te.wait_ge(s_o, i * 8 + (n + 1))
                                for k in range(2):
                                    mm = nc.tensor.matmul(pO[:, n, :], w3[:, k, m * KC:(m + 1) * KC],
                                                          x[:, half, k, q * 512:(q + 1) * 512], start=(k == 0), stop=(k == 1))
                                mm.then_inc(s_O, 1)

            @block.scalar
            def _(act):
                act.sem_inc(s_o, 8)
                with act.Fori(0, TURNS // 2) as ii:
                    for half in range(2):
                        i = ii * 2 + half
                        act.wait_ge(o_out[half], ii * 16 + 16)
                        for n in range(8):
                            act.wait_ge(s_O, i * 8 + (n + 17))
                            m, q = n // 4, n % 4
                            nc.scalar.activation(o[:, half, m, q * 512:(q + 1) * 512], pO[:, n, :], ACT.Identity,
                                                 bias=b3[:, m:m + 1]).then_inc(s_o, 1)

            @block.vector
            def _(ve):
                ve.wait_ge(pre_pe, 4)
                nc.vector.tensor_copy(w3[:, :, :], pO[:, 0:2, 0:C]).then_inc(pre_dv, 1)
                with ve.Fori(0, TURNS // 2) as ii:
                    for half in range(2):
                        ve.wait_ge(x_in[half], ii * 32 + 32)
                        nc.vector.tensor_tensor(x[:, half, :, :], x[:, half, :, :], f[:, half, :, :], ALU.add).then_inc(s_x, 1)


class Semaphores:

    def __init__(self, nc):
        self.nc, self.held = nc, []

    def new(self, name):
        self.held.append(self.nc.alloc_semaphore(name=name))
        return self.held[-1]

    def clear(self):
        self.nc.clear_and_free_semaphores(self.held)
        self.held = []
        self.nc.all_engine_barrier()


def build(nc, a, out, phases="tsafcmbl"):
    d = scratch(nc)
    sems = Semaphores(nc)
    work = {"t": phase_tokens, "s": phase_sort, "a": phase_attend, "f": phase_ffn,
            "c": phase_cut, "m": phase_mix, "b": phase_fold}
    for phase in phases:
        if phase == "l":
            phase_last(nc, sems, a, d, out)
        else:
            work[phase](nc, sems, a, d)
        if phase != phases[-1]:
            sems.clear()


_INS = ['x', 'L0_conv_td', 'L0_conv_g1', 'L0_conv_b1', 'L0_conv_g2', 'L0_conv_b2', 'L0_conv_g3', 'L0_conv_b3',
        'L0_conv_wq_w', 'L0_conv_wq_b', 'L0_conv_wk_w', 'L0_conv_wk_b', 'L0_conv_wv_w', 'L0_conv_wv_b',
        'L0_conv_ca_scale', 'L0_conv_wqkv_w', 'L0_conv_wqkv_b', 'L0_conv_proj_w', 'L0_conv_proj_b',
        'L0_conv_fc_td_w', 'L0_conv_fc_td_b', 'L0_conv_fc1_w', 'L0_conv_fc1_b', 'L0_conv_dw_w', 'L0_conv_dw_b',
        'L0_conv_fc2_w', 'L0_conv_fc2_b', 'L1_conv_w1', 'L1_conv_b1', 'L1_conv_w2', 'L1_conv_b2', 'L1_conv_w3',
        'L1_conv_b3', 'L1_conv_wpos', 'L1_conv_bpos', 'L1_conv_wse1', 'L1_conv_wse2']


def kernel(**inputs):
    import concourse.bacc as bacc
    from concourse.bass_utils import run_bass_kernel_spmd

    nc = bacc.Bacc("TRN2", target_bir_lowering=False, num_devices=1)
    arrays, args = {}, {}
    for name in _INS:
        x = np.ascontiguousarray(inputs[name])
        arrays["in_" + name] = x
        args[name] = nc.dram_tensor("in_" + name, x.shape, mybir.dt.from_np(x.dtype), kind="ExternalInput").ap()
    out = nc.dram_tensor("out_0", (B, C, H, W), F32, kind="ExternalOutput").ap()
    build(nc, args, out)
    r = run_bass_kernel_spmd(nc, [arrays], core_ids=[0])
    return r.results[0]["out_0"]
```

```python
from contextlib import ExitStack

import numpy as np

import concourse.bass as bass
from concourse import mybir

ALU = mybir.AluOpType
ACT = mybir.ActivationFunctionType
AX = mybir.AxisListType
F32 = mybir.dt.float32
BF16 = mybir.dt.bfloat16
I32 = mybir.dt.int32
U32 = mybir.dt.uint32

B, C, H, W = 2, 192, 128, 128
N = H * W
P = 128
KC = C // 2
M = 128
RD = 10
HEADS, HD = 4, C // 4
GS = 256
TDF = 16
HID = 4 * C
KS = 5
PADY = KS // 2
HP = H + 2 * PADY
BT = 512
TT = BT // P
NB = N // BT
EPS = 1e-5


class Scratch:
    pass


def scratch(nc):
    d = Scratch()

    def t(name, shape, dt=F32):
        return nc.dram_tensor(name, shape, dt, kind="Internal").ap()

    d.xh = t("xhat_rows", (B * N, C))
    d.xt = t("xhat_chan", (B, C + 1, HP * W))
    d.td = t("td_chan", (B, TDF, HP * W))
    d.res = t("res_chan", (B, C, N))
    d.xs = t("xhat_sorted", (B * N, C))
    d.pos = t("sorted_pos", (P, B * N // P), I32)
    d.aca = t("attn_sorted", (B * N, C))
    d.tdc = t("td_sum", (B, TDF, N))
    d.x1 = t("x1_chan", (B, C, N))
    d.xc = t("xc_chan", (B, C // 3, N))
    d.u = [t(f"cut_{nw}", (B, CB, (window(nw)[1] * nw) ** 2)) for nw in WINDOWS]
    d.v = [t(f"worked_{nw}", (B, CB, (window(nw)[1] * nw) ** 2)) for nw in WINDOWS]
    d.cat = t("folded", (B, C, N))
    return d


def at(ap, lo, n):
    return ap[:, bass.ds(lo, n)]


class Link:

    def __init__(self, eng, sem):
        self.eng, self.sem, self.base, self.n = eng, sem, 0, 0

    def __call__(self, ins):
        ins.then_inc(self.sem, 1)
        self.n += 1
        self.eng.wait_ge(self.sem, self.base + self.n)


def phase_tokens(nc, sems, a, d):
    with ExitStack() as mem:
        def sb(name, shape, dt=F32):
            return mem.enter_context(nc.sbuf_tensor("t_" + name, shape, dt))

        def ps(name, shape, dt=F32):
            return mem.enter_context(nc.psum_tensor("t_" + name, shape, dt))

        def sem(name):
            return sems.new("t_" + name)

        XB = 8
        ident = sb("ident", [P, P])
        identb = sb("identb", [P, P], BF16)
        onesb = sb("onesb", [P, P], BF16)
        tri = sb("tri", [P, P], BF16)
        onesf = sb("onesf", [P, P])
        zeros = sb("zeros", [P, 2 * W])
        iota = sb("iota", [P, P])
        tdr = sb("tdr", [P, C])
        tdT = sb("tdT", [KC, 2, P])
        g1 = sb("g1", [KC, 2])
        b1 = sb("b1", [KC, 2])
        wq = sb("wq", [KC, 2, RD])
        wqg = sb("wqg", [KC, 2, RD])
        wk = sb("wk", [KC, 2, RD])
        wv = sb("wv", [KC, 2, C])
        wt = sb("wt", [KC, 2, TDF])
        rows = sb("rows", [1, RD + C + TDF])
        bq = sb("bq", [RD, 1])
        ca = sb("ca", [P, 1])
        k0 = sb("k0", [P, RD])
        ksq = sb("ksq", [P, RD])
        kn2 = sb("kn2", [P, 1])
        kT = sb("kT", [RD, P])
        v = sb("v", [P, C])
        tdf = sb("tdf", [P, TDF])

        xin = sb("xin", [KC, 2, XB, BT])
        st6 = sb("st6", [P, TT, 6])
        mv = sb("mv", [P, TT, 2])
        rstd = sb("rstd", [P, TT])
        xh = sb("xh", [P, TT, C])
        xT = sb("xT", [KC, 2, BT])
        qT = sb("qT", [RD, BT])
        qsq = sb("qsq", [RD, BT])
        qn = sb("qn", [P, TT])
        smax = sb("smax", [P, TT])
        mx = sb("mx", [P, TT, 8])
        ix = sb("ix", [P, TT, 8], U32)
        nmx = sb("nmx", [P, TT])
        e = sb("e", [P, TT, M])
        esum = sb("esum", [P, TT])
        erec = sb("erec", [P, TT])
        pr = sb("pr", [P, TT, M])
        prT = sb("prT", [P, BT])
        cat = sb("cat", [P, TT])
        oh = sb("oh", [P, TT, M], BF16)
        ohT = sb("ohT", [P, BT])
        tdx = sb("tdx", [TDF, BT])
        rk = sb("rk", [P, TT, M])
        res = sb("res", [KC, 2, BT])
        seen = sb("seen", [P, M])
        cats = sb("cats", [P, B * NB * TT])
        rank = sb("rank", [P, B * NB * TT])
        tot = sb("tot", [P, B, M])
        TURN = 16
        picked = sb("picked", [P, TURN, M])
        ends = sb("ends", [P, B, M])
        off = sb("off", [P, B, M])
        pick = sb("pick", [P, M])
        eq = sb("eq", [P, M])
        posf = sb("posf", [P, B * NB * TT])
        posi = sb("posi", [P, B * NB * TT], I32)

        pT = ps("pT", [P, 2, 512])
        pX = ps("pX", [KC, 2, BT])
        pS = ps("pS", [P, TT, M])
        pP = ps("pP", [P, BT])
        pR = ps("pR", [P, TT, M])
        pON = ps("pON", [P, 512])
        pO = pON[:, 0:BT // 2].bitcast(BF16)
        pN = pON[:, BT // 2:BT // 2 + M]
        pN2 = pON[:, BT // 2 + M:BT // 2 + M + TT]
        pQT = pP[0:RD, :]
        pD = pP[0:TDF, :]

        marks = sem("marks")
        s_var = sem("s_var")
        s_rs = sem("s_rs")
        s_sq = sem("s_sq")
        s_pw = sem("s_pw")
        con = sem("con")
        made = sem("made")
        pads = sem("pads")
        x_in = [sem(f"x_in{k}") for k in range(XB)]
        x_free = sem("x_free")
        pe = sem("pe")
        dv = sem("dv")
        dvp = sem("dvp")
        s_xT = sem("s_xT")
        s_xh = sem("s_xh")
        s_xb = sem("s_xb")
        s_xc = sem("s_xc")
        s_q = sem("s_q")
        s_qc = sem("s_qc")
        s_s = sem("s_s")
        s_m = sem("s_m")
        s_e = sem("s_e")
        s_p = sem("s_p")
        s_oh = sem("s_oh")
        s_pt = sem("s_pt")
        s_pc = sem("s_pc")
        s_ot = sem("s_ot")
        s_oc = sem("s_oc")
        s_a = sem("s_a")
        s_r = sem("s_r")
        s_d = sem("s_d")
        s_dc = sem("s_dc")
        s_res = sem("s_res")
        s_rk = sem("s_rk")
        o_xh = sem("o_xh")
        o_xT = sem("o_xT")
        o_td = sem("o_td")
        o_res = sem("o_res")
        s_tot = sem("s_tot")
        s_cum = sem("s_cum")
        s_pos = sem("s_pos")
        o_pos = sem("o_pos")

        CON = 12
        x_v = a["x"].rearrange("b (k p) h w -> b p k (h w)", k=2)
        xt_v = d.xt[:, 0:C, :].rearrange("b (k p) n -> b p k n", k=2)
        res_v = d.res.rearrange("b (k p) n -> b p k n", k=2)
        xh_v = d.xh.rearrange("(n t p) c -> n p t c", t=TT, p=P)

        BLOCKS = B * NB
        LOOPS = (BLOCKS - 3) // XB

        def image(v, i, skip):
            return v[bass.ds(i // NB, 1), :, :, bass.ds((i % NB) * BT + skip, BT)].rearrange("b p k n -> (b p) k n")

        with nc.Block() as block:
            @block.sync
            def _(sp):
                def col(dst, src):
                    sp.dma_start(dst, src).then_inc(con, 16)

                with nc.allow_non_contiguous_dma('small constants'):
                    col(g1[:, :], a["L0_conv_g1"].rearrange("(k p) -> p k", k=2))
                    col(b1[:, :], a["L0_conv_b1"].rearrange("(k p) -> p k", k=2))
                    col(tdr[:, :], a["L0_conv_td"])
                    col(wq[:, :, :], a["L0_conv_wq_w"].rearrange("(k p) r -> p k r", k=2))
                    col(wk[:, :, :], a["L0_conv_wk_w"].rearrange("(k p) r -> p k r", k=2))
                    col(wv[:, :, :], a["L0_conv_wv_w"].rearrange("(k p) r -> p k r", k=2))
                    col(wt[:, :, :], a["L0_conv_fc_td_w"].rearrange("(k p) r -> p k r", k=2))
                    col(bq[:, :], a["L0_conv_wq_b"].rearrange("(r o) -> r o", o=1))
                    at0 = 0
                    for name in ("wk_b", "wv_b", "fc_td_b"):
                        src = a["L0_conv_" + name]
                        n = src.shape[0]
                        col(rows[:, at0:at0 + n], src.rearrange("(a n) -> a n", a=1))
                        at0 += n
                    col(ca[:, :], a["L0_conv_ca_scale"].rearrange("(a n) -> a n", a=1).broadcast_to([P, 1]))
                with sp.Fori(0, BLOCKS) as i:
                    sp.wait_ge(s_res, i + 2)
                    sp.dma_start(image(res_v, i, 0), res[:, :, :]).then_inc(o_res, 16)
                sp.wait_ge(o_res, 16 * B * NB + 16)
                sp.wait_ge(s_pos, 1)
                sp.dma_start(d.pos, posi[:, :]).then_inc(o_pos, 16)
                sp.wait_ge(o_pos, 16)

            @block.gpsimd
            def _(gp):
                nc.gpsimd.memset(ident[:, :], 0.0).then_inc(made, 1)
                nc.gpsimd.memset(identb[:, :], 0.0).then_inc(made, 1)
                nc.gpsimd.memset(tri[:, :], 1.0).then_inc(made, 1)
                nc.gpsimd.memset(onesb[:, :], 1.0).then_inc(made, 1)
                nc.gpsimd.memset(onesf[:, :], 1.0).then_inc(made, 1)
                nc.gpsimd.memset(zeros[:, :], 0.0).then_inc(made, 1)
                gp.wait_ge(made, 6)
                for m in (ident, identb):
                    nc.gpsimd.affine_select(out=m[:, :], in_=m[:, :], compare_op=ALU.not_equal, fill=1.0,
                                            base=0, pattern=[[-1, P]], channel_multiplier=1).then_inc(made, 1)
                nc.gpsimd.affine_select(out=tri[:, :], in_=tri[:, :], compare_op=ALU.is_gt, fill=0.0,
                                        base=0, pattern=[[1, P]], channel_multiplier=-1).then_inc(made, 1)
                nc.gpsimd.iota(iota[:, :], pattern=[[1, P]], base=0, channel_multiplier=0,
                               allow_small_or_imprecise_dtypes=True).then_inc(made, 1)
                gp.wait_ge(made, 10)
                edge = PADY * W
                for b in range(B):
                    for lo in (0, edge + N):
                        for c0, n in ((0, P), (P, C + 1 - P)):
                            gp.dma_start(d.xt[b, c0:c0 + n, lo:lo + edge], zeros[0:n, :]).then_inc(pads, 16)
                        gp.dma_start(d.td[b, :, lo:lo + edge], zeros[0:TDF, :]).then_inc(pads, 16)
                    gp.dma_start(d.xt[b, C, edge:edge + N].rearrange("(h w) -> h w", h=H),
                                 onesf[:, :]).then_inc(pads, 16)
                gp.wait_ge(pads, 16 * B * 7)
                with gp.Fori(0, BLOCKS // XB) as ii:
                    for k in range(XB):
                        gp.wait_ge(x_free, ii * XB + (k + 1))
                        gp.dma_start(xin[:, :, k, :], image(x_v, ii * XB + k, 0)).then_inc(x_in[k], 16)

            @block.tensor
            def _(te):
                te.wait_ge(made, 10)
                te.wait_ge(con, 16 * CON)
                te.wait_ge(dvp, 1)
                for k in range(2):
                    nc.tensor.transpose(pT[0:KC, 0, k * P:(k + 1) * P], tdr[:, k * KC:(k + 1) * KC],
                                        ident[:, :]).then_inc(pe, 1)
                te.wait_ge(dvp, 2)
                at0 = 0
                for o, w_, n in ((0, wk, RD), (16, wv, C), (256, wt, TDF)):
                    dst = pT[:, 1, o:o + n]
                    for k in range(2):
                        nc.tensor.matmul(dst, tdT[:, k, :], w_[:, k, :], start=(k == 0), stop=False)
                    nc.tensor.matmul(dst, onesf[0:1, :], rows[:, at0:at0 + n], start=False, stop=True).then_inc(pe, 1)
                    at0 += n
                for k in range(2):
                    nc.tensor.matmul(pS[0:RD, 0, 0:1], wq[:, k, :], b1[:, k:k + 1], start=(k == 0),
                                     stop=(k == 1)).then_inc(pe, 1)
                te.wait_ge(dvp, 3)
                nc.tensor.transpose(pS[0:RD, 1, :], k0[:, :], ident[:, :]).then_inc(pe, 1)
                te.wait_ge(dvp, 4)

                def x_turned(i, k, turn):
                    te.wait_ge(x_in[k], turn * 16 + 16)
                    if not isinstance(i, int) or i:
                        te.wait_ge(s_xh, i)
                    for t in range(TT):
                        for c in range(2):
                            mm = nc.tensor.transpose(
                                pT[:, t // 2, (t % 2) * C + c * KC:(t % 2) * C + (c + 1) * KC],
                                xin[:, c, k, t * P:(t + 1) * P], ident[0:KC, 0:KC])
                    mm.then_inc(s_xT, 1)

                def onehot_turned(b):
                    te.wait_ge(s_oh, b + 1)
                    for t in range(TT):
                        mm = nc.tensor.transpose(pO[:, t * P:(t + 1) * P], oh[:, t, :], identb[:, :])
                    mm.then_inc(s_ot, 1)

                def xhat_turned(i):
                    te.wait_ge(s_xh, i + 1)
                    if not isinstance(i, int) or i > 1:
                        te.wait_ge(s_res, i - 1)
                    for t in range(TT):
                        for k in range(2):
                            mm = nc.tensor.transpose(pX[:, k, t * P:(t + 1) * P], xh[:, t, k * KC:(k + 1) * KC],
                                                     ident[:, :])
                    mm.then_inc(s_xb, 1)

                def ranks(b):
                    te.wait_ge(s_rk, b + 1)
                    te.wait_ge(s_oc, b + 1)
                    nc.tensor.matmul(pR[:, :, :], tri[:, :], oh[:, :, :], start=True, stop=False)
                    for u in range(TT - 1):
                        nc.tensor.matmul(pR[:, u + 1:TT, :], onesb[:, :],
                                         oh[:, u, :].unsqueeze(1).to_broadcast([P, TT - 1 - u, M]),
                                         start=False, stop=(u == TT - 2))
                    for u in range(TT):
                        mm = nc.tensor.matmul(pN, onesb[:, :], oh[:, u, :], start=(u == 0), stop=(u == TT - 1))
                    mm.then_inc(s_r, 1)

                def probs_turned(b):
                    te.wait_ge(s_p, b + 1)
                    te.wait_ge(s_dc, b + 1)
                    for t in range(TT):
                        mm = nc.tensor.transpose(pP[:, t * P:(t + 1) * P], pr[:, t, :], ident[:, :])
                    mm.then_inc(s_pt, 1)

                def queries(i):
                    te.wait_ge(s_xc, i + 2)
                    if not isinstance(i, int) or i:
                        te.wait_ge(s_dc, i)
                    for k in range(2):
                        mm = nc.tensor.matmul(pQT, wqg[:, k, :], xT[:, k, :], start=(k == 0), stop=(k == 1))
                    mm.then_inc(s_q, 1)

                def features(b):
                    te.wait_ge(s_pc, b + 1)
                    te.wait_ge(s_oc, b + 1)
                    nc.tensor.matmul(pD, tdf[:, :], ohT[:, :], start=True, stop=True).then_inc(s_d, 1)

                def looked_up(b, ahead):
                    if ahead:
                        te.wait_ge(s_xc, b + 4)
                    te.wait_ge(s_res, b + 1)
                    for k in range(2):
                        mm = nc.tensor.matmul(pX[:, k, :], v[:, k * KC:(k + 1) * KC], prT[:, :], start=True, stop=True)
                    mm.then_inc(s_a, 1)

                def similarities(i):
                    te.wait_ge(s_qc, i + 2)
                    if not isinstance(i, int) or i:
                        te.wait_ge(s_e, i)
                        te.wait_ge(s_rk, i)
                    for t in range(TT):
                        nc.tensor.matmul(pS[:, t, :], qT[:, t * P:(t + 1) * P], kT[:, :], start=True, stop=True)
                    for t in range(TT):
                        mm = nc.tensor.matmul(pN2[:, t:t + 1], qsq[:, t * P:(t + 1) * P], onesf[0:RD, 0:1],
                                              start=True, stop=True)
                    mm.then_inc(s_s, 1)

                def period(i, k, turn, ahead=True, front=True, mid=True, back=True, tail=True):
                    if mid:
                        queries(i)
                    if tail:
                        ranks(i - 2)
                    if mid:
                        similarities(i)
                    if back:
                        onehot_turned(i - 1)
                        probs_turned(i - 1)
                    if front:
                        xhat_turned(i + 1)
                    if back:
                        features(i - 1)
                    if ahead:
                        x_turned(i + 2, k, turn)
                    if back:
                        looked_up(i - 1, front)

                period(-2, 0, 0, front=False, mid=False, back=False, tail=False)
                period(-1, 1, 0, mid=False, back=False, tail=False)
                period(0, 2, 0, back=False, tail=False)
                period(1, 3, 0, tail=False)
                with te.Fori(0, LOOPS) as ii:
                    for c in range(2, XB + 2):
                        period(ii * XB + c, (c + 2) % XB, ii + (c + 2) // XB)
                for i in range(XB * LOOPS + 2, BLOCKS - 1):
                    period(i, (i + 2) % XB, (i + 2) // XB, ahead=(i + 2 < BLOCKS))
                period(BLOCKS - 1, None, None, ahead=False, front=False)
                period(BLOCKS, None, None, ahead=False, front=False, mid=False)
                ranks(BLOCKS - 1)
                te.wait_ge(s_tot, 1)
                for b in range(B):
                    mm = nc.tensor.matmul(pS[:, b, :], onesf[:, :], ends[:, b, :], start=True, stop=True)
                mm.then_inc(s_cum, 1)

            @block.scalar
            def _(act):
                for s in (s_xc, s_qc, s_dc):
                    act.sem_inc(s, 1)
                act.sem_inc(o_xh, 16)
                act.sem_inc(o_xT, 16)
                act.sem_inc(o_td, 16)
                act.sem_inc(o_res, 16)
                act.wait_ge(s_sq, 1)
                nc.scalar.activation(kn2[:, :], kn2[:, :], ACT.Sqrt).then_inc(s_pw, 1)

                def period(i, front=True, mid=True, back=True):
                    b, j = i - 1, i + 1
                    if back:
                        act.wait_ge(s_m, b + 1)
                        for t in range(TT):
                            ins = nc.scalar.activation(e[:, t, :], pS[:, t, :], ACT.Exp, bias=nmx[:, t:t + 1],
                                                       scale=qn[:, t:t + 1], accum_out=esum[:, t:t + 1])
                        ins.then_inc(s_e, 1)
                    if mid:
                        act.wait_ge(s_q, i + 1)
                        nc.scalar.activation(qT[:, :], pQT, ACT.Identity, bias=bq[:, 0:1])
                        nc.scalar.activation(qsq[:, :], pQT, ACT.Square, bias=bq[:, 0:1]).then_inc(s_qc, 1)
                    if front:
                        act.wait_ge(s_var, j + 1)
                        nc.scalar.activation(rstd[:, :], rstd[:, :], ACT.Sqrt).then_inc(s_rs, 1)
                    if mid:
                        act.wait_ge(s_sq, i + 2)
                        nc.scalar.activation(qn[:, :], qn[:, :], ACT.Sqrt).then_inc(s_pw, 1)
                    if back:
                        act.wait_ge(s_ot, b + 1)
                        nc.scalar.activation(ohT[:, :], pO, ACT.Copy).then_inc(s_oc, 1)
                        act.wait_ge(s_pt, b + 1)
                        nc.scalar.activation(prT[:, :], pP[:, :], ACT.Copy).then_inc(s_pc, 1)
                    if front:
                        act.wait_ge(s_xh, j + 1)
                        act.dma_start(xh_v[bass.ds(j, 1)].rearrange("a p t c -> (a p) t c"),
                                      xh[:, :, :]).then_inc(o_xh, 16)
                        act.wait_ge(s_xb, j + 1)
                        act.wait_ge(o_xT, j * 16 + 16)
                        nc.scalar.activation(xT[:, :, :], pX[:, :, :], ACT.Copy).then_inc(s_xc, 1)
                        act.wait_ge(s_xc, j + 2)
                        act.dma_start(image(xt_v, j, PADY * W), xT[:, :, :]).then_inc(o_xT, 16)
                    if back:
                        act.wait_ge(s_d, b + 1)
                        act.wait_ge(o_td, b * 16 + 16)
                        nc.scalar.activation(tdx[:, :], pD, ACT.Copy).then_inc(s_dc, 1)
                        act.wait_ge(s_dc, b + 2)
                        act.dma_start(d.td[bass.ds(b // NB, 1), :, bass.ds((b % NB) * BT + PADY * W, BT)]
                                      .rearrange("b p n -> (b p) n"), tdx[:, :]).then_inc(o_td, 16)

                period(-1, mid=False, back=False)
                period(0, back=False)
                with act.Fori(1, BLOCKS - 1) as i:
                    period(i)
                period(BLOCKS - 1, front=False)
                period(BLOCKS, front=False, mid=False)
                act.wait_ge(o_xh, 16 * B * NB + 16)
                act.wait_ge(o_xT, 16 * B * NB + 16)
                act.wait_ge(o_td, 16 * B * NB + 16)

            @block.vector
            def _(ve):
                link = Link(ve, dv)
                ve.sem_inc(dvp, 1)
                ve.sem_inc(x_free, XB)
                ve.sem_inc(s_rk, 1)
                ve.wait_ge(con, 16 * CON)
                ve.wait_ge(pe, 2)
                nc.vector.tensor_copy(tdT[:, :, :], pT[0:KC, 0, 0:2 * P].rearrange("p (k n) -> p k n", k=2)).then_inc(dvp, 1)
                for k in range(2):
                    nc.vector.tensor_scalar(wqg[:, k, :], wq[:, k, :], g1[:, k:k + 1], None, ALU.mult)
                nc.vector.memset(seen[:, :], 0.0)
                link(nc.vector.tensor_scalar(ca[:, :], ca[:, :], 0.0, 3.0, ALU.max, ALU.min))
                link(nc.vector.tensor_scalar(ca[:, :], ca[:, :], float(np.log(M)), 1.0, ALU.mult, ALU.add))
                ve.wait_ge(pe, 5)
                link(nc.vector.tensor_copy(k0[:, :], pT[:, 1, 0:RD]))
                nc.vector.tensor_copy(v[:, :], pT[:, 1, 16:16 + C])
                nc.vector.tensor_copy(tdf[:, :], pT[:, 1, 256:256 + TDF])
                link(nc.vector.tensor_tensor(ksq[:, :], k0[:, :], k0[:, :], ALU.mult))
                link(nc.vector.tensor_reduce(kn2[:, :], ksq[:, :], AX.X, ALU.add))
                nc.vector.tensor_scalar(kn2[:, :], kn2[:, :], 1e-24, None, ALU.max).then_inc(s_sq, 1)
                ve.wait_ge(s_pw, 1)
                link(nc.vector.reciprocal(kn2[:, :], kn2[:, :]))
                nc.vector.tensor_scalar(k0[:, :], k0[:, :], kn2[:, 0:1], ca[:, 0:1], ALU.mult,
                                        ALU.mult).then_inc(dvp, 1)
                ve.wait_ge(pe, 8)
                nc.vector.tensor_copy(kT[:, :], pS[0:RD, 1, :])
                link(nc.vector.tensor_tensor(bq[:, :], pS[0:RD, 0, 0:1], bq[:, :], ALU.add))
                ve.sem_inc(s_res, 1)
                ve.sem_inc(dvp, 1)
                start = link.n
                FRONT, MID, BACK, TAIL = 3, 1, 5, 3

                def statistics(i):
                    ve.wait_ge(s_xT, i + 1)
                    for t in range(TT):
                        ins = nc.vector.bn_stats(st6[:, t, :], pT[:, t // 2, (t % 2) * C:(t % 2) * C + C])
                    link(ins)
                    ve.sem_inc(marks, 1)
                    for t in range(TT):
                        ins = nc.vector.bn_aggr(mv[:, t, :], st6[:, t, :])
                    link(ins)
                    nc.vector.tensor_scalar(rstd[:, :], mv[:, :, 1], EPS, None, ALU.add).then_inc(s_var, 1)

                def normalised(i):
                    ve.wait_ge(s_rs, i + 1)
                    link(nc.vector.reciprocal(rstd[:, :], rstd[:, :]))
                    ve.wait_ge(o_xh, i * 16 + 16)
                    for t in range(TT):
                        ins = nc.vector.tensor_scalar(xh[:, t, :], pT[:, t // 2, (t % 2) * C:(t % 2) * C + C],
                                                      mv[:, t, 0:1], rstd[:, t:t + 1], ALU.subtract, ALU.mult)
                    ins.then_inc(s_xh, 1)

                def query_norms(i):
                    nc.vector.tensor_scalar(qn[:, :], pN2, 1e-24, None, ALU.max).then_inc(s_sq, 1)

                def norms_inverted(i):
                    ve.wait_ge(s_pw, i + 2)
                    link(nc.vector.reciprocal(qn[:, :], qn[:, :]))

                def maxima(b):
                    ve.wait_ge(s_s, b + 1)
                    link(nc.vector.tensor_reduce(smax[:, :], pS[:, :, :], AX.X, ALU.max))
                    nc.vector.scalar_tensor_tensor(nmx[:, :], smax[:, :], -1.0, qn[:, :], ALU.mult,
                                                   ALU.mult).then_inc(s_m, 1)

                def categories(b):
                    ve.wait_ge(s_e, b + 1)
                    ve.sem_inc(marks, 1)
                    for t in range(TT):
                        ins = nc.vector.max(mx[:, t, :], e[:, t, :])
                    link(ins)
                    ve.sem_inc(marks, 1)
                    for t in range(TT):
                        ins = nc.vector.max_index(ix[:, t, :], mx[:, t, :], e[:, t, :])
                    link(ins)
                    link(nc.vector.tensor_copy(cat[:, :], ix[:, :, 0]))
                    nc.vector.tensor_copy(at(cats, b * TT, TT), cat[:, :])

                def onehots(b):
                    for t in range(TT):
                        ins = nc.vector.tensor_scalar(oh[:, t, :], iota[:, :], cat[:, t:t + 1], None, ALU.is_equal)
                    ins.then_inc(s_oh, 1)

                def probabilities(b):
                    link(nc.vector.reciprocal(erec[:, :], esum[:, :]))
                    for t in range(TT):
                        ins = nc.vector.tensor_scalar(pr[:, t, :], e[:, t, :], erec[:, t:t + 1], None, ALU.mult)
                    ins.then_inc(s_p, 1)

                def ranked(b):
                    ve.wait_ge(s_r, b + 1)
                    link(nc.vector.tensor_tensor(rk[:, :, :], pR[:, :, :],
                                                 seen[:, :].unsqueeze(1).to_broadcast([P, TT, M]), ALU.add))
                    nc.vector.tensor_tensor(seen[:, :], seen[:, :], pN, ALU.add)
                    link(nc.vector.tensor_tensor(rk[:, :, :], rk[:, :, :], oh[:, :, :], ALU.mult))
                    ve.sem_inc(s_rk, 1)
                    nc.vector.tensor_reduce(at(rank, b * TT, TT), rk[:, :, :], AX.X, ALU.add)
                    link(nc.vector.tensor_copy(tot[:, bass.ds(b // NB, 1), :].rearrange("p a m -> p (a m)"), seen[:, :]))

                def result(b, k):
                    ve.wait_ge(s_a, b + 1)
                    ve.wait_ge(o_res, b * 16 + 16)
                    nc.vector.tensor_tensor(res[:, :, :], pX[:, :, :], xin[:, :, k, :], ALU.add).then_inc(s_res, 1)
                    ve.wait_ge(s_res, b + 2)
                    ve.sem_inc(x_free, 1)

                def links(i):
                    if not isinstance(i, int):
                        return i * (FRONT + MID + BACK + TAIL) + (start + FRONT - BACK - 2 * TAIL)
                    n = [min(max(i + 1 - k, 0), BLOCKS) for k in range(4)]
                    return start + FRONT * n[0] + MID * n[1] + BACK * n[2] + TAIL * n[3]

                def period(i, k, front=True, mid=True, back=True, tail=True):
                    b = i - 1
                    link.base, link.n = links(i), 0
                    if back:
                        maxima(b)
                    if front:
                        statistics(i + 1)
                    if tail:
                        result(i - 2, k)
                        ranked(i - 2)
                    if back:
                        categories(b)
                    if mid:
                        ve.wait_ge(s_s, i + 1)
                        query_norms(i)
                    if back:
                        onehots(b)
                        probabilities(b)
                    if front:
                        normalised(i + 1)
                    if mid:
                        norms_inverted(i)
                    assert link.n == FRONT * front + MID * mid + BACK * back + TAIL * tail, link.n

                period(-1, None, mid=False, back=False, tail=False)
                period(0, None, back=False, tail=False)
                period(1, None, tail=False)
                with ve.Fori(0, LOOPS) as ii:
                    for c in range(2, XB + 2):
                        period(ii * XB + c, c - 2)
                for i in range(XB * LOOPS + 2, BLOCKS - 1):
                    period(i, (i - 2) % XB)
                period(BLOCKS - 1, (BLOCKS - 3) % XB, front=False)
                period(BLOCKS, (BLOCKS - 2) % XB, front=False, mid=False)
                period(BLOCKS + 1, (BLOCKS - 1) % XB, front=False, mid=False, back=False)
                link.base, link.n = links(BLOCKS + 2), 0
                for b in range(B):
                    if b:
                        link(nc.vector.tensor_tensor(pick[:, :], tot[:, 1, :], tot[:, 0, :], ALU.subtract))
                    src = pick if b else tot[:, 0, :]
                    link(nc.vector.tensor_tensor(eq[:, :], src if b == 0 else pick[:, :], ident[:, :], ALU.mult))
                    link(nc.vector.tensor_reduce(kn2[:, :], eq[:, :], AX.X, ALU.add))
                    link(nc.vector.tensor_scalar(ends[:, b, :], tri[:, :], kn2[:, 0:1], None, ALU.mult))
                ve.sem_inc(s_tot, 1)
                ve.wait_ge(s_cum, 1)
                link(nc.vector.tensor_copy(off[:, 0, :], pS[:, 0, :]))
                link(nc.vector.tensor_tensor(eq[:, :], pS[:, 1, :], tot[:, 0, :], ALU.subtract))
                link(nc.vector.tensor_scalar(off[:, 1, :], eq[:, :], float(N), None, ALU.add))
                start2 = link.base + link.n
                for b in range(B):
                    with ve.Fori(0, NB * TT // TURN) as j:
                        link.base, link.n = j + start2, 0
                        c = at(cats, (j + b * (NB * TT // TURN)) * TURN, TURN)
                        f = at(posf, (j + b * (NB * TT // TURN)) * TURN, TURN)
                        for t in range(TURN):
                            ins = nc.vector.scalar_tensor_tensor(picked[:, t, :], iota[:, :], c[:, t:t + 1], off[:, b, :],
                                                                 ALU.is_equal, ALU.mult, accum_out=f[:, t:t + 1])
                        link(ins)
                    start2 += NB * TT // TURN
                link.base, link.n = start2, 0
                link(nc.vector.tensor_tensor(posf[:, :], posf[:, :], rank[:, :], ALU.add))
                nc.vector.tensor_copy(posi[:, :], posf[:, :]).then_inc(s_pos, 1)


def phase_sort(nc, sems, a, d):
    with ExitStack() as mem:
        def sb(name, shape, dt=F32):
            return mem.enter_context(nc.sbuf_tensor("s_" + name, shape, dt))

        def sem(name):
            return sems.new("s_" + name)

        pos = sb("pos", [P, B * N // P], I32)
        idx = sb("idx", [P, 2, TT], I32)
        rows = sb("rows", [P, 2, TT, C])
        pos_in = sem("pos_in")
        marks = sem("marks")
        rows_in = [sem(f"rows_in{h}") for h in range(2)]
        rows_out = [sem(f"rows_out{h}") for h in range(2)]
        rows_free = sem("rows_free")
        idx_set = sem("idx_set")
        xh_v = d.xh.rearrange("(n t p) c -> n p t c", t=TT, p=P)
        TURNS = N // P // TT

        h = sb("h", [P, B, HROWS, WP])
        acc = sb("acc", [P, SN])
        g = sb("g", [P, B, SN])
        w = sb("w", [P, KS * KS])
        bias = sb("bias", [P, 1])
        cleared = sem("cleared")
        feat_in = sem("feat_in")
        dv = sem("dv")
        s_acc = sem("s_acc")
        s_g = sem("s_g")
        s_sum = sem("s_sum")
        stored = sem("stored")
        BANDS = H // ROWS

        with nc.Block() as block:
            @block.sync
            def _(sp):
                sp.dma_start(pos[:, :], d.pos).then_inc(pos_in, 16)
                sp.wait_ge(cleared, 1)
                with nc.allow_non_contiguous_dma("small constants"):
                    for j in range(BANDS):
                        sp.dma_start(w[j * TDF:(j + 1) * TDF, :],
                                     a["L0_conv_dw_w"][HID:HID + TDF].rearrange("c o y x -> c (o y x)")).then_inc(feat_in, 16)
                        sp.dma_start(bias[j * TDF:(j + 1) * TDF, :],
                                     a["L0_conv_dw_b"][HID:HID + TDF].rearrange("(c o) -> c o", o=1)).then_inc(feat_in, 16)
                        for b in range(B):
                            lo = j * ROWS * W
                            sp.dma_start(h[j * TDF:(j + 1) * TDF, b, :, PADY:PADY + W],
                                         d.td[b, :, lo:lo + HROWS * W].rearrange("c (y x) -> c y x", x=W)).then_inc(feat_in, 16)
                with sp.Fori(0, TURNS // 2) as ii:
                    for half in range(2):
                        i = ii * 2 + half
                        sp.wait_ge(rows_free, i + 1)
                        sp.dma_start(rows[:, half, :, :],
                                     xh_v[bass.ds(i, 1)].rearrange("a p t c -> (a p) t c")).then_inc(rows_in[half], 16)
                sp.wait_ge(s_sum, B)
                for j in range(BANDS):
                    for b in range(B):
                        sp.dma_start(d.tdc[b, :, j * SN:(j + 1) * SN], g[j * TDF:(j + 1) * TDF, b, :]).then_inc(stored, 16)
                sp.wait_ge(stored, 16 * B * BANDS)

            @block.gpsimd
            def _(gp):
                gp.sem_inc(rows_free, 2)
                gp.wait_ge(pos_in, 16)

                def send(ii, half):
                    i = ii * 2 + half
                    nc.gpsimd.tensor_copy(idx[:, half, :], at(pos, i * TT, TT)).then_inc(idx_set, 1)
                    gp.wait_ge(idx_set, i + 1)
                    gp.wait_ge(rows_in[half], ii * 16 + 16)
                    gp.sem_inc(marks, 1)
                    for t in range(TT):
                        gp.indirect_dma_start(d.xs[:, :], bass.IndirectOffsetOnAxis(ap=idx[:, half, t:t + 1], axis=0),
                                              rows[:, half, t, :], None).then_inc(rows_out[half], 16)

                def sent(ii, half):
                    gp.wait_ge(rows_out[half], ii * (16 * TT) + 16 * TT)
                    gp.sem_inc(rows_free, 1)

                send(0, 0)
                with gp.Fori(0, TURNS // 2 - 1) as ii:
                    send(ii, 1)
                    sent(ii, 0)
                    send(ii + 1, 0)
                    sent(ii, 1)
                send(TURNS // 2 - 1, 1)
                sent(TURNS // 2 - 1, 0)
                sent(TURNS // 2 - 1, 1)

            @block.scalar
            def _(act):
                for b in range(B):
                    act.wait_ge(s_acc, b + 1)
                    nc.scalar.activation(g[:, b, :], acc[:, :], ACT.Gelu, bias=bias[:, 0:1]).then_inc(s_g, 1)

            @block.vector
            def _(ve):
                link = Link(ve, dv)
                nc.vector.memset(h[:, :, :, :], 0.0).then_inc(cleared, 1)
                ve.wait_ge(feat_in, 16 * BANDS * (2 + B))
                for b in range(B):
                    for n, (y, x) in enumerate(ALL_TAPS):
                        view = h[:, b, y:y + ROWS, x:x + W]
                        out = acc[:, :].rearrange("p (y x) -> p y x", x=W)
                        if n == 0:
                            link(nc.vector.tensor_scalar(out, view, w[:, 0:1], None, ALU.mult))
                        elif n < len(ALL_TAPS) - 1:
                            link(nc.vector.scalar_tensor_tensor(out, view, w[:, n:n + 1], out, ALU.mult, ALU.add))
                        else:
                            nc.vector.scalar_tensor_tensor(out, view, w[:, n:n + 1], out, ALU.mult,
                                                           ALU.add).then_inc(s_acc, 1)
                    ve.wait_ge(s_g, b + 1)
                    nc.vector.tensor_tensor(g[:, b, :].rearrange("p (y x) -> p y x", x=W),
                                            g[:, b, :].rearrange("p (y x) -> p y x", x=W),
                                            h[:, b, PADY:PADY + ROWS, PADY:PADY + W], ALU.add).then_inc(s_sum, 1)


def phase_attend(nc, sems, a, d):
    with ExitStack() as mem:
        def sb(name, shape, dt=F32):
            return mem.enter_context(nc.sbuf_tensor("a_" + name, shape, dt))

        def ps(name, shape, dt=F32):
            return mem.enter_context(nc.psum_tensor("a_" + name, shape, dt))

        def sem(name):
            return sems.new("a_" + name)

        G = B * N // GS
        QT = GS // P
        SCALE = float(HD) ** -0.5
        ident = sb("ident", [P, P])
        ones = sb("ones", [1, P])
        g1 = sb("g1", [KC, 2])
        b1 = sb("b1", [KC, 2])
        b1w = sb("b1w", [KC, 2, P])
        wqk = sb("wqk", [KC, 2, 4, P])
        wqkg = sb("wqkg", [KC, 2, 4, P])
        wv = sb("wv", [KC, 2, C])
        wvg = sb("wvg", [KC, 2, C])
        wp = sb("wp", [KC, 2, C])
        bqk0 = sb("bqk0", [P, 4])
        bqk = sb("bqk", [P, 4])
        brow = sb("brow", [1, 2 * C])
        bv = sb("bv", [P, C])
        bp = sb("bp", [P, C])

        xs = sb("xs", [P, 2, QT, C])
        xT = sb("xT", [KC, 2, GS])
        qk = sb("qk", [P, 2, 4, GS])
        V = sb("V", [P, 2, QT, C])
        mxs = sb("mxs", [P, 2, QT])
        nmx = sb("nmx", [P, 2, QT])
        e = sb("e", [P, 2, QT, GS])
        esum = sb("esum", [P, QT, HEADS])
        erec = sb("erec", [P, QT, HEADS])
        eT = sb("eT", [P, 2, QT, GS])
        o = sb("o", [P, QT, C])
        oT = sb("oT", [KC, 2, GS])
        y = sb("y", [P, QT, C])

        pX = ps("pX", [KC, 2, GS])
        pQK = ps("pQK", [P, 4, GS])
        pS = ps("pS", [P, 2, QT, GS])
        pT = ps("pT", [P, QT, GS])
        pO = ps("pO", [P, 512])
        pM = ps("pM", [P, 512])
        oV = pO[:, 0:QT * C].rearrange("p (t h d) -> p t h d", t=QT, h=HEADS)
        mV = pM[:, 0:QT * C].rearrange("p (t c) -> p t c", t=QT)
        mT = pM[0:KC, :].rearrange("p (k n) -> p k n", k=2)

        made, con, cleared = sem("made"), sem("con"), sem("cleared")
        pre_pe, pre_dv = sem("pre_pe"), sem("pre_dv")
        dv = sem("dv")
        xs_in = [sem(f"xs_in{h}") for h in range(2)]
        pos = sb("pos", [P, B * N // P], I32)
        idx = sb("idx", [P, 2, TT], I32)
        rows = sb("rows", [P, 2, TT, C])
        pos_in = sem("pos_in")
        marks = sem("marks")
        rows_in = [sem(f"rows_in{h}") for h in range(2)]
        rows_out = [sem(f"rows_out{h}") for h in range(2)]
        idx_set = sem("idx_set")
        s_sorted = sem("s_sorted")
        s_X = sem("s_X")
        s_xc = sem("s_xc")
        s_QK = sem("s_QK")
        s_qk = sem("s_qk")
        s_V = sem("s_V")
        s_v = sem("s_v")
        s_S = sem("s_S")
        s_m = sem("s_m")
        s_E = sem("s_E")
        s_T = sem("s_T")
        s_tc = sem("s_tc")
        s_O = sem("s_O")
        s_o = sem("s_o")
        s_OT = sem("s_OT")
        s_oc = sem("s_oc")
        s_Y = sem("s_Y")
        s_y = sem("s_y")
        o_y = sem("o_y")

        xs_v = d.xs.rearrange("(g t p) c -> g p t c", t=QT, p=P)
        y_v = d.aca.rearrange("(g t p) c -> g p t c", t=QT, p=P)
        xh_v = d.xh.rearrange("(n t p) c -> n p t c", t=TT, p=P)

        def head(g, h):
            return g * HEADS + (h + 1 + HEADS)

        with nc.Block() as block:
            @block.sync
            def _(sp):
                def con_in(dst, src):
                    sp.dma_start(dst, src).then_inc(con, 16)

                wqkv, wb = a["L0_conv_wqkv_w"], a["L0_conv_wqkv_b"]
                sp.wait_ge(cleared, 2)
                with nc.allow_non_contiguous_dma("small constants"):
                    for k in range(2):
                        for w in range(2):
                            con_in(wqk[:, k, 2 * w:2 * w + 2, :].rearrange("p m (u e) -> p (m u) e", u=2)[:, :, 0:HD],
                                   wqkv[k * KC:(k + 1) * KC, w * C:(w + 1) * C].rearrange("p (h e) -> p h e", h=HEADS))
                    for u in range(2):
                        con_in(bqk0[64 * u:64 * u + HD, :],
                               wb[0:2 * C].rearrange("(m u e) -> u e m", u=2, e=HD)[u])
                    con_in(wv[:, :, :], wqkv[:, 2 * C:3 * C].rearrange("(k p) n -> p k n", k=2))
                    con_in(wp[:, :, :], a["L0_conv_proj_w"].rearrange("(k p) n -> p k n", k=2))
                    con_in(g1[:, :], a["L0_conv_g1"].rearrange("(k p) -> p k", k=2))
                    con_in(b1[:, :], a["L0_conv_b1"].rearrange("(k p) -> p k", k=2))
                    con_in(brow[:, 0:C], wb[2 * C:3 * C].rearrange("(a n) -> a n", a=1))
                    con_in(brow[:, C:2 * C], a["L0_conv_proj_b"].rearrange("(a n) -> a n", a=1))
                sp.sem_inc(o_y, 16)

                def load(g, half):
                    sp.wait_ge(s_X, g + 1)
                    sp.dma_start(xs[:, half, :, :], xs_v[bass.ds(g, 1)]
                                 .rearrange("a p t c -> (a p) t c")).then_inc(xs_in[half], 16)

                def store(g):
                    sp.wait_ge(s_y, g + 2)
                    sp.dma_start(y_v[bass.ds(g, 1)].rearrange("a p t c -> (a p) t c"), y[:, :, :]).then_inc(o_y, 16)

                LAG = 4
                for g in range(LAG):
                    load(g, g % 2)
                for b in range(B):
                    if b == 1:
                        sp.wait_ge(s_sorted, 1)
                    with sp.Fori(max(b * G // B, LAG) // 2, (b + 1) * G // B // 2) as gg:
                        for half in range(2):
                            load(gg * 2 + half, half)
                            store(gg * 2 + (half - LAG))
                for g in range(G - LAG, G):
                    store(g)
                sp.wait_ge(o_y, 16 * G + 16)

            @block.gpsimd
            def _(gp):
                nc.gpsimd.memset(ident[:, :], 0.0).then_inc(made, 1)
                nc.gpsimd.memset(ones[:, :], 1.0).then_inc(made, 1)
                gp.wait_ge(made, 2)
                nc.gpsimd.affine_select(out=ident[:, :], in_=ident[:, :], compare_op=ALU.not_equal, fill=1.0,
                                        base=0, pattern=[[-1, P]], channel_multiplier=1).then_inc(made, 1)

                TURNS = N // P // TT

                def fetch(ii, half):
                    gp.dma_start(rows[:, half, :, :], xh_v[bass.ds(ii * 2 + (TURNS + half), 1)]
                                 .rearrange("a p t c -> (a p) t c")).then_inc(rows_in[half], 16)

                def send(ii, half):
                    nc.gpsimd.tensor_copy(idx[:, half, :], at(pos, (ii * 2 + (TURNS + half)) * TT, TT))\
                        .then_inc(idx_set, 1)
                    gp.wait_ge(idx_set, ii * 2 + (half + 1))
                    gp.wait_ge(rows_in[half], ii * 16 + 16)
                    gp.sem_inc(marks, 1)
                    for t in range(TT):
                        gp.indirect_dma_start(d.xs[:, :], bass.IndirectOffsetOnAxis(ap=idx[:, half, t:t + 1], axis=0),
                                              rows[:, half, t, :], None).then_inc(rows_out[half], 16)

                def sent(ii, half):
                    gp.wait_ge(rows_out[half], ii * (16 * TT) + 16 * TT)

                gp.dma_start(pos[:, :], d.pos).then_inc(pos_in, 16)
                gp.wait_ge(pos_in, 16)
                fetch(0, 0)
                fetch(0, 1)
                send(0, 0)
                with gp.Fori(0, TURNS // 2 - 1) as ii:
                    send(ii, 1)
                    sent(ii, 0)
                    fetch(ii + 1, 0)
                    send(ii + 1, 0)
                    sent(ii, 1)
                    fetch(ii + 1, 1)
                send(TURNS // 2 - 1, 1)
                sent(TURNS // 2 - 1, 0)
                sent(TURNS // 2 - 1, 1)
                gp.sem_inc(s_sorted, 1)

            @block.tensor
            def _(te):
                te.sem_inc(s_X, 2)
                te.sem_inc(s_T, HEADS)
                te.sem_inc(s_O, HEADS)
                te.wait_ge(made, 3)
                te.wait_ge(con, 16 * 12)
                te.wait_ge(pre_dv, 1)
                for m in range(4):
                    for k in range(2):
                        nc.tensor.matmul(pQK[:, 0, m:m + 1], wqk[:, k, m, :], b1[:, k:k + 1], start=(k == 0),
                                         stop=(k == 1)).then_inc(pre_pe, 1)
                for k in range(2):
                    nc.tensor.matmul(pO[:, 0:C], b1w[:, k, :], wv[:, k, :], start=(k == 0), stop=False)
                nc.tensor.matmul(pO[:, 0:C], ones[:, :], brow[:, 0:C], start=False, stop=True).then_inc(pre_pe, 1)
                nc.tensor.matmul(pM[:, 0:C], ones[:, :], brow[:, C:2 * C], start=True, stop=True).then_inc(pre_pe, 1)
                te.wait_ge(pre_dv, 2)

                def rows_turned(gg, half, f):
                    te.wait_ge(xs_in[half], gg * 16 + 16)
                    te.wait_ge(s_xc, f + 1)
                    for t in range(QT):
                        for k in range(2):
                            mm = nc.tensor.transpose(pX[:, k, t * P:(t + 1) * P], xs[:, half, t, k * KC:(k + 1) * KC],
                                                     ident[:, :])
                    mm.then_inc(s_X, 1)

                def queries_keys(f):
                    te.wait_ge(s_xc, f + 2)
                    te.wait_ge(s_qk, f + 1)
                    for m in range(4):
                        for k in range(2):
                            mm = nc.tensor.matmul(pQK[:, m, :], wqkg[:, k, m, :], xT[:, k, :], start=(k == 0),
                                                  stop=(k == 1))
                    mm.then_inc(s_QK, 1)

                def values(f, first=False):
                    if not first:
                        te.wait_ge(s_y, f)
                    for t in range(QT):
                        for k in range(2):
                            mm = nc.tensor.matmul(mV[:, t, :], xT[:, k, t * P:(t + 1) * P], wvg[:, k, :],
                                                  start=(k == 0), stop=(k == 1))
                    mm.then_inc(s_V, 1)

                def scores(g, half, h):
                    te.wait_ge(s_E, head(g, h - 2))
                    lo = 64 * (h % 2)
                    for t in range(QT):
                        mm = nc.tensor.matmul(pS[:, h % 2, t, :], qk[lo:lo + HD, half, h // 2, t * P:(t + 1) * P],
                                              qk[lo:lo + HD, half, 2 + h // 2, :], start=True, stop=True)
                    mm.then_inc(s_S, 1)

                def turned(g, half, h):
                    te.wait_ge(s_E, head(g, h))
                    te.wait_ge(s_tc, head(g, h - 1))
                    for t in range(QT):
                        for k in range(QT):
                            mm = nc.tensor.transpose(pT[:, k, t * P:(t + 1) * P], e[:, h % 2, t, k * P:(k + 1) * P],
                                                     ident[:, :])
                    mm.then_inc(s_T, 1)

                def outputs(g, half, h):
                    te.wait_ge(s_tc, head(g, h))
                    if h == 0:
                        te.wait_ge(s_o, g + 1)
                        te.wait_ge(s_v, g + 2)
                    for t in range(QT):
                        for k in range(QT):
                            mm = nc.tensor.matmul(oV[:, t, h, :], eT[:, h % 2, k, t * P:(t + 1) * P],
                                                  V[:, half, k, h * HD:(h + 1) * HD], start=(k == 0), stop=(k == 1))
                    mm.then_inc(s_O, 1)

                def outputs_turned(g):
                    te.wait_ge(s_o, g + 2)
                    if not (isinstance(g, int) and g == G - 1):
                        te.wait_ge(s_v, g + 3)
                    for t in range(QT):
                        for k in range(2):
                            mm = nc.tensor.transpose(mT[:, k, t * P:(t + 1) * P], o[:, t, k * KC:(k + 1) * KC],
                                                     ident[:, :])
                    mm.then_inc(s_OT, 1)

                def project(g):
                    te.wait_ge(s_oc, g + 1)
                    for t in range(QT):
                        for k in range(2):
                            mm = nc.tensor.matmul(mV[:, t, :], oT[:, k, t * P:(t + 1) * P], wp[:, k, :],
                                                  start=(k == 0), stop=(k == 1))
                    mm.then_inc(s_Y, 1)

                def turn(gg, half, before, after):
                    g = gg * 2 + half
                    if after:
                        rows_turned(gg + half, 1 - half, g + 1)
                    te.wait_ge(s_qk, g + 2)
                    scores(g, half, 0)
                    if before:
                        outputs(g - 1, 1 - half, HEADS - 1)
                    scores(g, half, 1)
                    if before:
                        outputs_turned(g - 1)
                    if after:
                        queries_keys(g + 1)
                    if before:
                        project(g - 1)
                    turned(g, half, 0)
                    scores(g, half, 2)
                    turned(g, half, 1)
                    outputs(g, half, 0)
                    scores(g, half, 3)
                    outputs(g, half, 1)
                    turned(g, half, 2)
                    if after:
                        values(g + 1)
                    outputs(g, half, 2)
                    turned(g, half, 3)

                rows_turned(0, 0, 0)
                queries_keys(0)
                values(0, first=True)
                turn(0, 0, False, True)
                turn(0, 1, True, True)
                with te.Fori(1, G // 2 - 1) as gg:
                    turn(gg, 0, True, True)
                    turn(gg, 1, True, True)
                turn(G // 2 - 1, 0, True, True)
                turn(G // 2 - 1, 1, True, False)
                outputs(G - 1, 1, HEADS - 1)
                outputs_turned(G - 1)
                project(G - 1)

            @block.scalar
            def _(act):
                act.sem_inc(s_xc, 1)
                act.sem_inc(s_E, HEADS)
                act.sem_inc(s_tc, HEADS)

                def front(f):
                    act.wait_ge(s_X, f + 3)
                    act.wait_ge(s_V, f + 1)
                    nc.scalar.activation(xT[:, :, :], pX[:, :, :], ACT.Copy).then_inc(s_xc, 1)

                def expo(g, h):
                    act.wait_ge(s_m, g * HEADS + (h + 1))
                    act.wait_ge(s_T, head(g, h - 2))
                    for t in range(QT):
                        ins = nc.scalar.activation(e[:, h % 2, t, :], pS[:, h % 2, t, :], ACT.Exp,
                                                   bias=nmx[:, h % 2, t:t + 1], scale=SCALE,
                                                   accum_out=esum[:, t, h:h + 1])
                    ins.then_inc(s_E, 1)

                def copied(g, h):
                    act.wait_ge(s_T, head(g, h))
                    act.wait_ge(s_O, head(g, h - 2))
                    nc.scalar.activation(eT[:, h % 2, :, :], pT[:, :, :], ACT.Copy).then_inc(s_tc, 1)

                def turned_back(g):
                    act.wait_ge(s_OT, g + 1)
                    nc.scalar.activation(oT[:, :, :], mT, ACT.Copy).then_inc(s_oc, 1)

                def turn(g, before, after):
                    if after:
                        front(g + 1)
                    expo(g, 0)
                    if before:
                        turned_back(g - 1)
                    expo(g, 1)
                    copied(g, 0)
                    expo(g, 2)
                    copied(g, 1)
                    expo(g, 3)
                    copied(g, 2)
                    copied(g, 3)

                front(0)
                turn(0, False, True)
                with act.Fori(1, G - 1) as g:
                    turn(g, True, True)
                turn(G - 1, True, False)
                turned_back(G - 1)

            @block.vector
            def _(ve):
                link = Link(ve, dv)
                ve.sem_inc(s_V, 1)
                nc.vector.memset(wqk[:, :, :, :], 0.0).then_inc(cleared, 1)
                nc.vector.memset(bqk0[:, :], 0.0).then_inc(cleared, 1)
                ve.wait_ge(con, 16 * 12)
                nc.vector.tensor_copy(b1w[:, :, :], b1[:, :].unsqueeze(2).to_broadcast([KC, 2, P])).then_inc(pre_dv, 1)
                for k in range(2):
                    nc.vector.tensor_scalar(wqkg[:, k, :, :], wqk[:, k, :, :], g1[:, k:k + 1], None, ALU.mult)
                    nc.vector.tensor_scalar(wvg[:, k, :], wv[:, k, :], g1[:, k:k + 1], None, ALU.mult)
                ve.wait_ge(pre_pe, 10)
                nc.vector.tensor_tensor(bqk[:, :], pQK[:, 0, 0:4], bqk0[:, :], ALU.add)
                nc.vector.tensor_copy(bv[:, :], pO[:, 0:C])
                link(nc.vector.tensor_copy(bp[:, :], pM[:, 0:C]))
                ve.sem_inc(pre_dv, 1)
                ve.sem_inc(s_qk, 1)
                ve.sem_inc(s_v, 1)
                ve.sem_inc(s_o, 1)
                ve.sem_inc(s_y, 1)

                def queries_keys(f, half):
                    ve.wait_ge(s_QK, f + 1)
                    nc.vector.tensor_tensor(qk[:, half, :, :], pQK[:, :, :],
                                            bqk[:, :].unsqueeze(2).to_broadcast([P, 4, GS]), ALU.add).then_inc(s_qk, 1)

                def values(f, half):
                    ve.wait_ge(s_V, f + 2)
                    nc.vector.tensor_tensor(V[:, half, :, :], mV, bv[:, :].unsqueeze(1).to_broadcast([P, QT, C]),
                                            ALU.add).then_inc(s_v, 1)

                def maxima(g, h):
                    ve.wait_ge(s_S, g * HEADS + (h + 1))
                    link(nc.vector.tensor_reduce(mxs[:, h % 2, :], pS[:, h % 2, :, :], AX.X, ALU.max))
                    nc.vector.tensor_scalar(nmx[:, h % 2, :], mxs[:, h % 2, :], -SCALE, None, ALU.mult).then_inc(s_m, 1)

                def projected(g):
                    ve.wait_ge(s_Y, g + 1)
                    ve.wait_ge(o_y, g * 16 + 16)
                    nc.vector.tensor_tensor(y[:, :, :], mV, bp[:, :].unsqueeze(1).to_broadcast([P, QT, C]),
                                            ALU.add).then_inc(s_y, 1)

                def turn(gg, half, before, after):
                    g = gg * 2 + half
                    link.base, link.n = g * 5 + 1, 0
                    maxima(g, 0)
                    maxima(g, 1)
                    if after:
                        queries_keys(g + 1, 1 - half)
                    if before:
                        projected(g - 1)
                    maxima(g, 2)
                    maxima(g, 3)
                    if after:
                        values(g + 1, 1 - half)
                    ve.wait_ge(s_E, head(g, 3))
                    link(nc.vector.reciprocal(erec[:, :, :], esum[:, :, :]))
                    ve.wait_ge(s_O, head(g, 3))
                    nc.vector.tensor_tensor(o[:, :, :].rearrange("p t (h e) -> p t h e", h=HEADS), oV,
                                            erec[:, :, :].unsqueeze(3).to_broadcast([P, QT, HEADS, HD]),
                                            ALU.mult).then_inc(s_o, 1)

                queries_keys(0, 0)
                values(0, 0)
                turn(0, 0, False, True)
                turn(0, 1, True, True)
                with ve.Fori(1, G // 2 - 1) as gg:
                    turn(gg, 0, True, True)
                    turn(gg, 1, True, True)
                turn(G // 2 - 1, 0, True, True)
                turn(G // 2 - 1, 1, True, False)
                projected(G - 1)


ROWS = 16
STRIPS = B * H // ROWS
HROWS = ROWS + 2 * PADY
WP = W + 2 * PADY
CH = HID // P
SN = ROWS * W
FN = 4 * W
GR = HROWS // 4
CB = 64
ALL_TAPS = [(y, x) for y in range(KS) for x in range(KS)]
PE_SHARE = [6, 6, 9, 9, 8, 8]
HN = SN // 2


def phase_ffn(nc, sems, a, d):
    with ExitStack() as mem:
        def sb(name, shape, dt=F32):
            return mem.enter_context(nc.sbuf_tensor("f_" + name, shape, dt))

        def ps(name, shape, dt=F32):
            return mem.enter_context(nc.psum_tensor("f_" + name, shape, dt))

        def sem(name):
            return sems.new("f_" + name)

        ident = sb("ident", [P, P])
        ones = sb("ones", [1, P])
        g2 = sb("g2", [KC, 2])
        b2 = sb("b2", [KC, 2])
        w1 = sb("w1", [KC + 1, 2, HID])
        dww = sb("dww", [P, CH, KS * KS])
        dwb = sb("dwb", [P, CH])
        diag = sb("diag", [P, sum(PE_SHARE), P])
        w2 = sb("w2", [P, CH, C])
        w2t = sb("w2t", [TDF + 1, C])
        g3 = sb("g3", [P, C])
        b3 = sb("b3", [P, C])
        wc = sb("wc", [KC, 2, CB])
        wcr = sb("wcr", [CB, C])
        bc = sb("bc", [CB, 1])
        pos = sb("pos", [P, B * N // P], I32)
        idx = sb("idx", [P, ROWS], I32)

        xt = sb("xt", [KC + 1, 2, HROWS * W])
        h = sb("h", [P, 3, HROWS, WP])
        g = sb("g", [P, 2, SN])
        hs = sb("hs", [P, CH, SN])
        tds = sb("tds", [TDF + 1, SN])
        F = sb("F", [P, ROWS, C])
        brow = F[0:1, 0:HID // C, :].rearrange("a r c -> a (r c)")
        st6 = sb("st6", [P, ROWS, 6])
        mv = sb("mv", [P, ROWS, 2])
        dev = sb("dev", [P, ROWS])
        nmu = sb("nmu", [P, ROWS])
        aca = sb("aca", [P, ROWS, C])
        x1 = sb("x1", [KC, 2, SN // 2])
        res = sb("res", [KC, 2, SN // 2])
        xc = sb("xc", [CB, 2, FN])

        p1 = ps("p1", [P, 2, FN])
        pC = ps("pC", [P, 2, HN])
        p2 = ps("p2", [P, 2, 512])

        made, con, pre_dv, pre_pe, cleared = (sem(n) for n in ("made", "con", "pre_dv", "pre_pe", "cleared"))
        dv = sem("dv")
        marks = sem("marks")
        xt_in = sem("xt_in")
        tds_in = sem("tds_in")
        res_in = sem("res_in")
        aca_in = sem("aca_in")
        s_fc1 = sem("s_fc1")
        s_g = sem("s_g")
        s_tap = sem("s_tap")
        s_acc = sem("s_acc")
        s_g2 = sem("s_g2")
        s_add = sem("s_add")
        s_p2 = sem("s_p2")
        s_p2f = sem("s_p2f")
        s_st = sem("s_st")
        s_dev = sem("s_dev")
        s_rs = sem("s_rs")
        s_n = sem("s_n")
        s_ln = sem("s_ln")
        s_x1c = sem("s_x1c")
        s_x1 = sem("s_x1")
        o_xc = [sem(f"o_xc{k}") for k in range(2)]
        o_x1 = sem("o_x1")
        idx_set = sem("idx_set")
        s_lg = sem("s_lg")

        xt_v = d.xt.rearrange("b c n -> (b c) n")
        PER_IMAGE = H // ROWS
        USES = 20

        def split(s):
            return (s // PER_IMAGE, s % PER_IMAGE)

        with nc.Block() as block:
            @block.sync
            def _(sp):
                def cin(dst, src):
                    sp.dma_start(dst, src).then_inc(con, 16)

                sp.wait_ge(cleared, 1)
                with nc.allow_non_contiguous_dma("small constants"):
                    cin(hs[0:KC, 0:2, 0:HID], a["L0_conv_fc1_w"].rearrange("(k p) n -> p k n", k=2))
                    cin(g2[:, :], a["L0_conv_g2"].rearrange("(k p) -> p k", k=2))
                    cin(b2[:, :], a["L0_conv_b2"].rearrange("(k p) -> p k", k=2))
                    cin(brow, a["L0_conv_fc1_b"].rearrange("(a n) -> a n", a=1))
                    cin(dww[:, :, :], a["L0_conv_dw_w"][0:HID].rearrange("(c p) o y x -> p c (o y x)", p=P))
                    cin(dwb[:, :], a["L0_conv_dw_b"][0:HID].rearrange("(c p) -> p c", p=P))
                    cin(w2[:, :, :], a["L0_conv_fc2_w"][0:HID].rearrange("(c p) n -> p c n", p=P))
                    cin(w2t[0:TDF, :], a["L0_conv_fc2_w"][HID:HID + TDF])
                    cin(w2t[TDF:TDF + 1, :], a["L0_conv_fc2_b"].rearrange("(a n) -> a n", a=1))
                    cin(g3[:, :], a["L0_conv_g3"].rearrange("(a n) -> a n", a=1).broadcast_to([P, C]))
                    cin(b3[:, :], a["L0_conv_b3"].rearrange("(a n) -> a n", a=1).broadcast_to([P, C]))
                    cin(wcr[:, :], a["L1_conv_w1"])
                    cin(bc[:, :], a["L1_conv_b1"].rearrange("(c o) -> c o", o=1))
                    cin(pos[:, :], d.pos)

                def load_xt(b, j, s):
                    sp.dma_start(xt[0:KC, 0, :], d.xt[bass.ds(b, 1), 0:KC, bass.ds(j * SN, HROWS * W)]
                                 .rearrange("b c n -> (b c) n")).then_inc(xt_in, 16)
                    sp.dma_start(xt[:, 1, :], d.xt[bass.ds(b, 1), KC:C + 1, bass.ds(j * SN, HROWS * W)]
                                 .rearrange("b c n -> (b c) n")).then_inc(xt_in, 16)

                def tail_loads(b, j, t):
                    if not isinstance(t, int) or t:
                        sp.wait_ge(s_p2, t * USES - (USES - 8))
                    sp.dma_start(tds[0:TDF, :], d.tdc[bass.ds(b, 1), :, bass.ds(j * SN, SN)]
                                 .rearrange("b c n -> (b c) n")).then_inc(tds_in, 16)

                def load_res(b, j, t, half):
                    if not isinstance(t, int) or t or half:
                        sp.wait_ge(s_x1, t * 2 + half)
                    sp.dma_start(res[:, :, :], d.res[bass.ds(b, 1), :, bass.ds(j * SN + half * (SN // 2), SN // 2)]
                                 .rearrange("b (k p) n -> (b p) k n", k=2)).then_inc(res_in, 16)

                def tail_stores(b, j, t, half):
                    sp.wait_ge(s_x1, t * 2 + (half + 1))
                    sp.dma_start(d.x1[bass.ds(b, 1), :, bass.ds(j * SN + half * (SN // 2), SN // 2)]
                                 .rearrange("b (k p) n -> (b p) k n", k=2), x1[:, :, :]).then_inc(o_x1, 16)
                    if half == 0:
                        load_res(b, j, t, 1)
                    for q in range(2):
                        sp.wait_ge(s_p2f, t * USES + (8 + 6 * half + 4 + q + 3))
                        sp.dma_start(d.xc[bass.ds(b, 1), :, bass.ds(j * SN + (2 * half + q) * FN, FN)]
                                     .rearrange("b c n -> (b c) n"), xc[:, q, :]).then_inc(o_xc[q], 16)

                sp.sem_inc(o_x1, 16)
                for k in range(2):
                    sp.sem_inc(o_xc[k], 16)
                load_xt(0, 0, 0)
                sp.wait_ge(s_fc1, CH * GR)
                load_xt(0, 1, 1)

                def turn(t, more):
                    bt, jt = (t // PER_IMAGE, t % PER_IMAGE)
                    tail_loads(bt, jt, t)
                    load_res(bt, jt, t, 0)
                    if more:
                        sp.wait_ge(s_fc1, t * (CH * GR) + 2 * CH * GR)
                        load_xt((t + 2) // PER_IMAGE, (t + 2) % PER_IMAGE, None)
                    tail_stores(bt, jt, t, 0)
                    tail_stores(bt, jt, t, 1)

                turn(0, True)
                with sp.Fori(1, STRIPS - 2) as t:
                    turn(t, True)
                for t in (STRIPS - 2, STRIPS - 1):
                    turn(t, False)
                sp.wait_ge(o_x1, 32 * STRIPS + 16)
                for k in range(2):
                    sp.wait_ge(o_xc[k], 16 * 2 * STRIPS + 16)

            @block.gpsimd
            def _(gp):
                nc.gpsimd.memset(ident[:, :], 0.0).then_inc(made, 1)
                nc.gpsimd.memset(ones[:, :], 1.0).then_inc(made, 1)
                gp.wait_ge(made, 2)
                nc.gpsimd.affine_select(out=ident[:, :], in_=ident[:, :], compare_op=ALU.not_equal, fill=1.0,
                                        base=0, pattern=[[-1, P]], channel_multiplier=1).then_inc(made, 1)
                nc.gpsimd.memset(tds[:, :], 1.0).then_inc(cleared, 1)
                gp.sem_inc(s_add, 2)
                gp.wait_ge(con, 16 * 14)

                def add(s, c):
                    n = s * CH + c
                    gp.wait_ge(s_g2, n * 2 + 4)
                    if not isinstance(s, int) or s >= 1:
                        gp.wait_ge(s_p2, (s - 1) * USES + 8)
                    view = g[:, c % 2, :].rearrange("p (y x) -> p y x", x=W)
                    nc.gpsimd.tensor_tensor(hs[:, c, :].rearrange("p (y x) -> p y x", x=W), view,
                                            h[:, c % 3, PADY:PADY + ROWS, PADY:PADY + W], ALU.add).then_inc(s_add, 1)

                def gathers(t, lo, hi):
                    if lo == 0:
                        nc.gpsimd.tensor_copy(idx[:, :], at(pos, t * ROWS, ROWS)).then_inc(idx_set, 1)
                        gp.wait_ge(idx_set, t + 1)
                        gp.sem_inc(marks, 1)
                    for r in range(lo, hi):
                        gp.indirect_dma_start(aca[:, r, :], None, d.aca[:, :],
                                              bass.IndirectOffsetOnAxis(ap=idx[:, r:r + 1], axis=0)).then_inc(aca_in, 16)

                def finish(t):
                    gp.wait_ge(s_n, t + 1)
                    nc.gpsimd.tensor_tensor(F[:, :, :], F[:, :, :], g3[:, :].unsqueeze(1).to_broadcast([P, ROWS, C]),
                                            ALU.mult).then_inc(s_lg, 1)
                    gp.wait_ge(s_lg, t * 2 + 1)
                    nc.gpsimd.tensor_tensor(F[:, :, :], F[:, :, :], b3[:, :].unsqueeze(1).to_broadcast([P, ROWS, C]),
                                            ALU.add).then_inc(s_lg, 1)
                    gp.wait_ge(s_lg, t * 2 + 2)
                    gp.wait_ge(aca_in, t * (16 * ROWS) + 16 * ROWS)
                    nc.gpsimd.tensor_tensor(F[:, :, :], F[:, :, :], aca[:, :, :], ALU.add).then_inc(s_ln, 1)

                def add_res(t, half):
                    gp.wait_ge(res_in, t * 32 + 16 * (half + 1))
                    gp.wait_ge(s_x1c, t * 8 + 4 * (half + 1))
                    nc.gpsimd.tensor_tensor(x1[:, :, :], x1[:, :, :], res[:, :, :], ALU.add).then_inc(s_x1, 1)

                def turn(s, tail):
                    t = s - 1
                    if tail:
                        if not isinstance(s, int) or s > 1:
                            gp.wait_ge(s_ln, t)
                        gathers(t, 0, 8)
                    add(s, 0)
                    if tail:
                        gathers(t, 8, 16)
                    add(s, 1)
                    if tail:
                        finish(t)
                    add(s, 2)
                    add(s, 3)
                    if tail:
                        add_res(t, 0)
                    add(s, 4)
                    if tail:
                        add_res(t, 1)
                    add(s, 5)

                turn(0, False)
                turn(1, True)
                with gp.Fori(2, STRIPS) as s:
                    turn(s, True)
                gp.wait_ge(s_ln, STRIPS - 1)
                gathers(STRIPS - 1, 0, ROWS)
                finish(STRIPS - 1)
                add_res(STRIPS - 1, 0)
                add_res(STRIPS - 1, 1)

            @block.tensor
            def _(te):
                te.wait_ge(made, 3)
                te.wait_ge(con, 16 * 14)
                for k in range(2):
                    nc.tensor.transpose(pC[0:KC, 0, k * CB:(k + 1) * CB], wcr[:, k * KC:(k + 1) * KC],
                                        ident[0:CB, 0:CB]).then_inc(pre_pe, 1)
                for o in range(2):
                    for k in range(2):
                        nc.tensor.matmul(pC[0:1, 1, 512 * o:512 * o + HID // 2], b2[:, k:k + 1],
                                         hs[0:KC, k, o * (HID // 2):(o + 1) * (HID // 2)], start=(k == 0),
                                         stop=(k == 1)).then_inc(pre_pe, 1)
                te.wait_ge(pre_dv, 1)

                def fc1(s, c):
                    if c == 0:
                        te.wait_ge(xt_in, s * 32 + 32)
                    for j in range(GR):
                        m = c * GR + j
                        te.wait_ge(s_g, s * (CH * GR) + (m + 1))
                        for k in range(2):
                            kk = KC + k
                            mm = nc.tensor.matmul(p1[:, m % 2, :], w1[0:kk, k, c * P:(c + 1) * P],
                                                  xt[0:kk, k, j * FN:(j + 1) * FN], start=(k == 0), stop=(k == 1))
                        mm.then_inc(s_fc1, 1)

                def taps(s, c, half):
                    n = s * CH + c
                    te.wait_ge(s_g, s * (CH * GR) + ((c + 1) * GR + 2))
                    te.wait_ge(s_g2, n * 2 + (half + 1))
                    at0 = sum(PE_SHARE[:c])
                    for i, (y, x) in enumerate(ALL_TAPS[:PE_SHARE[c]]):
                        for q in range(2):
                            row = 8 * half + 4 * q + y
                            mm = nc.tensor.matmul(pC[:, half, q * FN:(q + 1) * FN], diag[:, at0 + i, :],
                                                  h[:, c % 3, row:row + 4, x:x + W], start=(i == 0),
                                                  stop=(i == PE_SHARE[c] - 1))
                    mm.then_inc(s_tap, 1)

                def use(t, n):
                    te.wait_ge(s_p2f, t * USES + (n + 1))

                def fc2(t, half):
                    te.wait_ge(s_add, t * CH + CH + 2)
                    te.wait_ge(tds_in, t * 16 + 16)
                    for k in range(4 * half, 4 * half + 4):
                        use(t, k)
                        for r in range(2):
                            row = 2 * k + r
                            dst = p2[:, k % 2, r * C:(r + 1) * C]
                            for c in range(CH):
                                nc.tensor.matmul(dst, hs[:, c, row * W:(row + 1) * W], w2[:, c, :], start=(c == 0), stop=False)
                            mm = nc.tensor.matmul(dst, tds[:, row * W:(row + 1) * W], w2t[:, :], start=False, stop=True)
                        mm.then_inc(s_p2, 1)

                def turned(t, half):
                    te.wait_ge(s_ln, t + 1)
                    for k in range(4):
                        use(t, 8 + 6 * half + k)
                        q, kt = 2 * half + k // 2, k % 2
                        for r in range(4):
                            mm = nc.tensor.transpose(p2[0:KC, k % 2, r * W:(r + 1) * W],
                                                     F[:, 4 * q + r, kt * KC:(kt + 1) * KC], ident[:, :])
                        mm.then_inc(s_p2, 1)

                def first(t, half):
                    te.wait_ge(s_x1, t * 2 + (half + 1))
                    for q in range(2):
                        use(t, 8 + 6 * half + 4 + q)
                        for k in range(2):
                            mm = nc.tensor.matmul(p2[0:CB, q, :], wc[:, k, :], x1[:, k, q * FN:(q + 1) * FN],
                                                  start=(k == 0), stop=(k == 1))
                        mm.then_inc(s_p2, 1)

                def turn(s, tail, more):
                    t = s - 1
                    taps(s, 0, 1)
                    fc1(s, 2)
                    if tail:
                        fc2(t, 0)
                    taps(s, 1, 0)
                    taps(s, 1, 1)
                    if tail:
                        fc2(t, 1)
                    taps(s, 2, 0)
                    fc1(s, 3)
                    taps(s, 2, 1)
                    fc1(s, 4)
                    taps(s, 3, 0)
                    taps(s, 3, 1)
                    fc1(s, 5)
                    taps(s, 4, 0)
                    taps(s, 4, 1)
                    if more:
                        fc1(s + 1, 0)
                    if tail:
                        turned(t, 0)
                    taps(s, 5, 0)
                    taps(s, 5, 1)
                    if tail:
                        first(t, 0)
                        turned(t, 1)
                    if more:
                        fc1(s + 1, 1)
                    if tail:
                        first(t, 1)
                    if more:
                        taps(s + 1, 0, 0)

                fc1(0, 0)
                fc1(0, 1)
                taps(0, 0, 0)
                turn(0, False, True)
                with te.Fori(1, STRIPS - 1) as s:
                    turn(s, True, True)
                turn(STRIPS - 1, True, False)
                for half in range(2):
                    fc2(STRIPS - 1, half)
                for half in range(2):
                    turned(STRIPS - 1, half)
                    first(STRIPS - 1, half)

            @block.scalar
            def _(act):
                act.sem_inc(s_g, 2)
                act.sem_inc(s_g2, 2)
                act.sem_inc(s_p2f, 2)

                def gelu1(s, c):
                    act.wait_ge(s_add, s * CH + c)
                    for j in range(GR):
                        m = c * GR + j
                        act.wait_ge(s_fc1, s * (CH * GR) + (m + 1))
                        nc.scalar.activation(h[:, c % 3, 4 * j:4 * j + 4, PADY:PADY + W],
                                             p1[:, m % 2, :].rearrange("p (y x) -> p y x", x=W),
                                             ACT.Gelu).then_inc(s_g, 1)

                def gelu2(s, c, half):
                    act.wait_ge(s_acc, s * (CH * 2) + (2 * c + half + 1))
                    act.wait_ge(s_add, s * CH + (c + 1))
                    nc.scalar.activation(g[:, c % 2, half * HN:(half + 1) * HN], pC[:, half, :], ACT.Gelu,
                                         bias=dwb[:, c:c + 1]).then_inc(s_g2, 1)

                def evac(t, half):
                    for k in range(4 * half, 4 * half + 4):
                        act.wait_ge(s_p2, t * USES + (k + 1))
                        nc.scalar.activation(F[:, 2 * k:2 * k + 2, :], p2[:, k % 2, 0:2 * C]
                                             .rearrange("p (r c) -> p r c", r=2), ACT.Copy).then_inc(s_p2f, 1)

                def deviate(t):
                    act.wait_ge(s_st, t + 1)
                    nc.scalar.activation(dev[:, :], dev[:, :], ACT.Sqrt).then_inc(s_dev, 1)

                def normalise(t):
                    act.wait_ge(s_rs, t + 1)
                    for r in range(ROWS):
                        ins = nc.scalar.activation(F[:, r, :], F[:, r, :], ACT.Identity, bias=nmu[:, r:r + 1],
                                                   scale=dev[:, r:r + 1])
                    ins.then_inc(s_n, 1)

                def turned(t, half):
                    act.wait_ge(o_x1, t * 32 + 16 * (half + 1))
                    for k in range(4):
                        q, kt = k // 2, k % 2
                        act.wait_ge(s_p2, t * USES + (8 + 6 * half + k + 1))
                        nc.scalar.activation(x1[:, kt, q * FN:(q + 1) * FN], p2[0:KC, k % 2, :], ACT.Copy)\
                            .then_inc(s_x1c, 1)
                        act.wait_ge(s_x1c, t * 8 + (4 * half + k + 1))
                        act.sem_inc(s_p2f, 1)

                def first(t, half):
                    for q in range(2):
                        act.wait_ge(s_p2, t * USES + (8 + 6 * half + 4 + q + 1))
                        act.wait_ge(o_xc[q], t * 32 + 16 * (half + 1))
                        nc.scalar.activation(xc[:, q, :], p2[0:CB, q, :], ACT.Identity,
                                             bias=bc[:, 0:1]).then_inc(s_p2f, 1)

                def turn(s, tail, more):
                    t = s - 1
                    if tail:
                        gelu2(t, 5, 1)
                    gelu1(s, 2)
                    if tail:
                        evac(t, 0)
                    gelu2(s, 0, 0)
                    gelu2(s, 0, 1)
                    if tail:
                        evac(t, 1)
                    gelu2(s, 1, 0)
                    gelu1(s, 3)
                    gelu2(s, 1, 1)
                    if tail:
                        deviate(t)
                    gelu1(s, 4)
                    gelu2(s, 2, 0)
                    if tail:
                        normalise(t)
                    gelu2(s, 2, 1)
                    gelu1(s, 5)
                    gelu2(s, 3, 0)
                    gelu2(s, 3, 1)
                    if more:
                        gelu1(s + 1, 0)
                    if tail:
                        turned(t, 0)
                    gelu2(s, 4, 0)
                    gelu2(s, 4, 1)
                    if tail:
                        first(t, 0)
                        turned(t, 1)
                    if more:
                        gelu1(s + 1, 1)
                    if tail:
                        first(t, 1)
                    gelu2(s, 5, 0)

                gelu1(0, 0)
                gelu1(0, 1)
                turn(0, False, True)
                with act.Fori(1, STRIPS - 1) as s:
                    turn(s, True, True)
                turn(STRIPS - 1, True, False)
                t = STRIPS - 1
                gelu2(t, 5, 1)
                for half in range(2):
                    evac(t, half)
                deviate(t)
                normalise(t)
                for half in range(2):
                    turned(t, half)
                    first(t, half)

            @block.vector
            def _(ve):
                link = Link(ve, dv)
                for i in range(3):
                    nc.vector.memset(h[:, i, :, :], 0.0)
                ve.wait_ge(made, 3)
                ve.wait_ge(con, 16 * 14)
                for k in range(2):
                    nc.vector.tensor_scalar(w1[0:KC, k, :], hs[0:KC, k, 0:HID], g2[:, k:k + 1], None, ALU.mult)
                for c in range(CH):
                    for n in range(PE_SHARE[c]):
                        nc.vector.tensor_scalar(diag[:, sum(PE_SHARE[:c]) + n, :], ident[:, :], dww[:, c, n:n + 1],
                                                None, ALU.mult)
                ve.wait_ge(pre_pe, 6)
                nc.vector.tensor_copy(wc[:, :, :], pC[0:KC, 0, 0:2 * CB].rearrange("p (k n) -> p k n", k=2))
                for o in range(2):
                    link(nc.vector.tensor_tensor(w1[KC:KC + 1, 1, o * (HID // 2):(o + 1) * (HID // 2)],
                                                 pC[0:1, 1, 512 * o:512 * o + HID // 2],
                                                 brow[:, o * (HID // 2):(o + 1) * (HID // 2)], ALU.add))
                ve.sem_inc(pre_dv, 1)
                start = link.n
                LINKS = sum(2 * (KS * KS - n - 1) for n in PE_SHARE)
                per = LINKS + 4

                def chunk(s, c, half):
                    ve.wait_ge(s_tap, s * (CH * 2) + (2 * c + half + 1))
                    out = pC[:, half, :].rearrange("p (y x) -> p y x", x=W)
                    for n in range(PE_SHARE[c], KS * KS):
                        y, x = ALL_TAPS[n]
                        ins = nc.vector.scalar_tensor_tensor(out, h[:, c % 3, y + 8 * half:y + 8 * half + 8, x:x + W],
                                                             dww[:, c, n:n + 1], out, ALU.mult, ALU.add)
                        if n < KS * KS - 1:
                            link(ins)
                        else:
                            ins.then_inc(s_acc, 1)

                def stats(t):
                    ve.wait_ge(s_p2f, t * USES + 10)
                    ve.sem_inc(marks, 1)
                    for r in range(ROWS):
                        ins = nc.vector.bn_stats(st6[:, r, :], F[:, r, :])
                    link(ins)
                    ve.sem_inc(marks, 1)
                    for r in range(ROWS):
                        ins = nc.vector.bn_aggr(mv[:, r, :], st6[:, r, :])
                    link(ins)
                    nc.vector.tensor_scalar(dev[:, :], mv[:, :, 1], EPS, None, ALU.add).then_inc(s_st, 1)

                def scales(t):
                    ve.wait_ge(s_dev, t + 1)
                    link(nc.vector.reciprocal(dev[:, :], dev[:, :]))
                    link(nc.vector.tensor_scalar(nmu[:, :], mv[:, :, 0], -1.0, None, ALU.mult))
                    nc.vector.tensor_tensor(nmu[:, :], nmu[:, :], dev[:, :], ALU.mult).then_inc(s_rs, 1)

                def turn(s, tail):
                    link.base, link.n = (s - 1) * per + (start + LINKS) if tail else start, 0
                    for c in range(CH):
                        if tail and c == 2:
                            stats(s - 1)
                        chunk(s, c, 0)
                        if tail and c == 2:
                            scales(s - 1)
                        chunk(s, c, 1)
                    assert link.n == (per if tail else LINKS)

                turn(0, False)
                with ve.Fori(1, STRIPS) as s:
                    turn(s, True)
                link.base, link.n = (STRIPS - 1) * per + (start + LINKS), 0
                stats(STRIPS - 1)
                scales(STRIPS - 1)


WINDOWS = (4, 8, 12)
WB = len(WINDOWS)
PITCH = W + 2


ROWS_AT = {4: 4, 8: 2, 12: 1}


def window(nw):
    step = H // nw
    return step, step + H % nw


def window_parts(t, nw):
    step, k = window(nw)
    parts = []
    for y0 in range(0, k, step):
        for x0 in range(0, k, step):
            v = t[:, y0:y0 + nw * step, x0:x0 + nw * step].rearrange("p (u y) (v x) -> p y x u v", u=nw, v=nw)
            parts.append((y0, min(step, k - y0), x0, min(step, k - x0), v))
    return parts


def phase_cut(nc, sems, a, d):
    with ExitStack() as mem:
        def sb(name, shape, dt=F32):
            return mem.enter_context(nc.sbuf_tensor("c_" + name, shape, dt))

        def sem(name):
            return sems.new("c_" + name)

        img = sb("img", [P, H + 2, PITCH])
        tile = sb("tile", [P, 2, max(ROWS_AT[n] * window(n)[1] * n * n for n in WINDOWS)])
        img_in = sem("img_in")
        s_cut = [sem(f"s_cut{k}") for k in range(2)]
        stored = [sem(f"stored{k}") for k in range(2)]
        ROWS_OF = [(j, nw, part) for j, nw in enumerate(WINDOWS) for part in range(0, window(nw)[1], window(nw)[0])]

        def cut_row(eng, copy, half):
            eng.wait_ge(img_in, 32)
            done = 0
            for j, nw, y0 in ROWS_OF:
                parts = [p for p in window_parts(img, nw) if p[0] == y0]
                R, k = ROWS_AT[nw], window(nw)[1]
                turns = parts[0][1] // (2 * R)
                with eng.Fori(0, turns) as i:
                    eng.wait_ge(stored[half], i * 16 + 16 * (done + 1))
                    for r in range(R):
                        for _, _, x0, nx, v in parts:
                            lo = (r * k + x0) * nw * nw
                            src = v[:, bass.ds(i * (2 * R) + (half * R + r), 1), 0:nx].rearrange("p o x u v -> p (o x) u v")
                            dst = tile[:, half, lo:lo + nx * nw * nw].rearrange("p (x u v) -> p x u v", u=nw, v=nw)
                            ins = copy(dst, src)
                    ins.then_inc(s_cut[half], 1)
                done += turns

        with nc.Block() as block:
            @block.sync
            def _(sp):
                for b in range(B):
                    sp.dma_start(img[b * CB:(b + 1) * CB, 0:H, 0:W],
                                 d.xc[b].rearrange("c (y x) -> c y x", x=W)).then_inc(img_in, 16)
                for k in range(2):
                    sp.sem_inc(stored[k], 16)
                done = 0
                for j, nw, y0 in ROWS_OF:
                    k = window(nw)[1]
                    n = k * nw * nw
                    u = d.u[j].rearrange("b c n -> (b c) n")
                    R = ROWS_AT[nw]
                    turns = [p for p in window_parts(img, nw) if p[0] == y0][0][1] // (2 * R)
                    with sp.Fori(0, turns) as i:
                        for half in range(2):
                            sp.wait_ge(s_cut[half], i + (done + 1))
                            sp.dma_start(at(u, (i * (2 * R) + (y0 + half * R)) * n, R * n),
                                         tile[:, half, 0:R * n]).then_inc(stored[half], 16)
                    done += turns
                for k in range(2):
                    sp.wait_ge(stored[k], 16 * done + 16)

            @block.vector
            def _(ve):
                cut_row(ve, nc.vector.tensor_copy, 0)

            @block.scalar
            def _(act):
                cut_row(act, lambda dst, src: nc.scalar.activation(dst, src, ACT.Copy), 1)


def phase_mix(nc, sems, a, d):
    with ExitStack() as mem:
        def sb(name, shape, dt=F32):
            return mem.enter_context(nc.sbuf_tensor("m_" + name, shape, dt))

        def ps(name, shape, dt=F32):
            return mem.enter_context(nc.psum_tensor("m_" + name, shape, dt))

        def sem(name):
            return sems.new("m_" + name)

        AT_ONCE = {4: 1, 8: 4, 12: 2}
        TAPS = (4, 3, 5, 1, 7, 0, 2, 6, 8)
        PE_TAPS = {4: 4, 8: 4, 12: 4}
        UB = 4
        BANK = 512
        SE = 8
        BIG = 1024
        ident = sb("ident", [P, P])
        w2r = sb("w2r", [P, P])
        w2 = sb("w2", [P, P])
        se1r = sb("se1r", [SE, P])
        se1 = sb("se1", [P, SE])
        se2r = sb("se2r", [P, SE])
        se2 = sb("se2", [SE, P])
        b2 = sb("b2", [P, 1])
        wp = sb("wp", [P, 9])
        bp = sb("bp", [P, 1])
        diag = sb("diag", [P, max(PE_TAPS.values()), P])
        u = sb("u", [P, UB, BIG])
        y = sb("y", [P, 2, BIG])
        acc = sb("acc", [P, 2, BIG])
        ysum = sb("ysum", [P, 2, 4])
        r = sb("r", [SE, 2, 4])
        sg = sb("sg", [P, 2, 4])
        pY = ps("pY", [P, BIG])
        pC = ps("pC", [P, 2, BIG])
        pE = ps("pE", [P, 512])
        pG = ps("pG", [P, 512])

        made, con, cleared, pre_pe, pre_dv = (sem(n) for n in ("made", "con", "cleared", "pre_pe", "pre_dv"))
        dv = sem("dv")
        u_in = [sem(f"u_in{k}") for k in range(UB)]
        s_Y = sem("s_Y")
        s_t = sem("s_t")
        s_y = sem("s_y")
        s_E = sem("s_E")
        s_r = sem("s_r")
        s_G = sem("s_G")
        s_sg = sem("s_sg")
        s_z = sem("s_z")
        s_a = sem("s_a")
        a_out = [sem(f"a_out{k}") for k in range(2)]

        def chunks(nw):
            return nw * nw // AT_ONCE[nw]

        def each():
            done = 0
            for j, nw in enumerate(WINDOWS):
                yield j, nw, AT_ONCE[nw], window(nw)[1] ** 2, done
                done += chunks(nw)

        TOTAL = sum(chunks(nw) for nw in WINDOWS)

        def by_window(t, nw):
            k, nb = window(nw)[1], AT_ONCE[nw]
            return t.rearrange("p (w n) -> p w n", w=nb)[:, :, 0:k * k]

        def shifted(k, t, lo=0, hi=None):
            dy, dx = t // 3 - 1, t % 3 - 1
            hi = k if hi is None else hi
            ys, xs = slice(max(lo, -dy), min(hi, k - dy)), slice(max(0, -dx), k - max(0, dx))
            return ys, xs, slice(ys.start + dy, ys.stop + dy), slice(xs.start + dx, xs.stop + dx)

        with nc.Block() as block:
            @block.gpsimd
            def _(gp):
                nc.gpsimd.memset(ident[:, :], 0.0).then_inc(made, 1)
                gp.wait_ge(made, 1)
                nc.gpsimd.affine_select(out=ident[:, :], in_=ident[:, :], compare_op=ALU.not_equal, fill=1.0,
                                        base=0, pattern=[[-1, P]], channel_multiplier=1).then_inc(made, 1)
                for j, nw, nb, kk, done in each():
                    src = [d.u[j][b].rearrange("c n -> (c n)").rearrange("(w c n) -> c w n", c=CB, n=kk) for b in range(B)]
                    with gp.Fori(0, chunks(nw) // UB) as ii:
                        for n in range(UB):
                            gp.wait_ge(s_a, ii * UB + (done + n + 1))
                            for b in range(B):
                                gp.dma_start(by_window(u[b * CB:(b + 1) * CB, n, :], nw),
                                             src[b][:, bass.ds((ii * UB + n) * nb, nb), :]).then_inc(u_in[n], 16)

            @block.sync
            def _(sp):
                def cin(dst, src):
                    sp.dma_start(dst, src).then_inc(con, 16)

                sp.wait_ge(cleared, 3)
                with nc.allow_non_contiguous_dma("small constants"):
                    for b in range(B):
                        s = slice(b * CB, (b + 1) * CB)
                        e = slice(b * SE // 2, (b + 1) * SE // 2)
                        cin(w2r[s, s], a["L1_conv_w2"])
                        cin(se1r[e, s], a["L1_conv_wse1"])
                        cin(se2r[s, e], a["L1_conv_wse2"])
                        cin(b2[s, :], a["L1_conv_b2"].rearrange("(c o) -> c o", o=1))
                        cin(bp[s, :], a["L1_conv_bpos"].rearrange("(c o) -> c o", o=1))
                        cin(wp[s, :], a["L1_conv_wpos"].rearrange("c o y x -> c (o y x)"))
                for k in range(2):
                    sp.sem_inc(a_out[k], 32)
                for j, nw, nb, kk, done in each():
                    dst = [d.v[j][b].rearrange("c n -> (c n)").rearrange("(w c n) -> c w n", c=CB, n=kk) for b in range(B)]
                    with sp.Fori(0, chunks(nw) // 2) as ii:
                        for half in range(2):
                            sp.wait_ge(s_a, ii * 2 + (done + half + UB + 1))
                            for b in range(B):
                                sp.dma_start(dst[b][:, bass.ds((ii * 2 + half) * nb, nb), :],
                                             by_window(acc[b * CB:(b + 1) * CB, half, :], nw)).then_inc(a_out[half], 16)
                for k in range(2):
                    sp.wait_ge(a_out[k], 16 * TOTAL + 32)

            @block.tensor
            def _(te):
                te.wait_ge(made, 2)
                te.wait_ge(con, 16 * 12)
                nc.tensor.transpose(pE[:, 0:P], w2r[:, :], ident[:, :]).then_inc(pre_pe, 1)
                nc.tensor.transpose(pE[:, P:P + SE], se1r[:, :], ident[0:SE, 0:SE]).then_inc(pre_pe, 1)
                nc.tensor.transpose(pG[0:SE, 0:P], se2r[:, :], ident[:, :]).then_inc(pre_pe, 1)
                te.wait_ge(pre_dv, 1)

                def taps(n, half, nw, bank):
                    k, per = window(nw)[1], BANK * AT_ONCE[nw] // BIG
                    uw, cw = by_window(u[:, n, :], nw), by_window(pC[:, half, :], nw)
                    if per:
                        ws, lo, hi = slice(bank * per, (bank + 1) * per), 0, k
                    else:
                        ws, lo, hi = slice(0, 1), bank * k // 2, (bank + 1) * k // 2
                    uw = uw[:, ws].rearrange("p w (y x) -> p w y x", x=k)
                    cw = cw[:, ws].rearrange("p w (y x) -> p w y x", x=k)
                    for m, t in enumerate(TAPS[:PE_TAPS[nw]]):
                        ys, xs, yi, xi = shifted(k, t, lo, hi)
                        mm = nc.tensor.matmul(cw[:, :, ys, xs], diag[:, m, :], uw[:, :, yi, xi], start=(m == 0),
                                              stop=(m == PE_TAPS[nw] - 1))
                    return mm

                for j, nw, nb, kk, done in each():
                    cols = [(q * BANK, BANK) for q in range(2)] if nb != 2 else [(q * BANK, kk) for q in range(2)]
                    with te.Fori(0, chunks(nw) // UB) as ii:
                        for n in range(UB):
                            half = n % 2
                            i = ii * UB + (done + n)
                            te.wait_ge(u_in[n], ii * 32 + (32 + 32 * (done // UB)))
                            te.wait_ge(s_y, i + 1)
                            for lo, size in cols:
                                mm = nc.tensor.matmul(pY[:, lo:lo + size], w2[:, :], u[:, n, lo:lo + size],
                                                      start=True, stop=True)
                            mm.then_inc(s_Y, 1)
                            te.wait_ge(s_a, i + (UB - 1))
                            taps(n, half, nw, 0)
                            te.wait_ge(s_y, i + 2)
                            nc.tensor.matmul(pE[0:SE, 0:nb], se1[:, :], ysum[:, half, 0:nb], start=True,
                                             stop=True).then_inc(s_E, 1)
                            taps(n, half, nw, 1).then_inc(s_t, 1)
                            te.wait_ge(s_r, i + 1)
                            nc.tensor.matmul(pG[:, 0:nb], se2[:, :], r[:, half, 0:nb], start=True,
                                             stop=True).then_inc(s_G, 1)

            @block.scalar
            def _(act):
                act.sem_inc(s_y, 1)
                for j, nw, nb, kk, done in each():
                    with act.Fori(0, chunks(nw) // 2) as ii:
                        for half in range(2):
                            i = ii * 2 + (done + half)
                            yw, pw = by_window(y[:, half, :], nw), by_window(pY[:, :], nw)
                            act.wait_ge(s_Y, i + 1)
                            act.wait_ge(s_a, i + (UB - 1))
                            for w in range(nb):
                                ins = nc.scalar.activation(yw[:, w], pw[:, w], ACT.Identity, bias=b2[:, 0:1],
                                                           accum_out=ysum[:, half, w:w + 1])
                            ins.then_inc(s_y, 1)
                            act.wait_ge(s_E, i + 1)
                            nc.scalar.activation(r[:, half, 0:nb], pE[0:SE, 0:nb], ACT.Relu,
                                                 scale=1.0 / kk).then_inc(s_r, 1)
                            act.wait_ge(s_G, i + 1)
                            nc.scalar.activation(sg[:, half, 0:nb], pG[:, 0:nb], ACT.Sigmoid).then_inc(s_sg, 1)
                            act.wait_ge(s_sg, i + 1)
                            for w in range(nb):
                                ins = nc.scalar.activation(yw[:, w], yw[:, w], ACT.Identity, bias=bp[:, 0:1],
                                                           scale=sg[:, half, w:w + 1])
                            ins.then_inc(s_z, 1)

            @block.vector
            def _(ve):
                link = Link(ve, dv)
                nc.vector.memset(w2r[:, :], 0.0).then_inc(cleared, 1)
                nc.vector.memset(se1r[:, :], 0.0).then_inc(cleared, 1)
                nc.vector.memset(se2r[:, :], 0.0).then_inc(cleared, 1)
                ve.sem_inc(s_a, UB)
                ve.wait_ge(pre_pe, 3)
                link(nc.vector.tensor_copy(w2[:, :], pE[:, 0:P]))
                link(nc.vector.tensor_copy(se1[:, :], pE[:, P:P + SE]))
                link(nc.vector.tensor_copy(se2[:, :], pG[0:SE, 0:P]))
                for m in range(max(PE_TAPS.values())):
                    t = TAPS[m]
                    link(nc.vector.tensor_scalar(diag[:, m, :], ident[:, :], wp[:, t:t + 1], None, ALU.mult))
                ve.sem_inc(pre_dv, 1)
                start = link.n
                for j, nw, nb, kk, done in each():
                    k = window(nw)[1]
                    per = (len(TAPS) - PE_TAPS[nw]) * nb
                    with ve.Fori(0, chunks(nw) // UB) as ii:
                        for n in range(UB):
                            half = n % 2
                            before = ii * (UB * per) + (start + n * per)
                            ops = 0
                            ve.wait_ge(s_t, ii * UB + (done + n + 1))
                            uw = by_window(u[:, n, :], nw).rearrange("p w (y x) -> p w y x", x=k)
                            cw = by_window(pC[:, half, :], nw).rearrange("p w (y x) -> p w y x", x=k)
                            for t in TAPS[PE_TAPS[nw]:]:
                                ys, xs, yi, xi = shifted(k, t)
                                for w in range(nb):
                                    if ops >= nb:
                                        ve.wait_ge(dv, before + (ops - nb + 1))
                                    nc.vector.scalar_tensor_tensor(cw[:, w, ys, xs], uw[:, w, yi, xi],
                                                                   wp[:, t:t + 1], cw[:, w, ys, xs],
                                                                   ALU.mult, ALU.add).then_inc(dv, 1)
                                    ops += 1
                            ve.wait_ge(dv, before + per)
                            ve.wait_ge(s_z, ii * UB + (done + n + 1))
                            ve.wait_ge(a_out[half], ii * 64 + (16 * done + 32 * (n // 2) + 32))
                            nc.vector.tensor_tensor(by_window(acc[:, half, :], nw), by_window(y[:, half, :], nw),
                                                    by_window(pC[:, half, :], nw), ALU.add).then_inc(s_a, 1)
                    start += chunks(nw) * per


def phase_fold(nc, sems, a, d):
    with ExitStack() as mem:
        def sb(name, shape, dt=F32):
            return mem.enter_context(nc.sbuf_tensor("b_" + name, shape, dt))

        def sem(name):
            return sems.new("b_" + name)

        field = [sb(f"field{k}", [P, H + 2, PITCH]) for k in range(2)]
        tile = sb("tile", [P, 2, max(ROWS_AT[n] * window(n)[1] * n * n for n in WINDOWS)])
        tile_in = [sem(f"tile_in{k}") for k in range(2)]
        s_used = [sem(f"s_used{k}") for k in range(2)]
        dv = sem("dv")
        s_done = sem("s_done")
        out_f = [sem(f"out_f{k}") for k in range(WB)]
        ROWS_OF = [(j, nw, part) for j, nw in enumerate(WINDOWS) for part in range(0, window(nw)[1], window(nw)[0])]
        PLAIN = [x for x in ROWS_OF if H % x[1] == 0]
        SHARED = [x for x in ROWS_OF if H % x[1]]

        def turns_of(nw, y0):
            return min(window(nw)[0], window(nw)[1] - y0) // (2 * ROWS_AT[nw])

        def place(eng, copy, half):
            done = 0
            for j, nw, y0 in PLAIN:
                y0_, ny, x0, nx, v = window_parts(field[j % 2], nw)[0]
                R, n = ROWS_AT[nw], nx * nw * nw
                with eng.Fori(0, turns_of(nw, y0)) as i:
                    eng.wait_ge(tile_in[half], i * 16 + 16 * (done + 1))
                    for r in range(R):
                        dst = v[:, bass.ds(i * (2 * R) + (half * R + r), 1), 0:nx].rearrange("p o x u v -> p (o x) u v")
                        src = tile[:, half, r * n:(r + 1) * n].rearrange("p (x u v) -> p x u v", u=nw, v=nw)
                        ins = copy(dst, src)
                    ins.then_inc(s_used[half], 1)
                done += turns_of(nw, y0)
            return done

        with nc.Block() as block:
            @block.gpsimd
            def _(gp):
                done = 0
                for j, nw, y0 in ROWS_OF:
                    k = window(nw)[1]
                    n = k * nw * nw
                    v = d.v[j].rearrange("b c n -> (b c) n")
                    R = ROWS_AT[nw]
                    with gp.Fori(0, turns_of(nw, y0)) as i:
                        for half in range(2):
                            gp.wait_ge(s_used[half], i + (done + 1))
                            gp.dma_start(tile[:, half, 0:R * n],
                                         at(v, (i * (2 * R) + (y0 + half * R)) * n, R * n)).then_inc(tile_in[half], 16)
                    done += turns_of(nw, y0)

            @block.sync
            def _(sp):
                def store(j):
                    for b in range(B):
                        sp.dma_start(d.cat[b, j * CB:(j + 1) * CB].rearrange("c (y x) -> c y x", x=W),
                                     field[j % 2][b * CB:(b + 1) * CB, 0:H, 0:W]).then_inc(out_f[j], 16)

                done = 0
                for j, nw, y0 in PLAIN:
                    done += turns_of(nw, y0)
                    for k in range(2):
                        sp.wait_ge(s_used[k], done + 1)
                    store(j)
                sp.wait_ge(s_done, 1)
                store(WB - 1)
                for k in range(WB):
                    sp.wait_ge(out_f[k], 16 * B)

            @block.scalar
            def _(act):
                act.sem_inc(s_used[1], 1)
                place(act, lambda dst, src: nc.scalar.activation(dst, src, ACT.Copy), 1)

            @block.vector
            def _(ve):
                link = Link(ve, dv)
                ve.sem_inc(s_used[0], 1)
                done = place(ve, nc.vector.tensor_copy, 0)
                F_ = field[(WB - 1) % 2]
                ve.wait_ge(out_f[0], 16 * B)
                ve.wait_ge(s_used[1], done + 1)
                link(nc.vector.memset(F_[:, :, :], 0.0))
                base = link.n
                for j, nw, y0 in SHARED:
                    parts = [p for p in window_parts(F_, nw) if p[0] == y0]
                    turns = turns_of(nw, y0)
                    with ve.Fori(0, turns) as i:
                        for half in range(2):
                            link.base, link.n = i * 4 + base, 2 * half
                            ve.wait_ge(tile_in[half], i * 16 + 16 * (done + 1))
                            for _, _, x0, nx, v in parts:
                                dst = v[:, bass.ds(i * 2 + half, 1), 0:nx].rearrange("p o x u v -> p (o x) u v")
                                src = tile[:, half, x0 * nw * nw:(x0 + nx) * nw * nw].rearrange("p (x u v) -> p x u v", u=nw, v=nw)
                                link(nc.vector.tensor_tensor(dst, dst, src, ALU.add))
                            ve.sem_inc(s_used[half], 1)
                    base += turns * 4
                    done += turns
                link.base, link.n = base, 0
                nw = WINDOWS[-1]
                step, k = window(nw)
                rows = F_[:, step:nw * step, 0:W].rearrange("p (u y) x -> p u y x", y=step)[:, :, 0:k - step]
                link(nc.vector.tensor_scalar(rows, rows, 0.5, None, ALU.mult))
                cols = F_[:, 0:H, step:nw * step].rearrange("p y (v x) -> p y v x", x=step)[:, :, :, 0:k - step]
                nc.vector.tensor_scalar(cols, cols, 0.5, None, ALU.mult).then_inc(s_done, 1)


def phase_last(nc, sems, a, d, out):
    with ExitStack() as mem:
        def sb(name, shape, dt=F32):
            return mem.enter_context(nc.sbuf_tensor("l_" + name, shape, dt))

        def ps(name, shape, dt=F32):
            return mem.enter_context(nc.psum_tensor("l_" + name, shape, dt))

        def sem(name):
            return sems.new("l_" + name)

        TN = 1024
        XB = 4
        Q = TN // 512
        TURNS = B * N // TN
        PI = N // TN
        ident = sb("ident", [P, P])
        w3r = sb("w3r", [KC, 2, C])
        w3 = sb("w3", [KC, 2, C])
        b3 = sb("b3", [KC, 2])
        x = sb("x", [KC, XB, 2, TN])
        f = sb("f", [KC, XB, 2, TN])
        o = sb("o", [KC, XB, 2, TN])
        pO = ps("pO", [KC, 8, 512])
        made, con, pre_pe, pre_dv = (sem(n) for n in ("made", "con", "pre_pe", "pre_dv"))
        x_in = [sem(f"x_in{k}") for k in range(XB)]
        s_x = sem("s_x")
        s_O = sem("s_O")
        s_o = sem("s_o")
        o_out = [sem(f"o_out{k}") for k in range(XB)]
        x_v = d.x1.rearrange("b (k p) n -> b p k n", k=2)
        f_v = d.cat.rearrange("b (k p) n -> b p k n", k=2)
        o_v = out.rearrange("b (k p) h w -> b p k (h w)", k=2)

        with nc.Block() as block:
            @block.gpsimd
            def _(gp):
                nc.gpsimd.memset(ident[:, :], 0.0).then_inc(made, 1)
                gp.wait_ge(made, 1)
                nc.gpsimd.affine_select(out=ident[:, :], in_=ident[:, :], compare_op=ALU.not_equal, fill=1.0,
                                        base=0, pattern=[[-1, P]], channel_multiplier=1).then_inc(made, 1)
                with gp.Fori(0, TURNS // XB) as ii:
                    for slot in range(XB):
                        i = ii * XB + slot
                        gp.wait_ge(s_O, i * (2 * Q) + 2 * Q)
                        for t, v in ((x, x_v), (f, f_v)):
                            gp.dma_start(t[:, slot, :, :], v[bass.ds(i // PI, 1), :, :, bass.ds((i % PI) * TN, TN)]
                                         .rearrange("b p k n -> (b p) k n")).then_inc(x_in[slot], 16)

            @block.sync
            def _(sp):
                sp.dma_start(w3r[:, :, :], a["L1_conv_w3"].rearrange("(m p) c -> p m c", m=2)).then_inc(con, 16)
                with nc.allow_non_contiguous_dma("small constants"):
                    sp.dma_start(b3[:, :], a["L1_conv_b3"].rearrange("(m p) -> p m", m=2)).then_inc(con, 16)
                for k in range(XB):
                    sp.sem_inc(o_out[k], 16)
                with sp.Fori(0, TURNS // XB) as ii:
                    for slot in range(XB):
                        i = ii * XB + slot
                        sp.wait_ge(s_o, i * (2 * Q) + (8 + 2 * Q))
                        sp.dma_start(o_v[bass.ds(i // PI, 1), :, :, bass.ds((i % PI) * TN, TN)]
                                     .rearrange("b p k n -> (b p) k n"), o[:, slot, :, :]).then_inc(o_out[slot], 16)
                for k in range(XB):
                    sp.wait_ge(o_out[k], 16 * (TURNS // XB) + 16)

            @block.tensor
            def _(te):
                te.sem_inc(s_O, 2 * Q * XB)
                te.wait_ge(made, 2)
                te.wait_ge(con, 32)
                for m in range(2):
                    for k in range(2):
                        nc.tensor.transpose(pO[:, k, m * KC:(m + 1) * KC], w3r[:, m, k * KC:(k + 1) * KC],
                                            ident[0:KC, 0:KC]).then_inc(pre_pe, 1)
                te.wait_ge(pre_dv, 1)
                with te.Fori(0, TURNS // XB) as ii:
                    for slot in range(XB):
                        i = ii * XB + slot
                        te.wait_ge(s_x, i + 1)
                        for m in range(2):
                            for q in range(Q):
                                n = m * Q + q
                                bank = (slot * 2 * Q + n) % 8
                                te.wait_ge(s_o, i * (2 * Q) + (n + 1))
                                for k in range(2):
                                    mm = nc.tensor.matmul(pO[:, bank, :], w3[:, k, m * KC:(m + 1) * KC],
                                                          x[:, slot, k, q * 512:(q + 1) * 512], start=(k == 0), stop=(k == 1))
                                mm.then_inc(s_O, 1)

            @block.scalar
            def _(act):
                act.sem_inc(s_o, 8)
                with act.Fori(0, TURNS // XB) as ii:
                    for slot in range(XB):
                        i = ii * XB + slot
                        act.wait_ge(o_out[slot], ii * 16 + 16)
                        for n in range(2 * Q):
                            act.wait_ge(s_O, i * (2 * Q) + (n + 1 + 2 * Q * XB))
                            m, q, bank = n // Q, n % Q, (slot * 2 * Q + n) % 8
                            nc.scalar.activation(o[:, slot, m, q * 512:(q + 1) * 512], pO[:, bank, :], ACT.Identity,
                                                 bias=b3[:, m:m + 1]).then_inc(s_o, 1)

            @block.vector
            def _(ve):
                ve.wait_ge(pre_pe, 4)
                nc.vector.tensor_copy(w3[:, :, :], pO[:, 0:2, 0:C]).then_inc(pre_dv, 1)
                with ve.Fori(0, TURNS // XB) as ii:
                    for slot in range(XB):
                        ve.wait_ge(x_in[slot], ii * 32 + 32)
                        nc.vector.tensor_tensor(x[:, slot, :, :], x[:, slot, :, :], f[:, slot, :, :], ALU.add).then_inc(s_x, 1)


class Semaphores:

    def __init__(self, nc):
        self.nc, self.held = nc, []

    def new(self, name):
        self.held.append(self.nc.alloc_semaphore(name=name))
        return self.held[-1]

    def clear(self):
        self.nc.clear_and_free_semaphores(self.held)
        self.held = []
        self.nc.all_engine_barrier()


def build(nc, a, out, phases="tsafcmbl"):
    d = scratch(nc)
    sems = Semaphores(nc)
    work = {"t": phase_tokens, "s": phase_sort, "a": phase_attend, "f": phase_ffn,
            "c": phase_cut, "m": phase_mix, "b": phase_fold}
    for phase in phases:
        if phase == "l":
            phase_last(nc, sems, a, d, out)
        else:
            work[phase](nc, sems, a, d)
        if phase != phases[-1]:
            sems.clear()


_INS = ['x', 'L0_conv_td', 'L0_conv_g1', 'L0_conv_b1', 'L0_conv_g2', 'L0_conv_b2', 'L0_conv_g3', 'L0_conv_b3',
        'L0_conv_wq_w', 'L0_conv_wq_b', 'L0_conv_wk_w', 'L0_conv_wk_b', 'L0_conv_wv_w', 'L0_conv_wv_b',
        'L0_conv_ca_scale', 'L0_conv_wqkv_w', 'L0_conv_wqkv_b', 'L0_conv_proj_w', 'L0_conv_proj_b',
        'L0_conv_fc_td_w', 'L0_conv_fc_td_b', 'L0_conv_fc1_w', 'L0_conv_fc1_b', 'L0_conv_dw_w', 'L0_conv_dw_b',
        'L0_conv_fc2_w', 'L0_conv_fc2_b', 'L1_conv_w1', 'L1_conv_b1', 'L1_conv_w2', 'L1_conv_b2', 'L1_conv_w3',
        'L1_conv_b3', 'L1_conv_wpos', 'L1_conv_bpos', 'L1_conv_wse1', 'L1_conv_wse2']


def kernel(**inputs):
    import concourse.bacc as bacc
    from concourse.bass_utils import run_bass_kernel_spmd

    nc = bacc.Bacc("TRN2", target_bir_lowering=False, num_devices=1)
    arrays, args = {}, {}
    for name in _INS:
        x = np.ascontiguousarray(inputs[name])
        arrays["in_" + name] = x
        args[name] = nc.dram_tensor("in_" + name, x.shape, mybir.dt.from_np(x.dtype), kind="ExternalInput").ap()
    out = nc.dram_tensor("out_0", (B, C, H, W), F32, kind="ExternalOutput").ap()
    build(nc, args, out)
    r = run_bass_kernel_spmd(nc, [arrays], core_ids=[0])
    return r.results[0]["out_0"]
```
